# Optimizing a Trainium2 kernel written in Bass

```python
import numpy as np
import jax
import jax.numpy as jnp

def _softmax(x, axis=-1):
    return jax.nn.softmax(x, axis=axis)

def _gelu(x):
    return jax.nn.gelu(x, approximate=True)

def _silu(x):
    return jax.nn.silu(x)

def _sigmoid(x):
    return jax.nn.sigmoid(x)

def _layernorm(x, axis=-1, eps=1e-05):
    m = jnp.mean(x, axis=axis, keepdims=True)
    v = jnp.var(x, axis=axis, keepdims=True)
    return (x - m) / jnp.sqrt(v + eps)

def _scatter_add(tgt, idx, src, axis=0):
    return tgt.at[idx].add(src)

def _segment_sum(src, seg, n):
    return jax.ops.segment_sum(src, seg, n)
kernel_name = 'mk_gnn_resnorm_d4_gnn_r32_473abb'

def setup_inputs(seed: int=0):
    np.random.seed(seed)
    _w = jnp.asarray

    def _rec_inputs():
        import jax
        import jax.numpy as jnp
        _gk = jax.random.key(seed)
        x = -0.0006008 + 1.001 * jax.random.normal(jax.random.fold_in(_gk, 1), (3125, 256), jnp.float32)
        src = jax.random.randint(jax.random.fold_in(_gk, 2), (50000,), 0, 3125, jnp.int32)
        dst = jax.random.randint(jax.random.fold_in(_gk, 3), (50000,), 0, 3125, jnp.int32)
        _o = jnp.argsort(dst, stable=True)
        src = src[_o]
        dst = dst[_o]
        edge_type_20 = jax.random.randint(jax.random.fold_in(_gk, 13), (50000,), 0, 20, jnp.int32)
        edge_type_8 = jax.random.randint(jax.random.fold_in(_gk, 14), (50000,), 0, 8, jnp.int32)
        edge_weight1 = jax.random.uniform(jax.random.fold_in(_gk, 15), (50000, 1), jnp.float32, 0.0, 0.999998)
        node_type_4 = jax.random.randint(jax.random.fold_in(_gk, 16), (3125,), 0, 4, jnp.int32)
        return (x, src, dst, edge_type_20, edge_type_8, edge_weight1, node_type_4)
    x, src, dst, edge_type_20, edge_type_8, edge_weight1, node_type_4 = _rec_inputs()

    def _L0_gnn_setup():
        import jax, jax.numpy as jnp
        import numpy as np
        N_NODES = 10000
        N_EDGES = 10000
        NUM_RELS = 20
        IN_FEAT = 256
        OUT_FEAT = 256
        key = jax.random.key(seed)
        k1, k2, k3, k4, k5, k6 = jax.random.split(key, 6)
        h = jax.random.normal(k1, (N_NODES, IN_FEAT), dtype=jnp.float32)
        gain = float(np.sqrt(2.0))
        limit = gain * float(np.sqrt(6.0 / (IN_FEAT + OUT_FEAT)))
        weight = jax.random.uniform(k2, (NUM_RELS, IN_FEAT, OUT_FEAT), dtype=jnp.float32, minval=-limit, maxval=limit)
        norm = jax.random.uniform(k3, (N_EDGES, 1), dtype=jnp.float32)
        edge_src = jax.random.randint(k4, (N_EDGES,), 0, N_NODES, dtype=jnp.int32)
        edge_dst = jax.random.randint(k5, (N_EDGES,), 0, N_NODES, dtype=jnp.int32)
        rel_type = jax.random.randint(k6, (N_EDGES,), 0, NUM_RELS, dtype=jnp.int32)
        return {'h': h, 'weight': weight, 'norm': norm, 'edge_src': edge_src, 'edge_dst': edge_dst, 'rel_type': rel_type}
    _L0_gnn_all = _L0_gnn_setup()
    _L0_gnn_in = {k: v for k, v in _L0_gnn_all.items() if k in ('weight',)}
    del _L0_gnn_all

    def _L1_gnn_setup():
        import jax, jax.numpy as jnp
        import numpy as np
        N_NODES = 10000
        N_EDGES = 10000
        D = 256
        key = jax.random.key(seed)
        k_x, k_w, k_m, k_s, k_d = jax.random.split(key, 5)
        x = jax.random.normal(k_x, (N_NODES, D), dtype=jnp.float32)
        W = jax.random.normal(k_w, (D, D), dtype=jnp.float32)
        M = jax.random.normal(k_m, (D, D), dtype=jnp.float32)
        edge_src = jax.random.randint(k_s, (N_EDGES,), 0, N_NODES, dtype=jnp.int64)
        edge_dst = jax.random.randint(k_d, (N_EDGES,), 0, N_NODES, dtype=jnp.int64)
        return {'x': x, 'W': W, 'M': M, 'edge_src': edge_src, 'edge_dst': edge_dst}
    _L1_gnn_all = _L1_gnn_setup()
    _L1_gnn_in = {k: v for k, v in _L1_gnn_all.items() if k in ('W', 'M')}
    del _L1_gnn_all

    def _L2_gnn_setup():
        import jax, jax.numpy as jnp
        import numpy as np
        N_NODES = 625
        N_EDGES = 10000
        IN_DIM = 256
        OUT_DIM = 256
        N_HEADS = 4
        D_K = OUT_DIM // N_HEADS
        N_NTYPES = 4
        N_RELS = 8
        SQRT_DK = float(np.sqrt(D_K))

        def _typed_matmul(x, W, node_type):
            all_t = jnp.einsum('ni,tio->tno', x, W)
            return all_t[node_type, jnp.arange(x.shape[0])]
        key = jax.random.key(seed)
        ks = jax.random.split(key, 12)
        xav = lambda k, shape, fan: jax.random.normal(k, shape, jnp.float32) * (1.0 / np.sqrt(fan))
        return {'h': jax.random.normal(ks[0], (N_NODES, IN_DIM), jnp.float32), 'k_linears': xav(ks[1], (N_NTYPES, IN_DIM, OUT_DIM), IN_DIM), 'q_linears': xav(ks[2], (N_NTYPES, IN_DIM, OUT_DIM), IN_DIM), 'v_linears': xav(ks[3], (N_NTYPES, IN_DIM, OUT_DIM), IN_DIM), 'a_linears': xav(ks[4], (N_NTYPES, OUT_DIM, OUT_DIM), OUT_DIM), 'relation_att': xav(ks[5], (N_RELS, N_HEADS, D_K, D_K), D_K), 'relation_msg': xav(ks[6], (N_RELS, N_HEADS, D_K, D_K), D_K), 'relation_pri': jnp.ones((N_RELS, N_HEADS), jnp.float32), 'skip': jnp.ones((N_NTYPES,), jnp.float32), 'node_type': jax.random.randint(ks[7], (N_NODES,), 0, N_NTYPES), 'etype': jnp.sort(jax.random.randint(ks[8], (N_EDGES,), 0, N_RELS)), 'row_idx': jax.random.randint(ks[9], (N_EDGES,), 0, N_NODES), 'col_idx': jax.random.randint(ks[10], (N_EDGES,), 0, N_NODES)}
    _L2_gnn_all = _L2_gnn_setup()
    _L2_gnn_in = {k: v for k, v in _L2_gnn_all.items() if k in ('k_linears', 'q_linears', 'v_linears', 'a_linears', 'relation_att', 'relation_msg', 'relation_pri', 'skip')}
    del _L2_gnn_all

    def _L3_gnn_setup():
        import jax, jax.numpy as jnp
        import numpy as np
        N_NODES = 3125
        N_EDGES = 50000
        HIDDEN = 256
        N_LAYERS = 2
        key = jax.random.key(seed)
        k = jax.random.split(key, 7)
        x = jax.random.normal(k[0], (N_NODES, HIDDEN), dtype=jnp.float32)
        edge_index = jax.random.randint(k[1], (2, N_EDGES), 0, N_NODES, dtype=jnp.int64)
        s = 1.0 / np.sqrt(HIDDEN)
        W = jax.random.uniform(k[2], (N_LAYERS, HIDDEN, HIDDEN), jnp.float32, -s, s)
        b = jax.random.uniform(k[3], (N_LAYERS, HIDDEN), jnp.float32, -s, s)
        resW = jax.random.uniform(k[4], (HIDDEN, HIDDEN), jnp.float32, -s, s)
        resb = jax.random.uniform(k[5], (HIDDEN,), jnp.float32, -s, s)
        return {'x': x, 'edge_index': edge_index, 'W': W, 'b': b, 'resW': resW, 'resb': resb}
    _L3_gnn_all = _L3_gnn_setup()
    _L3_gnn_in = {k: v for k, v in _L3_gnn_all.items() if k in ('W', 'b', 'resW', 'resb')}
    del _L3_gnn_all
    return {'x': x, 'src': src, 'dst': dst, 'edge_type_20': edge_type_20, 'edge_type_8': edge_type_8, 'edge_weight1': edge_weight1, 'node_type_4': node_type_4, 'L0_gnn_weight': _L0_gnn_in['weight'], 'L1_gnn_W': _L1_gnn_in['W'], 'L1_gnn_M': _L1_gnn_in['M'], 'L2_gnn_k_linears': _L2_gnn_in['k_linears'], 'L2_gnn_q_linears': _L2_gnn_in['q_linears'], 'L2_gnn_v_linears': _L2_gnn_in['v_linears'], 'L2_gnn_a_linears': _L2_gnn_in['a_linears'], 'L2_gnn_relation_att': _L2_gnn_in['relation_att'], 'L2_gnn_relation_msg': _L2_gnn_in['relation_msg'], 'L2_gnn_relation_pri': _L2_gnn_in['relation_pri'], 'L2_gnn_skip': _L2_gnn_in['skip'], 'L3_gnn_W': _L3_gnn_in['W'], 'L3_gnn_b': _L3_gnn_in['b'], 'L3_gnn_resW': _L3_gnn_in['resW'], 'L3_gnn_resb': _L3_gnn_in['resb']}

def reference(x, src, dst, edge_type_20, edge_type_8, edge_weight1, node_type_4, L0_gnn_weight, L1_gnn_W, L1_gnn_M, L2_gnn_k_linears, L2_gnn_q_linears, L2_gnn_v_linears, L2_gnn_a_linears, L2_gnn_relation_att, L2_gnn_relation_msg, L2_gnn_relation_pri, L2_gnn_skip, L3_gnn_W, L3_gnn_b, L3_gnn_resW, L3_gnn_resb):
    import jax
    import jax.numpy as jnp

    def _L0_gnn_ref(h, weight, norm, edge_src, edge_dst, rel_type):
        import jax, jax.numpy as jnp
        import numpy as np
        N_NODES = 10000
        N_EDGES = 10000
        NUM_RELS = 20
        IN_FEAT = 256
        OUT_FEAT = 256
        h_all = jnp.einsum('ni,rio->nro', h, weight)
        msg = h_all[edge_src, rel_type] * norm
        agg = jax.ops.segment_sum(msg, edge_dst, num_segments=h.shape[0])
        return jax.nn.relu(agg)

    def _L1_gnn_ref(x, W, M, edge_src, edge_dst):
        import jax, jax.numpy as jnp
        import numpy as np
        N_NODES = 10000
        N_EDGES = 10000
        D = 256
        self_term = x @ W
        msg = x @ M
        agg = jax.ops.segment_sum(msg[edge_src], edge_dst, num_segments=x.shape[0])
        return jax.nn.relu(self_term + agg)

    def _L2_gnn_ref(h, k_linears, q_linears, v_linears, a_linears, relation_att, relation_msg, relation_pri, skip, node_type, etype, row_idx, col_idx):
        import jax, jax.numpy as jnp
        import numpy as np
        N_NODES = 625
        N_EDGES = 10000
        IN_DIM = 256
        OUT_DIM = 256
        N_HEADS = 4
        D_K = OUT_DIM // N_HEADS
        N_NTYPES = 4
        N_RELS = 8
        SQRT_DK = float(np.sqrt(D_K))

        def _typed_matmul(x, W, node_type):
            all_t = jnp.einsum('ni,tio->tno', x, W)
            return all_t[node_type, jnp.arange(x.shape[0])]
        n = h.shape[0]
        k = _typed_matmul(h, k_linears, node_type).reshape(n, N_HEADS, D_K)
        q = _typed_matmul(h, q_linears, node_type).reshape(n, N_HEADS, D_K)
        v = _typed_matmul(h, v_linears, node_type).reshape(n, N_HEADS, D_K)
        q_att = jnp.einsum('nhd,rhde->rnhe', q, relation_att)
        v_msg = jnp.einsum('nhd,rhde->rnhe', v, relation_msg)
        aw_q_edge = q_att[etype, col_idx]
        msg_edge = v_msg[etype, row_idx]
        attn_score = jnp.sum(aw_q_edge * k[row_idx], axis=-1)
        score = attn_score * (relation_pri[etype] / SQRT_DK)
        m = jax.ops.segment_max(score, col_idx, num_segments=n)
        ex = jnp.exp(score - m[col_idx])
        denom = jax.ops.segment_sum(ex, col_idx, num_segments=n)
        alpha = ex / denom[col_idx]
        agg = jax.ops.segment_sum(alpha[..., None] * msg_edge, col_idx, num_segments=n)
        agg = agg.reshape(n, OUT_DIM)
        out = _typed_matmul(agg, a_linears, node_type)
        out = jax.nn.sigmoid(skip)[node_type][:, None] * out
        return out

    def _L3_gnn_ref(x, edge_index, W, b, resW, resb):
        import jax, jax.numpy as jnp
        import numpy as np
        N_NODES = 3125
        N_EDGES = 50000
        HIDDEN = 256
        N_LAYERS = 2
        N = x.shape[0]
        loop = jnp.arange(N, dtype=edge_index.dtype)
        src = jnp.concatenate([edge_index[0], loop])
        dst = jnp.concatenate([edge_index[1], loop])
        ew = jnp.ones(src.shape[0], dtype=x.dtype)
        deg = jax.ops.segment_sum(ew, dst, num_segments=N)
        dis = jnp.where(deg > 0, jax.lax.rsqrt(jnp.where(deg > 0, deg, 1.0)), 0.0)
        norm = dis[src] * ew * dis[dst]
        for l in range(W.shape[0]):
            x_res = x
            h = x @ W[l]
            msg = norm[:, None] * h[src]
            agg = jax.ops.segment_sum(msg, dst, num_segments=N) + b[l]
            x = jax.nn.relu(agg + x_res @ resW + resb)
        return x
    edge_index = jnp.stack([src, dst])
    x = _layernorm(x + _L0_gnn_ref(x, L0_gnn_weight, edge_weight1, src, dst, edge_type_20), axis=-1)
    x = _layernorm(x + _L1_gnn_ref(x, L1_gnn_W, L1_gnn_M, src, dst), axis=-1)
    x = _layernorm(x + _L2_gnn_ref(x, L2_gnn_k_linears, L2_gnn_q_linears, L2_gnn_v_linears, L2_gnn_a_linears, L2_gnn_relation_att, L2_gnn_relation_msg, L2_gnn_relation_pri, L2_gnn_skip, node_type_4, edge_type_8, src, dst), axis=-1)
    x = _layernorm(x + _L3_gnn_ref(x, edge_index, L3_gnn_W, L3_gnn_b, L3_gnn_resW, L3_gnn_resb), axis=-1)
    return x

_drawn_inputs = setup_inputs


def setup_inputs(seed=0):
    import zlib

    import numpy as np

    out = dict(_drawn_inputs(seed))
    spreads = {'L2_gnn_relation_pri': (1.0, 0.2), 'L2_gnn_skip': (1.0, 0.6)}
    factors = {}
    for name, (base, spread) in spreads.items():
        noise = np.random.default_rng([zlib.crc32(name.encode()), seed]).standard_normal(out[name].shape)
        drawn = base * np.exp(spread * noise) if base else spread * noise
        out[name] = jnp.asarray(drawn.astype(out[name].dtype))
    for name, factor in factors.items():
        out[name] = (out[name] * factor).astype(out[name].dtype)
    return out
```

```python
from contextlib import ExitStack

import concourse.bass as bass
from concourse import mybir

F32 = mybir.dt.float32
I32 = mybir.dt.int32
BF16 = mybir.dt.bfloat16
ALU = mybir.AluOpType
ACT = mybir.ActivationFunctionType
AX = mybir.AxisListType

P = 128
NODES = 3125
EDGES = 50000
D = 256
HEADS = 4
DK = D // HEADS
RELS20 = 20
RELS8 = 8
NTYPES = 4
SQRT_DK = 8.0
EPS = 1e-5

NT = -(-NODES // P)
LAST = NODES - (NT - 1) * P
ROWS = NT * P
EP = 125
EJ = EDGES // EP
TILE_UNROLL = 8
TILES = -(-((EDGES + NT * (P - 1)) // P) // TILE_UNROLL) * TILE_UNROLL
CHUNK = TILE_UNROLL // 2
GATHERS_PER_STAGE = 16 * (TILES // TILE_UNROLL)
ACCW = D + HEADS
REC = 8
F_ROW20, F_SRC, F_ROW8, F_DST, F_WEIGHT = range(5)
NO_DST = 255.0
BIG = 3.0e38


class Named:
    pass


def window(buf, t, lo=0, hi=None):
    hi = buf.shape[2] if hi is None else hi
    return buf[:, bass.ds(t, 1), lo:hi].rearrange("p a b -> p (a b)")


def sems(ctx, nc, stage, *names):
    return [ctx.enter_context(nc.semaphore(f"{stage}_{n}")) for n in names]


def bank(m, b, lo, hi):
    return m.ps[:, b, lo:hi]


def constants(nc, m):
    with ExitStack() as ctx:
        made, used = sems(ctx, nc, "const", "made", "used")
        block = ctx.enter_context(nc.Block())

        @block.gpsimd
        def _(pool):
            nc.gpsimd.iota(m.iota_i[:, :], [[1, P]], base=0, channel_multiplier=0).then_inc(made, 1)
            nc.gpsimd.iota(m.iota_p[:, :], [[1, 1]], base=0, channel_multiplier=1).then_inc(made, 1)

        @block.vector
        def _(dve):
            dve.wait_ge(made, 2)
            nc.vector.tensor_copy(m.cols[:, :], m.iota_i[:, :]).then_inc(used, 1)
            nc.vector.tensor_copy(m.rowid[:, :], m.iota_p[:, :]).then_inc(used, 1)
            nc.vector.memset(m.ones[:, :], 1.0).then_inc(used, 1)
            nc.vector.memset(m.eps[:, :], EPS).then_inc(used, 1)
            dve.wait_ge(used, 2)
            nc.vector.tensor_scalar(m.ident[:, :], m.cols[:, :], m.rowid[:, :], None, ALU.is_equal)
            nc.vector.tensor_scalar(m.lower[:, :], m.cols[:, :], m.rowid[:, :], None, ALU.is_gt)


def sort_and_relation_table(nc, m, a):
    with ExitStack() as ctx:
        def sb(name, shape, dt=F32):
            return ctx.enter_context(nc.sbuf_tensor(name, shape, dt))

        dst_i = sb("dst_i", [EP, EJ], I32)
        src_i = sb("src_i", [EP, EJ], I32)
        r20_i = sb("r20_i", [EP, EJ], I32)
        r8_i = sb("r8_i", [EP, EJ], I32)
        weight = sb("weight", [EP, EJ])
        fld = sb("fld", [EP, 4, EJ])
        onehot = sb("onehot", [EP, NT, EJ], BF16)
        count = sb("count", [EP, NT, EJ])
        small = sb("small", [P, 8, NT + 1])
        small_i = sb("small_i", [P, 2, NT + 1], I32)
        tiles_f = sb("tiles_f", [1, TILES])
        tiles_i = sb("tiles_i", [1, TILES], I32)
        cmp = sb("cmp", [1, TILES])
        rec = sb("rec", [EP, EJ, REC])
        pos = sb("pos", [EP, EJ])
        slots = sb("slots", [EP, 2, 8], I32)
        rows = sb("rows", [EP, 2, 8, REC])
        w20 = sb("w20", [P, 2, RELS20 * D])
        xs = sb("xs0", [P, 2, D])
        xt = sb("xt0", [P, 2, 2, P])
        half = RELS20 * D // 2
        tb = sb("tb0", [P, 2, half])

        (inputs, edges_in, x_in, x_zero, w_in, blank, chain, sums_ready, totals, sorted_, staged,
         xs_ready, turned, xt_ready, product, evac_dve, evac_act, edge_ids, records_in) = sems(
            ctx, nc, "sort", "inputs", "edges_in", "x_in", "x_zero", "w_in", "blank", "chain", "sums_ready",
            "totals", "sorted", "staged", "xs_ready", "turned", "xt_ready", "product", "evac_dve",
            "evac_act", "edge_ids", "records_in")
        scattered = sems(ctx, nc, "sort", "scattered0", "scattered1")
        stored = sems(ctx, nc, "sort", "stored0", "stored1")
        block = ctx.enter_context(nc.Block())
        GROUPS = RELS20 * D // 512
        HG = GROUPS // 2
        table = m.table20.rearrange("(n r) d -> n (r d)", r=RELS20)
        SG = 8
        NG = EJ // SG

        @block.sync
        def _(sp):
            ev = lambda v: v.rearrange("(p j) -> p j", p=EP)
            sp.dma_start(dst_i[:, :], ev(a.dst)).then_inc(edges_in, 16)
            sp.wait_ge(x_zero, 1)
            sp.dma_start(m.x[:, 0:NT - 1, :], a.x[0:(NT - 1) * P, :].rearrange("(t p) d -> p t d", p=P)).then_inc(x_in, 16)
            sp.dma_start(m.x[0:LAST, NT - 1, :], a.x[(NT - 1) * P:NODES, :]).then_inc(x_in, 16)
            for r in range(RELS20):
                sp.dma_start(w20[:, :, r * D:(r + 1) * D], a.w20[r].rearrange("(k p) d -> p k d", p=P)).then_inc(w_in, 16)
            sp.dma_start(src_i[:, :], ev(a.src)).then_inc(inputs, 16)
            sp.dma_start(r20_i[:, :], ev(a.rel20)).then_inc(inputs, 16)
            sp.dma_start(r8_i[:, :], ev(a.rel8)).then_inc(inputs, 16)
            sp.dma_start(weight[:, :], a.weight.rearrange("(p j) o -> p (j o)", p=EP)).then_inc(inputs, 16)
            sp.wait_ge(blank, 2)
            sp.dma_start(m.records.rearrange("(p t) f -> p t f", p=P), m.rec[:, :, :]).then_inc(records_in, 16)

            def store(t, h):
                sp.dma_start(table[bass.ds(t * P, P), h * half:(h + 1) * half], tb[:, h, :]).then_inc(stored[h], 16)

            with sp.Fori(0, NT, 1) as t:
                for h in (0, 1):
                    sp.wait_ge(evac_dve, t * 5 + (3 if h == 0 else 5))
                    sp.sem_inc(m.sp_tick, 1)
                    sp.wait_ge(evac_act, t * 5 + (2 if h == 0 else 5))
                    sp.sem_inc(m.sp_tick, 1)
                    store(t, h)
            for h in (0, 1):
                sp.wait_ge(stored[h], 16 * NT)
                sp.wait_ge(scattered[h], 16 * (SG * NG // 2))

        @block.gpsimd
        def _(pool):
            pool.wait_ge(records_in, 16)
            with pool.Fori(0, NG, 2) as g:
                for b in (0, 1):
                    pool.wait_ge(staged, 2 * g + (2 * b + 2))
                    pool.sem_inc(m.tick, 1)
                    for j in range(SG):
                        pool.indirect_dma_start(
                            out=m.records, out_offset=bass.IndirectOffsetOnAxis(ap=slots[:, b, j:j + 1], axis=0),
                            in_=rows[:, b, j, :], in_offset=None).then_inc(scattered[b], 16)

        @block.scalar
        def _(act):
            act.wait_ge(x_in, 32)

            def node_tile(t, p):
                if isinstance(t, int) and t == 0:
                    act.wait_ge(x_in, 32)
                else:
                    act.wait_ge(turned, t - 0)
                act.wait_ge(x_in, 32)
                nc.scalar.activation(xs[:, 0, :], window(m.x, t), ACT.Copy).then_inc(xs_ready, 1)
                for g in range(GROUPS):
                    if g % 2:
                        if not (isinstance(t, int) and t == 0):
                            act.wait_ge(stored[g // HG], t * 16)
                        act.wait_ge(product, t * GROUPS + g + 1)
                        nc.scalar.activation(tb[:, g // HG, (g % HG) * 512:(g % HG + 1) * 512], bank(m, g % 6, 0, 512),
                                             ACT.Copy).then_inc(evac_act, 1)

            node_tile(0, 0)
            with act.Fori(1, NT, 1) as t:
                node_tile(t, 0)

        @block.tensor
        def _(pe):
            pe.wait_ge(sums_ready, 1)
            pe.matmul(bank(m, 7, 0, NT), m.lower[0:EP, 0:P], small[0:EP, 0, 0:NT], start=True, stop=True)
            pe.matmul(bank(m, 7, 64, 64 + NT), m.ones[0:EP, :], small[0:EP, 0, 0:NT], start=True, stop=True).then_inc(totals, 1)
            pe.wait_ge(w_in, 16 * RELS20)

            def node_tile(t, first):
                pe.wait_ge(xs_ready, t + 1)
                for k in (0, 1):
                    mm = pe.transpose(bank(m, 6, k * P, (k + 1) * P), xs[:, 0, k * P:(k + 1) * P], m.ident[:, :])
                mm.then_inc(turned, 1)
                pe.wait_ge(xt_ready, t + 1)
                for g in range(GROUPS):
                    if g >= 6:
                        if g % 2:
                            pe.wait_ge(evac_act, t * 5 + (g - 6) // 2 + 1)
                        else:
                            pe.wait_ge(evac_dve, t * 5 + (g - 6) // 2 + 1)
                    elif not first:
                        pe.wait_ge(evac_act, t * 5)
                        pe.wait_ge(evac_dve, t * 5)
                    for k in (0, 1):
                        mm = pe.matmul(bank(m, g % 6, 0, 512), xt[:, 0, k, :], w20[:, k, g * 512:(g + 1) * 512],
                                       start=(k == 0), stop=(k == 1))
                    mm.then_inc(product, 1)

            node_tile(0, True)
            with pe.Fori(1, NT, 1) as t:
                node_tile(t, False)

        @block.vector
        def _(dve):
            steps = [0]

            def step(ins):
                steps[0] += 1
                ins.then_inc(chain, 1)
                dve.wait_ge(chain, steps[0])

            nc.vector.memset(m.x[:, NT - 1, :], 0.0).then_inc(x_zero, 1)
            nc.vector.memset(m.rec[:, :, :], 0.0).then_inc(blank, 1)
            dve.wait_ge(blank, 1)
            nc.vector.memset(m.rec[:, :, F_DST], NO_DST).then_inc(blank, 1)

            dve.wait_ge(edges_in, 16)
            step(nc.vector.tensor_single_scalar(r8_win := fld_i(fld, 0), dst_i[:, :], 7, op=ALU.logical_shift_right))
            step(nc.vector.tensor_copy(fld[:, 1, :], r8_win))
            step(nc.vector.tensor_tensor(onehot[:, :, :], fld[:, 1:2, :].to_broadcast([EP, NT, EJ]),
                                         m.cols[0:EP, 0:NT].rearrange("p (b o) -> p b o", o=1).to_broadcast([EP, NT, EJ]),
                                         ALU.is_equal))
            oh_flat = onehot[:, :, :].rearrange("p b j -> p (b j)")
            step(nc.vector.tensor_tensor_scan(count[:, :, :].rearrange("p b j -> p (b j)"), oh_flat, oh_flat, 0.0,
                                              ALU.add, ALU.max))
            ends = count[:, :, EJ - 1]
            sm = lambda k, w=NT: small[0:EP, k, 0:w]
            step(nc.vector.memset(small[:, 1, :], 0.0))
            step(nc.vector.tensor_copy(small[0:EP, 1, 1:NT + 1], ends))
            step(nc.vector.tensor_tensor(small[0:EP, 0, 0:NT], small[0:EP, 1, 1:NT + 1], small[0:EP, 1, 0:NT], ALU.subtract))
            nc.vector.tensor_copy(small[0:EP, 7, 0:NT], small[0:EP, 0, 0:NT]).then_inc(sums_ready, 1)
            dve.wait_ge(totals, 1)
            step(nc.vector.tensor_scalar(small_i[:, 0, 0:NT], bank(m, 7, 64, 64 + NT), float(P - 1), None, ALU.add))
            step(nc.vector.tensor_single_scalar(small_i[:, 1, 0:NT], small_i[:, 0, 0:NT], 7, op=ALU.logical_shift_right))
            step(nc.vector.tensor_copy(small[:, 2, 0:NT], small_i[:, 1, 0:NT]))
            step(nc.vector.memset(small[:, 3, :], 0.0))
            step(nc.vector.tensor_tensor_scan(small[:, 3, 1:NT + 1], small[:, 2, 0:NT], small[:, 2, 0:NT], 0.0, ALU.add, ALU.max))
            step(nc.vector.scalar_tensor_tensor(sm(4), sm(3), float(P), bank(m, 7, 0, NT)[0:EP, :], ALU.mult, ALU.add))
            step(nc.vector.tensor_tensor(sm(5), sm(4), sm(1), ALU.subtract))
            step(nc.vector.tensor_scalar(sm(6), sm(5), -1.0, None, ALU.add))
            step(nc.vector.tensor_tensor(count[:, :, :], count[:, :, :],
                                         small[0:EP, 6, 0:NT].rearrange("p (b o) -> p b o", o=1).to_broadcast([EP, NT, EJ]), ALU.add))
            step(nc.vector.tensor_tensor(count[:, :, :], count[:, :, :], onehot[:, :, :], ALU.mult))
            step(nc.vector.tensor_reduce(pos[:, :], count[:, :, :].rearrange("p b j -> p j b"), AX.X, ALU.add))
            step(nc.vector.tensor_copy(fld_i(fld, 0), pos[:, :]))
            step(nc.vector.tensor_single_scalar(fld_i(fld, 2), fld_i(fld, 0), 7, op=ALU.logical_shift_right))
            step(nc.vector.tensor_single_scalar(fld_i(fld, 3), fld_i(fld, 0), P - 1, op=ALU.bitwise_and))
            step(nc.vector.tensor_copy(fld[:, 0, :], fld_i(fld, 3)))
            step(nc.vector.tensor_copy(pos[:, :], fld_i(fld, 2)))
            step(nc.vector.scalar_tensor_tensor(pos[:, :], fld[:, 0, :], float(TILES), pos[:, :], ALU.mult, ALU.add))
            dve.wait_ge(inputs, 64)
            step(nc.vector.memset(rec[:, :, :], 0.0))
            step(nc.vector.tensor_copy(fld[:, 2, :], dst_i[:, :]))
            step(nc.vector.scalar_tensor_tensor(rec[:, :, F_DST], fld[:, 1, :], -float(P), fld[:, 2, :], ALU.mult, ALU.add))
            step(nc.vector.tensor_copy(fld[:, 0, :], src_i[:, :]))
            step(nc.vector.tensor_copy(rec[:, :, F_SRC], fld[:, 0, :]))
            step(nc.vector.scalar_tensor_tensor(rec[:, :, F_ROW20], fld[:, 0, :], float(RELS20), r20_i[:, :], ALU.mult, ALU.add))
            step(nc.vector.scalar_tensor_tensor(rec[:, :, F_ROW8], fld[:, 0, :], float(RELS8), r8_i[:, :], ALU.mult, ALU.add))
            step(nc.vector.tensor_copy(rec[:, :, F_WEIGHT], weight[:, :]))
            step(nc.vector.memset(tiles_f[:, :], -1.0))
            for b in range(NT):
                step(nc.vector.tensor_scalar(cmp[:, :], m.tile_ids[0:1, :], small[0:1, 3, b:b + 1], None, ALU.is_ge))
                step(nc.vector.tensor_tensor(tiles_f[:, :], tiles_f[:, :], cmp[:, :], ALU.add))
            step(nc.vector.tensor_copy(m.win[0:1, :], tiles_f[:, :]))
            done = steps[0]

            def stage(g, b, first):
                if not first:
                    dve.wait_ge(scattered[b], (g - b) * (SG * 8))
                    dve.wait_ge(chain, done)
                nc.vector.tensor_copy(slots[:, b, :], pos[:, bass.ds(g * SG, SG)]).then_inc(staged, 1)
                nc.vector.tensor_copy(rows[:, b, :, :], rec[:, bass.ds(g * SG, SG), :]).then_inc(staged, 1)

            def node_tile(t, first):
                dve.wait_ge(turned, t + 1)
                nc.vector.tensor_copy(xt[:, 0, :, :], bank(m, 6, 0, D).rearrange("p (k n) -> p k n", k=2)).then_inc(xt_ready, 1)
                for g in range(0, GROUPS, 2):
                    if not first:
                        dve.wait_ge(stored[g // HG], t * 16)
                    dve.wait_ge(product, t * GROUPS + g + 1)
                    nc.vector.tensor_copy(tb[:, g // HG, (g % HG) * 512:(g % HG + 1) * 512],
                                          bank(m, g % 6, 0, 512)).then_inc(evac_dve, 1)

            stage(0, 0, True)
            stage(1, 1, True)
            node_tile(0, True)
            with dve.Fori(1, NT, 1) as t:
                for b in (0, 1):
                    stage(t * 2 + b, b, False)
                node_tile(t, False)

    with ExitStack() as ctx:
        back, = sems(ctx, nc, "sorted", "records_back")
        block = ctx.enter_context(nc.Block())

        @block.sync
        def _(sp):
            sp.dma_start(m.rec[:, :, :], m.records.rearrange("(p t) f -> p t f", p=P)).then_inc(back, 16)
            sp.wait_ge(back, 16)


def fld_i(fld, k):
    return fld[:, k, :].bitcast(I32)


def chunk_of_records(act, nc, m, t, par, field, free, c_free, ready):
    act.wait_ge(free, c_free)
    act.wait_ge(free, 1)
    nc.scalar.activation(m.rows_i[:, par, :], m.rec[:, bass.ds(t, CHUNK), field], ACT.Copy)
    nc.scalar.activation(m.chunk[:, par, :, :], m.rec[:, bass.ds(t, CHUNK), :], ACT.Copy).then_inc(ready, 1)


def gather(pool, table, m, k, par, j, sem):
    pool.indirect_dma_start(
        out=m.g[:, k, 0:D], out_offset=None, in_=table,
        in_offset=bass.IndirectOffsetOnAxis(ap=m.rows_i[:, par, j:j + 1], axis=0)).then_inc(sem, 16)


def aggregate_edges(nc, m, stage, table, field, weighted=False, count=False):
    width = D + 1 if count else D
    with ExitStack() as ctx:
        gathered, base = m.gathered, m.gathers_before
        m.gathers_before += GATHERS_PER_STAGE
        multiplied, onehot_ready, added, chunk_ready = sems(
            ctx, nc, stage, "multiplied", "onehot_ready", "added", "chunk_ready")
        block = ctx.enter_context(nc.Block())

        @block.gpsimd
        def _(pool):
            with pool.Fori(0, TILES // TILE_UNROLL, 1) as turn:
                i = turn * TILE_UNROLL
                for k in range(TILE_UNROLL):
                    if k % CHUNK == 0:
                        pool.wait_ge(chunk_ready, turn * 2 + k // CHUNK + 1)
                    pool.wait_ge(multiplied, i + k + 1)
                    pool.sem_inc(m.tick, 1)
                    gather(pool, table, m, k, k // CHUNK, k % CHUNK, gathered[k])

        @block.scalar
        def _(act):
            with act.Fori(0, TILES // TILE_UNROLL, 1) as turn:
                i = turn * TILE_UNROLL
                for c in (0, 1):
                    chunk_of_records(act, nc, m, i + c * CHUNK, c, field, multiplied, i + (c + 1) * CHUNK, chunk_ready)

        @block.tensor
        def _(pe):
            pe.sem_inc(multiplied, TILE_UNROLL)
            with pe.Fori(0, TILES // TILE_UNROLL, 1) as turn:
                i = turn * TILE_UNROLL
                for k in range(TILE_UNROLL):
                    pe.wait_ge(gathered[k], base + turn * 16 + 16)
                    pe.wait_ge(added, i + k + 1)
                    pe.wait_ge(onehot_ready, i + k + 1)
                    pe.matmul(bank(m, k, 0, width), m.onehot[:, k, :], m.g[:, k, 0:width],
                              start=True, stop=True).then_inc(multiplied, 1)

        @block.vector
        def _(dve):
            if count:
                nc.vector.memset(m.g[:, :, D:D + 1], 1.0).then_inc(added, TILE_UNROLL)
            else:
                dve.sem_inc(added, TILE_UNROLL)
            with dve.Fori(0, TILES // TILE_UNROLL, 1) as turn:
                i = turn * TILE_UNROLL
                for c in (0, 1):
                    wins = [dve.value_load(m.win[0:1, bass.ds(i + (c * CHUNK + j), 1)], min_val=0, max_val=NT - 1)
                            for j in range(CHUNK)]
                    dve.wait_ge(chunk_ready, turn * 2 + c + 1)
                    for j in range(CHUNK):
                        k = c * CHUNK + j
                        dve.wait_ge(multiplied, i + k + 1)
                        rec = m.chunk[:, c, j, :]
                        if weighted:
                            nc.vector.tensor_scalar(m.onehot[:, k, :], m.cols[:, :], rec[:, F_DST:F_DST + 1],
                                                    rec[:, F_WEIGHT:F_WEIGHT + 1], ALU.is_equal, ALU.mult).then_inc(onehot_ready, 1)
                        else:
                            nc.vector.tensor_scalar(m.onehot[:, k, :], m.cols[:, :], rec[:, F_DST:F_DST + 1], None,
                                                    ALU.is_equal).then_inc(onehot_ready, 1)
                    for j in range(CHUNK):
                        k = c * CHUNK + j
                        dve.wait_ge(multiplied, i + k + 1 + TILE_UNROLL)
                        dve.wait_ge(added, i + k + TILE_UNROLL)
                        acc = window(m.acc, wins[j], 0, width)
                        nc.vector.tensor_tensor(acc, acc, bank(m, k, 0, width), ALU.add).then_inc(added, 1)


def attention_scores(nc, m):
    R = 4
    with ExitStack() as ctx:
        def sb(name, shape, dt=F32):
            return ctx.enter_context(nc.sbuf_tensor(name, shape, dt))

        onehot_t = sb("onehot_t", [P, R, P])
        off = sb("off", [P, R, P])
        masked = sb("masked", [P, R, HEADS, P])
        prod = sb("prod", [P, D])
        sc = sb("sc", [P, R, HEADS])
        tmax = sb("tmax", [P, HEADS])
        gathered, base = m.gathered, m.gathers_before
        m.gathers_before += GATHERS_PER_STAGE
        (multiplied, onehot_ready, chunk_ready, turned, turned_copied, q_spread, scored, masked_ready,
         masked_turned, maxed, own) = sems(
            ctx, nc, "score", "multiplied", "onehot_ready", "chunk_ready", "turned", "turned_copied",
            "q_spread", "scored", "masked_ready", "masked_turned", "maxed", "own")
        block = ctx.enter_context(nc.Block())

        @block.gpsimd
        def _(pool):
            with pool.Fori(0, TILES // TILE_UNROLL, 1) as turn:
                i = turn * TILE_UNROLL
                for k in range(TILE_UNROLL):
                    if k % CHUNK == 0:
                        pool.wait_ge(chunk_ready, turn * 2 + k // CHUNK + 1)
                    pool.wait_ge(scored, i + k + 1)
                    pool.sem_inc(m.tick, 1)
                    gather(pool, m.table8k, m, k, k // CHUNK, k % CHUNK, gathered[k])

        @block.tensor
        def _(pe):
            pe.wait_ge(own, 1)

            def max_part(t, k):
                pe.wait_ge(masked_ready, t + 1)
                pe.wait_ge(maxed, t + 1)
                for h in range(HEADS):
                    mm = pe.transpose(bank(m, 4 + k % 4, h * P, (h + 1) * P), masked[:, k % R, h, :], m.ident[:, :])
                mm.then_inc(masked_turned, 1)

            with pe.Fori(0, TILES // TILE_UNROLL, 1) as turn:
                i = turn * TILE_UNROLL
                for c in (0, 1):
                    wins = [pe.value_load(m.win[0:1, bass.ds(i + (c * CHUNK + j), 1)], min_val=0, max_val=NT - 1)
                            for j in range(CHUNK)]
                    for j in range(CHUNK):
                        k = c * CHUNK + j
                        pe.wait_ge(turned_copied, i + k + 1)
                        pe.wait_ge(onehot_ready, i + k + 1)
                        pe.transpose(bank(m, k % 2, 0, P), m.onehot[:, k, :], m.ident[:, :]).then_inc(turned, 1)
                        pe.wait_ge(scored, i + k + 7)
                        pe.wait_ge(turned_copied, i + k + 3)
                        pe.matmul(bank(m, 2 + k % 2, 0, D), onehot_t[:, k % R, :], window(m.q, wins[j]),
                                  start=True, stop=True).then_inc(q_spread, 1)
                    for j in range(CHUNK):
                        max_part(i + (c * CHUNK + j), c * CHUNK + j)

        @block.scalar
        def _(act):
            act.wait_ge(own, 1)
            with act.Fori(0, TILES // TILE_UNROLL, 1) as turn:
                i = turn * TILE_UNROLL
                for c in (0, 1):
                    chunk_of_records(act, nc, m, i + c * CHUNK, c, F_ROW8, scored, i + (c + 1) * CHUNK, chunk_ready)
                    for j in range(CHUNK):
                        k = c * CHUNK + j
                        act.wait_ge(q_spread, i + k + 1)
                        act.wait_ge(turned, i + k + 1)
                        nc.scalar.activation(onehot_t[:, k % R, :], bank(m, k % 2, 0, P), ACT.Copy).then_inc(turned_copied, 1)
                    for j in range(CHUNK):
                        k = c * CHUNK + j
                        act.wait_ge(masked_turned, i + k + 1)
                        act.wait_ge(scored, i + k + 1 + TILE_UNROLL)
                        for h in range(HEADS):
                            ins = nc.scalar.activation(masked[:, k % R, h, :], off[:, k % R, :], ACT.Identity,
                                                       bias=sc[:, k % R, h:h + 1], scale=1.0)
                        ins.then_inc(masked_ready, 1)

        @block.vector
        def _(dve):
            dve.sem_inc(scored, TILE_UNROLL)
            dve.sem_inc(turned_copied, 2)
            dve.sem_inc(q_spread, R)
            dve.sem_inc(masked_turned, R)
            dve.sem_inc(maxed, R)
            nc.vector.memset(m.mx[:, :, :], -BIG).then_inc(own, 1)
            with dve.Fori(0, TILES // TILE_UNROLL, 1) as turn:
                i = turn * TILE_UNROLL
                for c in (0, 1):
                    wins = [dve.value_load(m.win[0:1, bass.ds(i + (c * CHUNK + j), 1)], min_val=0, max_val=NT - 1)
                            for j in range(CHUNK)]
                    dve.wait_ge(chunk_ready, turn * 2 + c + 1)
                    for j in range(CHUNK):
                        k = c * CHUNK + j
                        dst = m.chunk[:, c, j, F_DST:F_DST + 1]
                        nc.vector.tensor_scalar(m.onehot[:, k, :], m.cols[:, :], dst, None, ALU.is_equal).then_inc(onehot_ready, 1)
                        nc.vector.tensor_scalar(off[:, k % R, :], m.cols[:, :], dst, -BIG, ALU.not_equal, ALU.mult)
                    for j in range(CHUNK):
                        k = c * CHUNK + j
                        dve.wait_ge(gathered[k], base + turn * 16 + 16)
                        dve.wait_ge(q_spread, i + k + 1 + R)
                        nc.vector.tensor_tensor(prod[:, :], m.g[:, k, 0:D], bank(m, 2 + k % 2, 0, D), ALU.mult).then_inc(own, 1)
                        dve.wait_ge(own, (i + k) * 2 + 2)
                        nc.vector.tensor_reduce(sc[:, k % R, :], prod[:, :].rearrange("p (h d) -> p h d", h=HEADS),
                                                AX.X, ALU.add).then_inc(scored, 1)
                        dve.wait_ge(scored, i + k + 1 + TILE_UNROLL)
                        nc.vector.tensor_copy(window(m.scores, i + k), sc[:, k % R, :]).then_inc(own, 1)
                    for j in range(CHUNK):
                        k = c * CHUNK + j
                        dve.wait_ge(masked_turned, i + k + 1 + R)
                        nc.vector.tensor_reduce(tmax[:, :], bank(m, 4 + k % 4, 0, 512).rearrange("p (h e) -> p h e", h=HEADS),
                                                AX.X, ALU.max).then_inc(maxed, 1)
                        dve.wait_ge(maxed, i + k + 1 + R)
                        mx = window(m.mx, wins[j])
                        nc.vector.tensor_tensor(mx, mx, tmax[:, :], ALU.max).then_inc(m.mx_written, 1)
                        dve.wait_ge(m.mx_written, i + k + 1)


def attention_sum(nc, m):
    R = 4
    with ExitStack() as ctx:
        def sb(name, shape, dt=F32):
            return ctx.enter_context(nc.sbuf_tensor(name, shape, dt))

        onehot_t = sb("onehot_t2", [P, R, P])
        diff = sb("diff", [P, R, HEADS])
        vx = sb("vx", [P, R, ACCW])
        gathered, base = m.gathered, m.gathers_before
        m.gathers_before += GATHERS_PER_STAGE
        (multiplied, onehot_ready, chunk_ready, turned, turned_copied, max_spread, diff_ready, exp_ready,
         weighted, added) = sems(
            ctx, nc, "sum", "multiplied", "onehot_ready", "chunk_ready", "turned", "turned_copied",
            "max_spread", "diff_ready", "exp_ready", "weighted", "added")
        block = ctx.enter_context(nc.Block())

        @block.gpsimd
        def _(pool):
            with pool.Fori(0, TILES // TILE_UNROLL, 1) as turn:
                i = turn * TILE_UNROLL
                for k in range(TILE_UNROLL):
                    if k % CHUNK == 0:
                        pool.wait_ge(chunk_ready, turn * 2 + k // CHUNK + 1)
                    pool.wait_ge(multiplied, i + k + 1)
                    pool.sem_inc(m.tick, 1)
                    gather(pool, m.table8v, m, k, k // CHUNK, k % CHUNK, gathered[k])

        @block.tensor
        def _(pe):
            pe.sem_inc(multiplied, TILE_UNROLL)
            with pe.Fori(0, TILES // TILE_UNROLL, 1) as turn:
                i = turn * TILE_UNROLL
                for c in (0, 1):
                    wins = [pe.value_load(m.win[0:1, bass.ds(i + (c * CHUNK + j), 1)], min_val=0, max_val=NT - 1)
                            for j in range(CHUNK)]
                    for j in range(CHUNK):
                        k = c * CHUNK + j
                        pe.wait_ge(turned_copied, i + k + 1)
                        pe.wait_ge(onehot_ready, i + k + 1)
                        pe.transpose(bank(m, k % 2, 0, P), m.onehot[:, k, :], m.ident[:, :]).then_inc(turned, 1)
                        pe.wait_ge(diff_ready, i + k + 1)
                        pe.wait_ge(turned_copied, i + k + 3)
                        pe.matmul(bank(m, 2 + k % 2, 0, HEADS), onehot_t[:, k % R, :], window(m.mx, wins[j]),
                                  start=True, stop=True).then_inc(max_spread, 1)
                    for j in range(CHUNK):
                        k = c * CHUNK + j
                        pe.wait_ge(added, i + k + 1)
                        pe.wait_ge(weighted, i + k + 1)
                        pe.matmul(bank(m, 4 + k % 4, 0, ACCW), m.onehot[:, k, :], vx[:, k % R, :],
                                  start=True, stop=True).then_inc(multiplied, 1)

        @block.scalar
        def _(act):
            with act.Fori(0, TILES // TILE_UNROLL, 1) as turn:
                i = turn * TILE_UNROLL
                for c in (0, 1):
                    chunk_of_records(act, nc, m, i + c * CHUNK, c, F_ROW8, multiplied, i + (c + 1) * CHUNK, chunk_ready)
                    for j in range(CHUNK):
                        k = c * CHUNK + j
                        act.wait_ge(max_spread, i + k + 1)
                        act.wait_ge(turned, i + k + 1)
                        nc.scalar.activation(onehot_t[:, k % R, :], bank(m, k % 2, 0, P), ACT.Copy).then_inc(turned_copied, 1)
                    for j in range(CHUNK):
                        k = c * CHUNK + j
                        act.wait_ge(multiplied, i + k + 5)
                        act.wait_ge(diff_ready, i + k + 3)
                        nc.scalar.activation(vx[:, k % R, D:ACCW], diff[:, k % R, :], ACT.Exp).then_inc(exp_ready, 1)

        @block.vector
        def _(dve):
            dve.sem_inc(turned_copied, 2)
            dve.sem_inc(diff_ready, 2)
            dve.sem_inc(max_spread, R)
            dve.sem_inc(exp_ready, R)
            dve.sem_inc(added, R)
            with dve.Fori(0, TILES // TILE_UNROLL, 1) as turn:
                i = turn * TILE_UNROLL
                for c in (0, 1):
                    wins = [dve.value_load(m.win[0:1, bass.ds(i + (c * CHUNK + j), 1)], min_val=0, max_val=NT - 1)
                            for j in range(CHUNK)]
                    dve.wait_ge(chunk_ready, turn * 2 + c + 1)
                    for j in range(CHUNK):
                        k = c * CHUNK + j
                        dve.wait_ge(multiplied, i + k + 1)
                        nc.vector.tensor_scalar(m.onehot[:, k, :], m.cols[:, :], m.chunk[:, c, j, F_DST:F_DST + 1], None,
                                                ALU.is_equal).then_inc(onehot_ready, 1)
                    for j in range(CHUNK):
                        k = c * CHUNK + j
                        dve.wait_ge(exp_ready, i + k + 1)
                        dve.wait_ge(max_spread, i + k + 1 + R)
                        nc.vector.tensor_tensor(diff[:, k % R, :], window(m.scores, i + k), bank(m, 2 + k % 2, 0, HEADS),
                                                ALU.subtract).then_inc(diff_ready, 1)
                    for j in range(CHUNK):
                        k = c * CHUNK + j
                        dve.wait_ge(gathered[k], base + turn * 16 + 16)
                        dve.wait_ge(exp_ready, i + k + 1 + R)
                        for h in range(HEADS):
                            ins = nc.vector.tensor_scalar(vx[:, k % R, h * DK:(h + 1) * DK], m.g[:, k, h * DK:(h + 1) * DK],
                                                          vx[:, k % R, D + h:D + h + 1], None, ALU.mult)
                        ins.then_inc(weighted, 1)
                    for j in range(CHUNK):
                        k = c * CHUNK + j
                        dve.wait_ge(multiplied, i + k + 1 + TILE_UNROLL)
                        dve.wait_ge(added, i + k + R)
                        acc = window(m.acc, wins[j])
                        nc.vector.tensor_tensor(acc, acc, bank(m, 4 + k % 4, 0, ACCW), ALU.add).then_inc(added, 1)


def layer_norm(nc, m, stage, prepare, out):
    with ExitStack() as ctx:
        chain, stats_ready, root_ready = sems(ctx, nc, stage, "norm_chain", "norm_stats", "norm_root")
        block = ctx.enter_context(nc.Block())

        @block.vector
        def _(dve):
            steps = [0]

            def step(ins):
                steps[0] += 1
                ins.then_inc(chain, 1)
                dve.wait_ge(chain, steps[0])

            prepare(step)
            for t in range(NT):
                step_or_none = nc.vector.bn_stats(m.stats[:, t, :], m.acc[:, t, 0:D])
            step(step_or_none)
            for t in range(NT):
                last = nc.vector.bn_aggr(m.mv[:, t, :], m.stats[:, t, :])
            last.then_inc(stats_ready, 1)
            dve.wait_ge(root_ready, 1)
            step(nc.vector.reciprocal(m.rstd[:, :], m.std[:, :]))
            for t in range(NT):
                nc.vector.tensor_scalar(out[:, t, 0:D], m.acc[:, t, 0:D], m.mv[:, t, 0:1], m.rstd[:, t:t + 1],
                                        ALU.subtract, ALU.mult)

        @block.scalar
        def _(act):
            act.wait_ge(stats_ready, 1)
            nc.scalar.activation(m.std[:, :], m.mv[:, :, 1], ACT.Sqrt, bias=m.eps[:, :], scale=1.0).then_inc(root_ready, 1)


def dense_pair(nc, m, stage, src, w_left, w_right, table, left_scale, left_keep, right_keep, right_bias):
    with ExitStack() as ctx:
        def sb(name, shape, dt=F32):
            return ctx.enter_context(nc.sbuf_tensor(f"{stage}_{name}", shape, dt))

        w = sb("w", [P, 2, 2 * D])
        xs = sb("xs", [P, 2, D])
        xt = sb("xt", [P, 2, 2, P])
        tb = sb("tb", [P, 2, D])
        weights_in, xs_ready, turned, xt_ready, product, tb_ready, kept = sems(
            ctx, nc, stage, "weights_in", "xs_ready", "turned", "xt_ready", "product", "tb_ready", "kept")
        stored = [sems(ctx, nc, stage, f"stored{b}")[0] for b in (0, 1)]
        block = ctx.enter_context(nc.Block())
        KEEPS = 1 + (left_keep is not None)

        def over_tiles(eng, tile):
            tile(0, 0, True)
            tile(1, 1, True)
            with eng.Fori(1, NT // 2, 1) as pair:
                t = pair * 2
                tile(t, 0, False)
                tile(t + 1, 1, False)
            tile(NT - 1, 0, False)

        @block.sync
        def _(sp):
            sp.dma_start(w[:, :, 0:D], w_left.rearrange("(k p) d -> p k d", p=P)).then_inc(weights_in, 16)
            sp.dma_start(w[:, :, D:2 * D], w_right.rearrange("(k p) d -> p k d", p=P)).then_inc(weights_in, 16)

            def tile(t, b, first):
                sp.wait_ge(tb_ready, t + 1)
                sp.dma_start(table[bass.ds(t * P, P), :], tb[:, b, :]).then_inc(stored[b], 16)

            over_tiles(sp, tile)
            sp.wait_ge(stored[0], 16 * (NT // 2 + 1))
            sp.wait_ge(stored[1], 16 * (NT // 2))

        @block.tensor
        def _(pe):
            def tile(t, b, first):
                if not first:
                    pe.wait_ge(xt_ready, t - 1)
                pe.wait_ge(xs_ready, t + 1)
                for k in (0, 1):
                    mm = pe.transpose(bank(m, b, k * P, (k + 1) * P), xs[:, b, k * P:(k + 1) * P], m.ident[:, :])
                mm.then_inc(turned, 1)
                if first:
                    pe.wait_ge(weights_in, 32)
                else:
                    pe.wait_ge(tb_ready, t - 1)
                    pe.wait_ge(kept, KEEPS * (t - 1))
                pe.wait_ge(xt_ready, t + 1)
                for side in (0, 1):
                    for k in (0, 1):
                        mm = pe.matmul(bank(m, 2 + 2 * side + b, 0, D), xt[:, b, k, :], w[:, k, side * D:(side + 1) * D],
                                       start=(k == 0), stop=(k == 1))
                mm.then_inc(product, 1)

            over_tiles(pe, tile)

        @block.scalar
        def _(act):
            def load(t, b, first):
                if not first:
                    act.wait_ge(turned, t - 1)
                    act.wait_ge(turned, 1)
                nc.scalar.activation(xs[:, b, :], window(src, t, 0, D), ACT.Copy).then_inc(xs_ready, 1)

            def tile(t, b, first):
                if not first:
                    act.wait_ge(stored[b], (t - b) * 8)
                    if left_keep is not None:
                        act.wait_ge(kept, 2 * (t - 1))
                act.wait_ge(product, t + 1)
                if left_scale is None:
                    nc.scalar.activation(tb[:, b, :], bank(m, 2 + b, 0, D), ACT.Copy).then_inc(tb_ready, 1)
                else:
                    act.wait_ge(product, 1)
                    nc.scalar.activation(tb[:, b, :], bank(m, 2 + b, 0, D), ACT.Copy,
                                         scale=left_scale[:, bass.ds(t, 1)]).then_inc(tb_ready, 1)

            load(0, 0, True)
            load(1, 1, True)
            tile(0, 0, True)
            load(2, 0, False)
            tile(1, 1, True)
            with act.Fori(1, NT // 2, 1) as pair:
                t = pair * 2
                load(t + 1, 1, False)
                tile(t, 0, False)
                load(t + 2, 0, False)
                tile(t + 1, 1, False)
            tile(NT - 1, 0, False)

        @block.vector
        def _(dve):
            def tile(t, b, first):
                if not first:
                    dve.wait_ge(product, t - 1)
                dve.wait_ge(turned, t + 1)
                nc.vector.tensor_copy(xt[:, b, :, :], bank(m, b, 0, D).rearrange("p (k n) -> p k n", k=2)).then_inc(xt_ready, 1)
                dve.wait_ge(product, t + 1)
                right = bank(m, 4 + b, 0, D)
                if right_bias is None:
                    nc.vector.tensor_copy(window(right_keep, t, 0, D), right).then_inc(kept, 1)
                else:
                    nc.vector.tensor_tensor(window(right_keep, t, 0, D), right_bias, right, ALU.add).then_inc(kept, 1)
                if left_keep is not None:
                    dve.wait_ge(tb_ready, t + 1)
                    nc.vector.tensor_copy(window(left_keep, t, 0, D), tb[:, b, :]).then_inc(kept, 1)

            over_tiles(dve, tile)


def attention_tables(nc, m, a):
    with ExitStack() as ctx:
        def sb(name, shape, dt=F32):
            return ctx.enter_context(nc.sbuf_tensor(name, shape, dt))

        w = sb("w_kvq", [P, 2, NTYPES, 3 * D])
        xs = sb("xs5", [P, D])
        xm = sb("xm5", [P, NTYPES, 2, P])
        kv = sb("kv5", [P, 2 * D])
        kvt = sb("kvt5", [P, 4, P])
        rel = sb("rel", [P, 2, 2, RELS8 * DK])
        att = sb("att", [DK, 2, RELS8, P])
        pri = sb("pri", [P, RELS8 * HEADS])
        tb = sb("tb5", [P, 2, RELS8, D])
        types_i = sb("types_i", [P, ROWS], I32)
        (weights_in, rel_in, types_zero, types_in, chain, rel_ready, xs_ready, turned, xm_ready, typed, kv_ready,
         kv_turned, kvt_ready, product, even, odd, q_kept, att_turned) = sems(
            ctx, nc, "att", "weights_in", "rel_in", "types_zero", "types_in", "chain", "rel_ready", "xs_ready", "turned",
            "xm_ready", "typed", "kv_ready", "kv_turned", "kvt_ready", "product", "even", "odd", "q_kept", "att_turned")
        stored = sems(ctx, nc, "att", "stored_k", "stored_v")
        block = ctx.enter_context(nc.Block())
        tables = [m.table8k.rearrange("(n r) d -> n (r d)", r=RELS8), m.table8v.rearrange("(n r) d -> n (r d)", r=RELS8)]

        @block.sync
        def _(sp):
            for j, src in enumerate((a.k_lin, a.v_lin, a.q_lin)):
                for ty in range(NTYPES):
                    sp.dma_start(w[:, :, ty, j * D:(j + 1) * D], src[ty].rearrange("(k p) d -> p k d", p=P)).then_inc(weights_in, 16)
            for h in range(HEADS):
                o = (h % 2) * DK
                sp.dma_start(att[:, h // 2, :, o:o + DK], a.rel_att[:, h, :, :].rearrange("r d e -> d r e")).then_inc(rel_in, 16)
                sp.dma_start(rel[o:o + DK, 1, h // 2, :].rearrange("p (r e) -> p r e", r=RELS8),
                             a.rel_msg[:, h, :, :].rearrange("r d e -> d r e")).then_inc(rel_in, 16)
            sp.dma_start(pri[:, :], a.pri.rearrange("(o r) h -> o (r h)", o=1).to_broadcast([P, RELS8 * HEADS])).then_inc(rel_in, 16)
            sp.wait_ge(types_zero, 1)
            sp.dma_start(types_i[:, 0:NODES], a.node_type.rearrange("(o n) -> o n", o=1).to_broadcast([P, NODES])).then_inc(types_in, 16)
            with sp.Fori(0, NT, 1) as t:
                for j in (0, 1):
                    sp.wait_ge(even, t * 4 + 2 * j + 2)
                    sp.wait_ge(odd, t * 4 + 2 * j + 2)
                    sp.dma_start(tables[j][bass.ds(t * P, P), :], tb[:, j, :, :].rearrange("p r d -> p (r d)")).then_inc(stored[j], 16)
            for j in (0, 1):
                sp.wait_ge(stored[j], 16 * NT)

        @block.tensor
        def _(pe):
            def tile(t, first):
                pe.wait_ge(xs_ready, t + 1)
                for k in (0, 1):
                    mm = pe.transpose(bank(m, 0, k * P, (k + 1) * P), xs[:, k * P:(k + 1) * P], m.ident[:, :])
                mm.then_inc(turned, 1)
                if first:
                    pe.wait_ge(weights_in, 16 * 3 * NTYPES)
                else:
                    pe.wait_ge(q_kept, t)
                pe.wait_ge(xm_ready, t + 1)
                n = 0
                for ty in range(NTYPES):
                    for k in (0, 1):
                        for b, lo, hi in ((1, 0, 2 * D), (2, 2 * D, 3 * D)):
                            mm = pe.matmul(bank(m, b, 0, hi - lo), xm[:, ty, k, :], w[:, k, ty, lo:hi],
                                           start=(n == 0), stop=(n == 2 * NTYPES - 1))
                        n += 1
                mm.then_inc(typed, 1)
                pe.wait_ge(kv_ready, t + 1)
                for c in range(4):
                    mm = pe.transpose(bank(m, 3, c * P, (c + 1) * P), kv[:, c * P:(c + 1) * P], m.ident[:, :])
                mm.then_inc(kv_turned, 1)
                if first:
                    pe.wait_ge(rel_ready, 1)
                pe.wait_ge(kvt_ready, t + 1)
                for g in range(8):
                    j, h = g // HEADS, g % HEADS
                    s, n = (odd, t * 4 + g // 2 - 1) if g % 2 else (even, t * 4 + g // 2 - 1)
                    if g >= 4 or not first:
                        pe.wait_ge(s, n)
                    o = (h % 2) * DK
                    pe.matmul(bank(m, 4 + g % 4, 0, 512), kvt[o:o + DK, 2 * j + h // 2, :], rel[o:o + DK, j, h // 2, :],
                              start=True, stop=True).then_inc(product, 1)

            pe.wait_ge(rel_in, 16 * 9)
            for hh in (0, 1):
                for r in range(RELS8):
                    mm = pe.transpose(bank(m, 4 + hh, r * DK, (r + 1) * DK), att[:, hh, r, :], m.ident[0:DK, 0:DK])
            mm.then_inc(att_turned, 1)
            tile(0, True)
            with pe.Fori(1, NT, 1) as t:
                tile(t, False)

        def to_table(eng, copy, t, first, half, done):
            for g in range(half, 8, 2):
                j, h = g // HEADS, g % HEADS
                if not first:
                    eng.wait_ge(stored[j], t * 16)
                eng.wait_ge(product, t * 8 + g + 1)
                copy(tb[:, j, :, h * DK:(h + 1) * DK], bank(m, 4 + g % 4, 0, 512).rearrange("p (r e) -> p r e", r=RELS8)).then_inc(done, 1)

        @block.scalar
        def _(act):
            copy = lambda o, i: nc.scalar.activation(o, i, ACT.Copy)
            copy(xs[:, :], m.x[:, 0, :]).then_inc(xs_ready, 1)

            def tile(t, first, last):
                act.wait_ge(typed, t + 1)
                copy(kv[:, :], bank(m, 1, 0, 512)).then_inc(kv_ready, 1)
                if not last:
                    act.wait_ge(turned, t + 1)
                    act.wait_ge(turned, 1)
                    copy(xs[:, :], window(m.x, t + 1)).then_inc(xs_ready, 1)
                act.wait_ge(kv_turned, t + 1)
                copy(kvt[:, :, :], bank(m, 3, 0, 512).rearrange("p (c n) -> p c n", c=4)).then_inc(kvt_ready, 1)
                to_table(act, copy, t, first, 1, odd)

            tile(0, True, False)
            with act.Fori(1, NT - 1, 1) as t:
                tile(t, False, False)
            tile(NT - 1, False, True)

        @block.vector
        def _(dve):
            steps = [0]

            def step(ins):
                steps[0] += 1
                ins.then_inc(chain, 1)
                dve.wait_ge(chain, steps[0])

            nc.vector.memset(types_i[:, :], 0).then_inc(types_zero, 1)
            dve.wait_ge(rel_in, 16 * 9)
            step(nc.vector.tensor_scalar(pri[:, :], pri[:, :], 1.0 / SQRT_DK, None, ALU.mult))
            dve.wait_ge(att_turned, 1)
            for h in range(HEADS):
                o = (h % 2) * DK
                view = lambda v: v.rearrange("p (r e) -> p r e", r=RELS8)
                by = pri[o:o + DK, :].rearrange("p (r h) -> p r h", h=HEADS)[:, :, h:h + 1].to_broadcast([DK, RELS8, DK])
                ins = nc.vector.tensor_tensor(view(rel[o:o + DK, 0, h // 2, :]), by,
                                              view(m.ps[o:o + DK, 4 + h // 2, 0:512]), ALU.mult)
            ins.then_inc(rel_ready, 1)
            dve.wait_ge(types_in, 16)

            def tile(t, first):
                if not first:
                    dve.wait_ge(typed, t)
                dve.wait_ge(turned, t + 1)
                for ty in range(NTYPES):
                    for k in (0, 1):
                        ins = nc.vector.scalar_tensor_tensor(
                            xm[:, ty, k, :], types_i[:, bass.ds(t * P, P)], float(ty),
                            bank(m, 0, k * P, (k + 1) * P), ALU.is_equal, ALU.mult)
                ins.then_inc(xm_ready, 1)
                dve.wait_ge(typed, t + 1)
                nc.vector.tensor_copy(window(m.q, t), bank(m, 2, 0, D)).then_inc(q_kept, 1)
                to_table(dve, nc.vector.tensor_copy, t, first, 0, even)

            tile(0, True)
            with dve.Fori(1, NT, 1) as t:
                tile(t, False)


def attention_output(nc, m, a):
    with ExitStack() as ctx:
        def sb(name, shape, dt=F32):
            return ctx.enter_context(nc.sbuf_tensor(name, shape, dt))

        w = sb("w_a", [P, 2, NTYPES * D])
        xs = sb("xs8", [P, 2, D])
        xt = sb("xt8", [P, 2, 2, P])
        rden = sb("rden", [P, NT, HEADS])
        types_i = sb("types_i8", [P, NT], I32)
        skip = sb("skip", [P, NTYPES])
        gate = sb("gate", [P, NTYPES])
        gates = sb("gates", [P, NTYPES, NT])
        tmp = sb("tmp8", [P, 4, D])
        weights_in, small_in, types_zero, chain, exp_ready, divided, xs_ready, turned, xt_ready, product, summed, own = sems(
            ctx, nc, "out", "weights_in", "small_in", "types_zero", "chain", "exp_ready", "divided", "xs_ready",
            "turned", "xt_ready", "product", "summed", "own")
        block = ctx.enter_context(nc.Block())

        @block.sync
        def _(sp):
            sp.dma_start(skip[:, :], a.skip.rearrange("(o n) -> o n", o=1).to_broadcast([P, NTYPES])).then_inc(small_in, 16)
            sp.wait_ge(types_zero, 1)
            with nc.allow_non_contiguous_dma(reason="a node per partition"):
                sp.dma_start(types_i[:, 0:NT - 1], a.node_type[0:(NT - 1) * P].rearrange("(t p) -> p t", p=P)).then_inc(small_in, 16)
                sp.dma_start(types_i[0:LAST, NT - 1:NT], a.node_type[(NT - 1) * P:NODES].rearrange("(p o) -> p o", o=1)).then_inc(small_in, 16)
            for ty in range(NTYPES):
                sp.dma_start(w[:, :, ty * D:(ty + 1) * D], a.a_lin[ty].rearrange("(k p) d -> p k d", p=P)).then_inc(weights_in, 16)

        @block.tensor
        def _(pe):
            pe.wait_ge(weights_in, 16 * NTYPES)

            def tile(t, first):
                pe.wait_ge(xs_ready, t + 1)
                for k in (0, 1):
                    mm = pe.transpose(bank(m, 0, k * P, (k + 1) * P), xs[:, 0, k * P:(k + 1) * P], m.ident[:, :])
                mm.then_inc(turned, 1)
                if not first:
                    pe.wait_ge(summed, t)
                pe.wait_ge(xt_ready, t + 1)
                for k in (0, 1):
                    for b in (0, 1):
                        mm = pe.matmul(bank(m, 1 + b, 0, 512), xt[:, 0, k, :], w[:, k, b * 512:(b + 1) * 512],
                                       start=(k == 0), stop=(k == 1))
                mm.then_inc(product, 1)

            tile(0, True)
            with pe.Fori(1, NT, 1) as t:
                tile(t, False)

        @block.scalar
        def _(act):
            act.wait_ge(small_in, 48)
            nc.scalar.activation(gate[:, :], skip[:, :], ACT.Exp, scale=-1.0).then_inc(exp_ready, 1)
            act.wait_ge(divided, 1)
            nc.scalar.activation(xs[:, 0, :], m.acc[:, 0, 0:D], ACT.Copy).then_inc(xs_ready, 1)
            with act.Fori(1, NT, 1) as t:
                act.wait_ge(turned, t)
                act.wait_ge(turned, 1)
                nc.scalar.activation(xs[:, 0, :], window(m.acc, t, 0, D), ACT.Copy).then_inc(xs_ready, 1)

        @block.vector
        def _(dve):
            steps = [0]

            def step(ins):
                steps[0] += 1
                ins.then_inc(chain, 1)
                dve.wait_ge(chain, steps[0])

            nc.vector.memset(types_i[:, :], 0).then_inc(types_zero, 1)
            step(nc.vector.tensor_scalar(rden[:, :, :], m.acc[:, :, D:ACCW], 1e-30, None, ALU.max))
            step(nc.vector.reciprocal(rden[:, :, :], rden[:, :, :]))
            for h in range(HEADS):
                v = m.acc[:, :, h * DK:(h + 1) * DK]
                ins = nc.vector.tensor_tensor(v, v, rden[:, :, h:h + 1].to_broadcast([P, NT, DK]), ALU.mult)
            ins.then_inc(divided, 1)
            dve.wait_ge(exp_ready, 1)
            step(nc.vector.tensor_scalar(gate[:, :], gate[:, :], 1.0, None, ALU.add))
            step(nc.vector.reciprocal(skip[:, :], gate[:, :]))
            for ty in range(NTYPES):
                ins = nc.vector.tensor_scalar(gates[:, ty, :], types_i[:, :], float(ty), skip[:, ty:ty + 1], ALU.is_equal, ALU.mult)
            step(ins)

            def tile(t, first):
                if not first:
                    dve.wait_ge(product, t)
                dve.wait_ge(turned, t + 1)
                nc.vector.tensor_copy(xt[:, 0, :, :], bank(m, 0, 0, D).rearrange("p (k n) -> p k n", k=2)).then_inc(xt_ready, 1)
                dve.wait_ge(product, t + 1)
                for ty in range(NTYPES):
                    prev = window(m.x, t) if ty == 0 else tmp[:, ty - 1, :]
                    out = window(m.acc, t, 0, D) if ty == NTYPES - 1 else tmp[:, ty, :]
                    if ty:
                        dve.wait_ge(own, t * 3 + ty)
                    ins = nc.vector.scalar_tensor_tensor(out, bank(m, 1 + ty // 2, (ty % 2) * D, (ty % 2 + 1) * D),
                                                         gates[:, ty, bass.ds(t, 1)], prev, ALU.mult, ALU.add)
                    ins.then_inc(own if ty < NTYPES - 1 else summed, 1)

            tile(0, True)
            with dve.Fori(1, NT, 1) as t:
                tile(t, False)


def vector_block(nc, m, stage, body):
    with ExitStack() as ctx:
        chain, = sems(ctx, nc, stage, "chain")
        block = ctx.enter_context(nc.Block())

        @block.vector
        def _(dve):
            steps = [0]

            def step(ins):
                steps[0] += 1
                ins.then_inc(chain, 1)
                dve.wait_ge(chain, steps[0])

            body(step)


def four_graph_layers(nc, a, out):
    with ExitStack() as ctx:
        def sb(name, shape, dt=F32):
            return ctx.enter_context(nc.sbuf_tensor(name, shape, dt))

        m = Named()
        m.iota_i = sb("iota_i", [P, P], I32)
        m.iota_p = sb("iota_p", [P, 1], I32)
        m.cols = sb("cols", [P, P])
        m.rowid = sb("rowid", [P, 1])
        m.ones = sb("ones", [P, P])
        m.eps = sb("eps", [P, 1])
        m.ident = sb("ident", [P, P])
        m.lower = sb("lower", [P, P])
        m.tile_ids = sb("tile_ids", [1, TILES])
        m.win = sb("win", [1, TILES], I32)
        m.x = sb("x", [P, NT, D])
        m.rec = sb("rec_all", [P, TILES, REC])
        m.ps = ctx.enter_context(nc.psum_tensor("ps", [P, 8, 512], F32))
        m.records = nc.dram_tensor("records", (P * TILES, REC), F32, kind="Internal").ap()
        m.table20 = nc.dram_tensor("table20", (ROWS * RELS20, D), F32, kind="Internal").ap()
        m.table1 = nc.dram_tensor("table1", (ROWS, D), F32, kind="Internal").ap()
        m.table8k = nc.dram_tensor("table8k", (ROWS * RELS8, D), F32, kind="Internal").ap()
        m.table8v = nc.dram_tensor("table8v", (ROWS * RELS8, D), F32, kind="Internal").ap()

        m.tick, m.sp_tick = sems(ctx, nc, "own", "tick", "sp_tick")
        constants(nc, m)
        with ExitStack() as c2:
            made, = sems(c2, nc, "ids", "made")
            ids_i = c2.enter_context(nc.sbuf_tensor("ids_i", [1, TILES], I32))
            block = c2.enter_context(nc.Block())

            @block.gpsimd
            def _(pool):
                nc.gpsimd.iota(ids_i[:, :], [[1, TILES]], base=0, channel_multiplier=0).then_inc(made, 1)

            @block.vector
            def _(dve):
                dve.wait_ge(made, 1)
                nc.vector.tensor_copy(m.tile_ids[:, :], ids_i[:, :])

        sort_and_relation_table(nc, m, a)

        m.acc = sb("acc", [P, NT, ACCW])
        m.rows_i = sb("rows_i", [P, 2, CHUNK], I32)
        m.chunk = sb("chunk", [P, 2, CHUNK, REC])
        m.onehot = sb("onehot_e", [P, TILE_UNROLL, P])
        m.g = sb("gathered", [P, TILE_UNROLL, ACCW])
        m.stats = sb("stats", [P, NT, 6])
        m.mv = sb("mv", [P, NT, 2])
        m.std = sb("std", [P, NT])
        m.rstd = sb("rstd", [P, NT])
        m.dis = sb("dis", [P, NT])
        m.q = sb("q", [P, NT, D])
        m.mx = sb("mx", [P, NT, HEADS])
        m.scores = sb("scores", [P, TILES, HEADS])
        m.bias = sb("bias", [P, 3, D])
        m.gathered = sems(ctx, nc, "all", *(f"gathered{k}" for k in range(TILE_UNROLL)))
        m.gathers_before = 0
        m.mx_written, m.bias_in = sems(ctx, nc, "all", "mx_written", "bias_in")
        feat = m.acc[:, :, 0:D]

        def relu_add(step):
            step(nc.vector.scalar_tensor_tensor(feat, feat, 0.0, m.x[:, :, :], ALU.max, ALU.add))

        vector_block(nc, m, "zero", lambda step: step(nc.vector.memset(m.acc[:, :, :], 0.0)))
        aggregate_edges(nc, m, "rel", m.table20, F_ROW20, weighted=True)
        layer_norm(nc, m, "rel", relu_add, m.x)

        vector_block(nc, m, "count", lambda step: step(nc.vector.memset(m.acc[:, :, D:ACCW], 0.0)))
        dense_pair(nc, m, "conv", m.x, a.m1, a.w1, m.table1, None, None, m.acc, None)
        aggregate_edges(nc, m, "conv_edges", m.table1, F_SRC, count=True)

        def after_conv(step):
            relu_add(step)
            step(nc.vector.tensor_scalar(m.dis[:, :], m.acc[:, :, D], 1.0, None, ALU.add))
        layer_norm(nc, m, "conv", after_conv, m.x)

        with ExitStack() as c2:
            rooted, = sems(c2, nc, "dis", "rooted")
            block = c2.enter_context(nc.Block())

            @block.scalar
            def _(act):
                nc.scalar.activation(m.std[:, :], m.dis[:, :], ACT.Sqrt).then_inc(rooted, 1)

            @block.vector
            def _(dve):
                nc.vector.memset(m.acc[:, :, :], 0.0)
                dve.wait_ge(rooted, 1)
                nc.vector.reciprocal(m.dis[:, :], m.std[:, :])

            @block.sync
            def _(sp):
                for k, v in enumerate((a.b[0], a.b[1], a.resb)):
                    sp.dma_start(m.bias[:, k, :], v.rearrange("(o n) -> o n", o=1).to_broadcast([P, D])).then_inc(m.bias_in, 16)
                sp.wait_ge(m.bias_in, 48)

        attention_tables(nc, m, a)
        attention_scores(nc, m)
        attention_sum(nc, m)
        attention_output(nc, m, a)
        layer_norm(nc, m, "att", lambda step: None, m.x)

        def biases(step):
            for k in (0, 1):
                step(nc.vector.tensor_tensor(m.bias[:, k, :], m.bias[:, k, :], m.bias[:, 2, :], ALU.add))
        vector_block(nc, m, "bias", biases)
        h = m.acc2 = sb("h", [P, NT, D])

        def conv_out(step, into):
            for t in range(NT):
                ins = nc.vector.scalar_tensor_tensor(into[:, t, 0:D], m.acc[:, t, 0:D], m.dis[:, t:t + 1], m.q[:, t, :],
                                                     ALU.mult, ALU.add)
            step(ins)

        dense_pair(nc, m, "gcn0", m.x, a.w3[0], a.resw, m.table1, m.dis, m.acc, m.q, m.bias[:, 0, :])
        aggregate_edges(nc, m, "gcn0_edges", m.table1, F_SRC)

        def hidden(step):
            conv_out(step, h)
            step(nc.vector.tensor_scalar(h[:, :, :], h[:, :, :], 0.0, None, ALU.max))
        vector_block(nc, m, "gcn0_out", hidden)
        dense_pair(nc, m, "gcn1", h, a.w3[1], a.resw, m.table1, m.dis, m.acc, m.q, m.bias[:, 1, :])
        aggregate_edges(nc, m, "gcn1_edges", m.table1, F_SRC)

        def last(step):
            conv_out(step, m.acc)
            relu_add(step)
        layer_norm(nc, m, "gcn", last, h)

        with ExitStack() as c2:
            stored, = sems(c2, nc, "end", "stored")
            block = c2.enter_context(nc.Block())

            @block.sync
            def _(sp):
                sp.dma_start(out[0:(NT - 1) * P, :].rearrange("(t p) d -> p t d", p=P), h[:, 0:NT - 1, :]).then_inc(stored, 16)
                sp.dma_start(out[(NT - 1) * P:NODES, :], h[0:LAST, NT - 1, :]).then_inc(stored, 16)
                sp.wait_ge(stored, 32)


_INS = {
    "x": "x", "src": "src", "dst": "dst", "rel20": "edge_type_20", "rel8": "edge_type_8", "weight": "edge_weight1",
    "node_type": "node_type_4", "w20": "L0_gnn_weight", "w1": "L1_gnn_W", "m1": "L1_gnn_M",
    "k_lin": "L2_gnn_k_linears", "q_lin": "L2_gnn_q_linears", "v_lin": "L2_gnn_v_linears", "a_lin": "L2_gnn_a_linears",
    "rel_att": "L2_gnn_relation_att", "rel_msg": "L2_gnn_relation_msg", "pri": "L2_gnn_relation_pri",
    "skip": "L2_gnn_skip", "w3": "L3_gnn_W", "b": "L3_gnn_b", "resw": "L3_gnn_resW", "resb": "L3_gnn_resb",
}


def kernel(**inputs):
    import numpy as np
    import concourse.bacc as bacc
    from concourse.bass_utils import run_bass_kernel_spmd

    nc = bacc.Bacc("TRN2", target_bir_lowering=False, num_devices=1)
    arrays, a = {}, Named()
    for short, name in _INS.items():
        v = np.ascontiguousarray(inputs[name])
        arrays[f"in_{short}"] = v
        a.__dict__[short] = nc.dram_tensor(f"in_{short}", v.shape, mybir.dt.from_np(v.dtype), kind="ExternalInput").ap()
    out = nc.dram_tensor("out_x", (NODES, D), F32, kind="ExternalOutput").ap()
    four_graph_layers(nc, a, out)
    r = run_bass_kernel_spmd(nc, [arrays], core_ids=[0])
    return r.results[0]["out_x"]
```

```python
from contextlib import ExitStack

import concourse.bass as bass
from concourse import mybir

F32 = mybir.dt.float32
I32 = mybir.dt.int32
BF16 = mybir.dt.bfloat16
ALU = mybir.AluOpType
ACT = mybir.ActivationFunctionType
AX = mybir.AxisListType

P = 128
NODES = 3125
EDGES = 50000
D = 256
HEADS = 4
DK = D // HEADS
RELS20 = 20
RELS8 = 8
NTYPES = 4
SQRT_DK = 8.0
EPS = 1e-5

NT = -(-NODES // P)
LAST = NODES - (NT - 1) * P
ROWS = NT * P
EP = 125
EJ = EDGES // EP
SLOTS = 16
TILES = -(-((EDGES + NT * (P - 1)) // P) // SLOTS) * SLOTS
CHUNK = 4
CHUNKS = SLOTS // CHUNK
GATHERS_PER_STAGE = 16 * (TILES // SLOTS)
ACCW = D + HEADS
REC = 8
F_ROW20, F_SRC, F_ROW8, F_DST, F_WEIGHT = range(5)
NO_DST = 255.0
BIG = 3.0e38


class Named:
    pass


def window(buf, t, lo=0, hi=None):
    hi = buf.shape[2] if hi is None else hi
    return buf[:, bass.ds(t, 1), lo:hi].rearrange("p a b -> p (a b)")


def sems(ctx, nc, stage, *names):
    return [ctx.enter_context(nc.semaphore(f"{stage}_{n}")) for n in names]


def bank(m, b, lo, hi):
    return m.ps[:, b, lo:hi]


def constants(nc, m):
    with ExitStack() as ctx:
        made, used = sems(ctx, nc, "const", "made", "used")
        m.spent = [made, used]
        block = ctx.enter_context(nc.Block())

        @block.gpsimd
        def _(pool):
            nc.gpsimd.iota(m.iota_i[:, :], [[1, P]], base=0, channel_multiplier=0).then_inc(made, 1)
            nc.gpsimd.iota(m.iota_p[:, :], [[1, 1]], base=0, channel_multiplier=1).then_inc(made, 1)

        @block.vector
        def _(dve):
            dve.wait_ge(made, 2)
            nc.vector.tensor_copy(m.cols[:, :], m.iota_i[:, :]).then_inc(used, 1)
            nc.vector.tensor_copy(m.rowid[:, :], m.iota_p[:, :]).then_inc(used, 1)
            nc.vector.memset(m.ones[:, :], 1.0).then_inc(used, 1)
            nc.vector.memset(m.eps[:, :], EPS).then_inc(used, 1)
            dve.wait_ge(used, 2)
            nc.vector.tensor_scalar(m.ident[:, :], m.cols[:, :], m.rowid[:, :], None, ALU.is_equal)
            nc.vector.tensor_scalar(m.lower[:, :], m.cols[:, :], m.rowid[:, :], None, ALU.is_gt)


def sort_and_relation_table(nc, m, a):
    with ExitStack() as ctx:
        def sb(name, shape, dt=F32):
            return ctx.enter_context(nc.sbuf_tensor(name, shape, dt))

        dst_i = sb("dst_i", [EP, EJ], I32)
        src_i = sb("src_i", [EP, EJ], I32)
        r20_i = sb("r20_i", [EP, EJ], I32)
        r8_i = sb("r8_i", [EP, EJ], I32)
        weight = sb("weight", [EP, EJ])
        fld = sb("fld", [EP, 4, EJ])
        onehot = sb("onehot", [EP, NT, EJ], BF16)
        count = sb("count", [EP, NT, EJ])
        small = sb("small", [P, 8, NT + 1])
        small_i = sb("small_i", [P, 2, NT + 1], I32)
        tiles_f = sb("tiles_f", [1, TILES])
        tiles_i = sb("tiles_i", [1, TILES], I32)
        cmp = sb("cmp", [1, TILES])
        rec = sb("rec", [EP, EJ, REC])
        pos = sb("pos", [EP, EJ])
        slots = sb("slots", [EP, 2, 8], I32)
        rows = sb("rows", [EP, 2, 8, REC])
        w20 = sb("w20", [P, 2, RELS20 * D])
        xs = sb("xs0", [P, 2, D])
        xt = sb("xt0", [P, 2, 2, P])
        half = RELS20 * D // 2
        tb = sb("tb0", [P, 2, half])

        (inputs, edges_in, x_in, x_zero, w_in, blank, chain, sums_ready, totals, sorted_, staged,
         xs_ready, turned, xt_ready, product, evac_dve, evac_act, edge_ids, records_in) = sems(
            ctx, nc, "sort", "inputs", "edges_in", "x_in", "x_zero", "w_in", "blank", "chain", "sums_ready",
            "totals", "sorted", "staged", "xs_ready", "turned", "xt_ready", "product", "evac_dve",
            "evac_act", "edge_ids", "records_in")
        scattered = m.scattered
        stored = sems(ctx, nc, "sort", "stored0", "stored1")
        m.spent += (inputs, edges_in, x_in, x_zero, w_in, blank, chain, sums_ready, totals, sorted_, staged, xs_ready,
                      turned, xt_ready, product, evac_dve, evac_act, edge_ids, records_in, *stored)
        block = ctx.enter_context(nc.Block())
        GROUPS = RELS20 * D // 512
        HG = GROUPS // 2
        table = m.table20.rearrange("(n r) d -> n (r d)", r=RELS20)
        SG = 8
        NG = EJ // SG

        @block.sync
        def _(sp):
            ev = lambda v: v.rearrange("(p j) -> p j", p=EP)
            sp.dma_start(dst_i[:, :], ev(a.dst)).then_inc(edges_in, 16)
            sp.wait_ge(x_zero, 1)
            sp.dma_start(m.x[:, 0:NT - 1, :], a.x[0:(NT - 1) * P, :].rearrange("(t p) d -> p t d", p=P)).then_inc(x_in, 16)
            sp.dma_start(m.x[0:LAST, NT - 1, :], a.x[(NT - 1) * P:NODES, :]).then_inc(x_in, 16)
            for r in range(RELS20):
                sp.dma_start(w20[:, :, r * D:(r + 1) * D], a.w20[r].rearrange("(k p) d -> p k d", p=P)).then_inc(w_in, 16)
            sp.dma_start(src_i[:, :], ev(a.src)).then_inc(inputs, 16)
            sp.dma_start(r20_i[:, :], ev(a.rel20)).then_inc(inputs, 16)
            sp.dma_start(r8_i[:, :], ev(a.rel8)).then_inc(inputs, 16)
            sp.dma_start(weight[:, :], a.weight.rearrange("(p j) o -> p (j o)", p=EP)).then_inc(inputs, 16)
            sp.wait_ge(blank, 2)
            sp.dma_start(m.records.rearrange("(p t) f -> p t f", p=P), m.rec[:, :, :]).then_inc(records_in, 16)

            def store(t, h):
                sp.dma_start(table[bass.ds(t * P, P), h * half:(h + 1) * half], tb[:, h, :]).then_inc(stored[h], 16)

            with sp.Fori(0, NT, 1) as t:
                for h in (0, 1):
                    sp.wait_ge(evac_dve, t * 5 + (3 if h == 0 else 5))
                    sp.sem_inc(m.sp_tick, 1)
                    sp.wait_ge(evac_act, t * 5 + (2 if h == 0 else 5))
                    sp.sem_inc(m.sp_tick, 1)
                    store(t, h)
            for h in (0, 1):
                sp.wait_ge(stored[h], 16 * NT)
                sp.wait_ge(scattered[h], 16 * (SG * NG // 2))

        @block.gpsimd
        def _(pool):
            pool.wait_ge(records_in, 16)
            with pool.Fori(0, NG, 2) as g:
                for b in (0, 1):
                    pool.wait_ge(staged, 2 * g + (2 * b + 2))
                    pool.sem_inc(m.tick, 1)
                    for j in range(SG):
                        pool.indirect_dma_start(
                            out=m.records, out_offset=bass.IndirectOffsetOnAxis(ap=slots[:, b, j:j + 1], axis=0),
                            in_=rows[:, b, j, :], in_offset=None).then_inc(scattered[b], 16)

        @block.scalar
        def _(act):
            act.wait_ge(x_in, 32)

            def node_tile(t, p):
                if isinstance(t, int) and t == 0:
                    act.wait_ge(x_in, 32)
                else:
                    act.wait_ge(turned, t - 0)
                act.wait_ge(x_in, 32)
                nc.scalar.activation(xs[:, 0, :], window(m.x, t), ACT.Copy).then_inc(xs_ready, 1)
                for g in range(GROUPS):
                    if g % 2:
                        if not (isinstance(t, int) and t == 0):
                            act.wait_ge(stored[g // HG], t * 16)
                        act.wait_ge(product, t * GROUPS + g + 1)
                        nc.scalar.activation(tb[:, g // HG, (g % HG) * 512:(g % HG + 1) * 512], bank(m, g % 6, 0, 512),
                                             ACT.Copy).then_inc(evac_act, 1)

            node_tile(0, 0)
            with act.Fori(1, NT, 1) as t:
                node_tile(t, 0)

        @block.tensor
        def _(pe):
            pe.wait_ge(sums_ready, 1)
            pe.matmul(bank(m, 7, 0, NT), m.lower[0:EP, 0:P], small[0:EP, 0, 0:NT], start=True, stop=True)
            pe.matmul(bank(m, 7, 64, 64 + NT), m.ones[0:EP, :], small[0:EP, 0, 0:NT], start=True, stop=True).then_inc(totals, 1)
            pe.wait_ge(w_in, 16 * RELS20)

            def node_tile(t, first):
                pe.wait_ge(xs_ready, t + 1)
                for k in (0, 1):
                    mm = pe.transpose(bank(m, 6, k * P, (k + 1) * P), xs[:, 0, k * P:(k + 1) * P], m.ident[:, :])
                mm.then_inc(turned, 1)
                pe.wait_ge(xt_ready, t + 1)
                for g in range(GROUPS):
                    if g >= 6:
                        if g % 2:
                            pe.wait_ge(evac_act, t * 5 + (g - 6) // 2 + 1)
                        else:
                            pe.wait_ge(evac_dve, t * 5 + (g - 6) // 2 + 1)
                    elif not first:
                        pe.wait_ge(evac_act, t * 5)
                        pe.wait_ge(evac_dve, t * 5)
                    for k in (0, 1):
                        mm = pe.matmul(bank(m, g % 6, 0, 512), xt[:, 0, k, :], w20[:, k, g * 512:(g + 1) * 512],
                                       start=(k == 0), stop=(k == 1))
                    mm.then_inc(product, 1)

            node_tile(0, True)
            with pe.Fori(1, NT, 1) as t:
                node_tile(t, False)

        @block.vector
        def _(dve):
            steps = [0]

            def step(ins):
                steps[0] += 1
                ins.then_inc(chain, 1)
                dve.wait_ge(chain, steps[0])

            nc.vector.memset(m.x[:, NT - 1, :], 0.0).then_inc(x_zero, 1)
            nc.vector.memset(m.rec[:, :, :], 0.0).then_inc(blank, 1)
            dve.wait_ge(blank, 1)
            nc.vector.memset(m.rec[:, :, F_DST], NO_DST).then_inc(blank, 1)

            dve.wait_ge(edges_in, 16)
            step(nc.vector.tensor_single_scalar(r8_win := fld_i(fld, 0), dst_i[:, :], 7, op=ALU.logical_shift_right))
            step(nc.vector.tensor_copy(fld[:, 1, :], r8_win))
            step(nc.vector.tensor_tensor(onehot[:, :, :], fld[:, 1:2, :].to_broadcast([EP, NT, EJ]),
                                         m.cols[0:EP, 0:NT].rearrange("p (b o) -> p b o", o=1).to_broadcast([EP, NT, EJ]),
                                         ALU.is_equal))
            oh_flat = onehot[:, :, :].rearrange("p b j -> p (b j)")
            step(nc.vector.tensor_tensor_scan(count[:, :, :].rearrange("p b j -> p (b j)"), oh_flat, oh_flat, 0.0,
                                              ALU.add, ALU.max))
            ends = count[:, :, EJ - 1]
            sm = lambda k, w=NT: small[0:EP, k, 0:w]
            step(nc.vector.memset(small[:, 1, :], 0.0))
            step(nc.vector.tensor_copy(small[0:EP, 1, 1:NT + 1], ends))
            step(nc.vector.tensor_tensor(small[0:EP, 0, 0:NT], small[0:EP, 1, 1:NT + 1], small[0:EP, 1, 0:NT], ALU.subtract))
            nc.vector.tensor_copy(small[0:EP, 7, 0:NT], small[0:EP, 0, 0:NT]).then_inc(sums_ready, 1)
            dve.wait_ge(totals, 1)
            step(nc.vector.tensor_scalar(small_i[:, 0, 0:NT], bank(m, 7, 64, 64 + NT), float(P - 1), None, ALU.add))
            step(nc.vector.tensor_single_scalar(small_i[:, 1, 0:NT], small_i[:, 0, 0:NT], 7, op=ALU.logical_shift_right))
            step(nc.vector.tensor_copy(small[:, 2, 0:NT], small_i[:, 1, 0:NT]))
            step(nc.vector.memset(small[:, 3, :], 0.0))
            step(nc.vector.tensor_tensor_scan(small[:, 3, 1:NT + 1], small[:, 2, 0:NT], small[:, 2, 0:NT], 0.0, ALU.add, ALU.max))
            step(nc.vector.scalar_tensor_tensor(sm(4), sm(3), float(P), bank(m, 7, 0, NT)[0:EP, :], ALU.mult, ALU.add))
            step(nc.vector.tensor_tensor(sm(5), sm(4), sm(1), ALU.subtract))
            step(nc.vector.tensor_scalar(sm(6), sm(5), -1.0, None, ALU.add))
            step(nc.vector.tensor_tensor(count[:, :, :], count[:, :, :],
                                         small[0:EP, 6, 0:NT].rearrange("p (b o) -> p b o", o=1).to_broadcast([EP, NT, EJ]), ALU.add))
            step(nc.vector.tensor_tensor(count[:, :, :], count[:, :, :], onehot[:, :, :], ALU.mult))
            step(nc.vector.tensor_reduce(pos[:, :], count[:, :, :].rearrange("p b j -> p j b"), AX.X, ALU.add))
            step(nc.vector.tensor_copy(fld_i(fld, 0), pos[:, :]))
            step(nc.vector.tensor_single_scalar(fld_i(fld, 2), fld_i(fld, 0), 7, op=ALU.logical_shift_right))
            step(nc.vector.tensor_single_scalar(fld_i(fld, 3), fld_i(fld, 0), P - 1, op=ALU.bitwise_and))
            step(nc.vector.tensor_copy(fld[:, 0, :], fld_i(fld, 3)))
            step(nc.vector.tensor_copy(pos[:, :], fld_i(fld, 2)))
            step(nc.vector.scalar_tensor_tensor(pos[:, :], fld[:, 0, :], float(TILES), pos[:, :], ALU.mult, ALU.add))
            dve.wait_ge(inputs, 64)
            step(nc.vector.memset(rec[:, :, :], 0.0))
            step(nc.vector.tensor_copy(fld[:, 2, :], dst_i[:, :]))
            step(nc.vector.scalar_tensor_tensor(rec[:, :, F_DST], fld[:, 1, :], -float(P), fld[:, 2, :], ALU.mult, ALU.add))
            step(nc.vector.tensor_copy(fld[:, 0, :], src_i[:, :]))
            step(nc.vector.tensor_copy(rec[:, :, F_SRC], fld[:, 0, :]))
            step(nc.vector.scalar_tensor_tensor(rec[:, :, F_ROW20], fld[:, 0, :], float(RELS20), r20_i[:, :], ALU.mult, ALU.add))
            step(nc.vector.scalar_tensor_tensor(rec[:, :, F_ROW8], fld[:, 0, :], float(RELS8), r8_i[:, :], ALU.mult, ALU.add))
            step(nc.vector.tensor_copy(rec[:, :, F_WEIGHT], weight[:, :]))
            step(nc.vector.memset(tiles_f[:, :], -1.0))
            for b in range(NT):
                step(nc.vector.tensor_scalar(cmp[:, :], m.tile_ids[0:1, :], small[0:1, 3, b:b + 1], None, ALU.is_ge))
                step(nc.vector.tensor_tensor(tiles_f[:, :], tiles_f[:, :], cmp[:, :], ALU.add))
            step(nc.vector.tensor_copy(m.win[0:1, :], tiles_f[:, :]))
            done = steps[0]

            def stage(g, b, first):
                if not first:
                    dve.wait_ge(scattered[b], (g - b) * (SG * 8))
                    dve.wait_ge(chain, done)
                nc.vector.tensor_copy(slots[:, b, :], pos[:, bass.ds(g * SG, SG)]).then_inc(staged, 1)
                nc.vector.tensor_copy(rows[:, b, :, :], rec[:, bass.ds(g * SG, SG), :]).then_inc(staged, 1)

            def node_tile(t, first):
                dve.wait_ge(turned, t + 1)
                nc.vector.tensor_copy(xt[:, 0, :, :], bank(m, 6, 0, D).rearrange("p (k n) -> p k n", k=2)).then_inc(xt_ready, 1)
                for g in range(0, GROUPS, 2):
                    if not first:
                        dve.wait_ge(stored[g // HG], t * 16)
                    dve.wait_ge(product, t * GROUPS + g + 1)
                    nc.vector.tensor_copy(tb[:, g // HG, (g % HG) * 512:(g % HG + 1) * 512],
                                          bank(m, g % 6, 0, 512)).then_inc(evac_dve, 1)

            stage(0, 0, True)
            stage(1, 1, True)
            node_tile(0, True)
            with dve.Fori(1, NT, 1) as t:
                for b in (0, 1):
                    stage(t * 2 + b, b, False)
                node_tile(t, False)

    with ExitStack() as ctx:
        back, = sems(ctx, nc, "sorted", "records_back")
        block = ctx.enter_context(nc.Block())

        @block.sync
        def _(sp):
            for s in m.spent:
                sp.sem_clear(s)
            sp.dma_start(m.rec[:, :, :], m.records.rearrange("(p t) f -> p t f", p=P)).then_inc(back, 16)
            sp.wait_ge(back, 16)


def fld_i(fld, k):
    return fld[:, k, :].bitcast(I32)


def edge_buffers(ctx, nc, m, stage):
    m.g = ctx.enter_context(nc.sbuf_tensor(f"{stage}_g", [P, SLOTS, ACCW], F32))
    m.onehot = ctx.enter_context(nc.sbuf_tensor(f"{stage}_onehot", [P, SLOTS, P], F32))
    m.dst_bc = ctx.enter_context(nc.sbuf_tensor(f"{stage}_dst_bc", [P, 2, CHUNK * P], F32))
    before = m.gathers_before
    m.gathers_before += GATHERS_PER_STAGE
    return m.gathered, before


def stage_records(act, nc, m, t, c, field, used, ready):
    act.wait_ge(used, t + CHUNK)
    act.wait_ge(used, 1)
    nc.scalar.activation(m.rows_i[:, c, :], m.rec[:, bass.ds(t, CHUNK), field], ACT.Copy)
    nc.scalar.activation(m.chunk[:, c, :, :], m.rec[:, bass.ds(t, CHUNK), :], ACT.Copy).then_inc(ready, 1)


def gather_all(pool, m, table, staged, used):
    with pool.Fori(0, TILES // SLOTS, 1) as turn:
        i = turn * SLOTS
        for k in range(SLOTS):
            if k % CHUNK == 0:
                pool.wait_ge(staged, turn * CHUNKS + k // CHUNK + 1)
            pool.wait_ge(used, i + k + 1)
            pool.sem_inc(m.tick, 1)
            pool.indirect_dma_start(
                out=m.g[:, k, 0:D], out_offset=None, in_=table,
                in_offset=bass.IndirectOffsetOnAxis(ap=m.rows_i[:, k // CHUNK, k % CHUNK:k % CHUNK + 1], axis=0)
            ).then_inc(m.gathered[k], 16)


def windows_of(eng, m, t):
    return [eng.value_load(m.win[0:1, bass.ds(t + j, 1)], min_val=0, max_val=NT - 1) for j in range(CHUNK)]


def over_chunks(eng, step, lag):
    total = TILES // CHUNK
    assert lag <= CHUNKS
    for s in range(CHUNKS):
        step(s, s, lambda d: s - d >= 0)
    with eng.Fori(1, total // CHUNKS, 1) as turn:
        for c in range(CHUNKS):
            step(turn * CHUNKS + c, c, lambda d: d >= 0)
    for s in range(total, total + lag):
        step(s, s % CHUNKS, lambda d: s - d < total)


def aggregate_edges(nc, m, stage, table, field, weighted=False, count=False):
    width = D + 1 if count else D
    BANKS = 8
    with ExitStack() as ctx:
        gathered, base = edge_buffers(ctx, nc, m, stage)
        multiplied, onehot_ready, added, staged = sems(
            ctx, nc, stage, "multiplied", "onehot_ready", "added", "staged")
        block = ctx.enter_context(nc.Block())

        @block.gpsimd
        def _(pool):
            gather_all(pool, m, table, staged, multiplied)

        @block.scalar
        def _(act):
            with act.Fori(0, TILES // SLOTS, 1) as turn:
                for c in range(CHUNKS):
                    stage_records(act, nc, m, turn * SLOTS + c * CHUNK, c, field, multiplied, staged)

        @block.tensor
        def _(pe):
            pe.sem_inc(multiplied, SLOTS)
            with pe.Fori(0, TILES // SLOTS, 1) as turn:
                i = turn * SLOTS
                for k in range(SLOTS):
                    pe.wait_ge(gathered[k], base + turn * 16 + 16)
                    pe.wait_ge(added, i + k + 1)
                    pe.wait_ge(onehot_ready, i + k + 1)
                    pe.matmul(bank(m, k % BANKS, 0, width), m.onehot[:, k, :], m.g[:, k, 0:width],
                              start=True, stop=True).then_inc(multiplied, 1)

        @block.vector
        def _(dve):
            if count:
                nc.vector.memset(m.g[:, :, D:D + 1], 1.0).then_inc(added, BANKS)
            else:
                dve.sem_inc(added, BANKS)

            def onehots(s, c):
                dve.wait_ge(staged, s + 1)
                for j in range(CHUNK):
                    k = c * CHUNK + j
                    dve.wait_ge(multiplied, s * CHUNK + j + 1)
                    rec = m.chunk[:, c, j, :]
                    if weighted:
                        ins = nc.vector.tensor_scalar(m.onehot[:, k, :], m.cols[:, :], rec[:, F_DST:F_DST + 1],
                                                      rec[:, F_WEIGHT:F_WEIGHT + 1], ALU.is_equal, ALU.mult)
                    else:
                        ins = nc.vector.tensor_scalar(m.onehot[:, k, :], m.cols[:, :], rec[:, F_DST:F_DST + 1], None,
                                                      ALU.is_equal)
                    ins.then_inc(onehot_ready, 1)

            def add(s, c):
                t = s * CHUNK
                wins = windows_of(dve, m, t)
                for j in range(CHUNK):
                    dve.wait_ge(multiplied, t + j + 1 + SLOTS)
                    dve.wait_ge(added, t + j + BANKS)
                    acc = window(m.acc, wins[j], 0, width)
                    nc.vector.tensor_tensor(acc, acc, bank(m, (c * CHUNK + j) % BANKS, 0, width), ALU.add).then_inc(added, 1)

            def step(s, c, live):
                if live(0):
                    onehots(s, c)
                if live(1):
                    add(s - 1, (c - 1) % CHUNKS)

            over_chunks(dve, step, 1)


def destination_rows(nc, m):
    with ExitStack() as ctx:
        turned, copied, stored = sems(ctx, nc, "rows", "turned", "copied", "stored")
        flat = ctx.enter_context(nc.sbuf_tensor("flat_rows", [P, 4, P], F32))
        block = ctx.enter_context(nc.Block())
        parts = [(b, min(P, TILES - b * P)) for b in range(-(-TILES // P))]

        @block.tensor
        def _(pe):
            for b, n in parts:
                mm = pe.transpose(m.ps[0:n, 0, b * P:(b + 1) * P], m.rec[:, b * P:b * P + n, F_DST], m.ident[:, :])
            mm.then_inc(turned, 1)

        @block.vector
        def _(dve):
            dve.wait_ge(turned, 1)
            for b, n in parts:
                ins = nc.vector.tensor_copy(flat[0:n, b, :], m.ps[0:n, 0, b * P:(b + 1) * P])
            ins.then_inc(copied, 1)

        @block.sync
        def _(sp):
            sp.wait_ge(copied, 1)
            for b, n in parts:
                sp.dma_start(m.dst_rows[b * P * P:(b * P + n) * P].rearrange("(t e) -> t e", e=P),
                             flat[0:n, b, :]).then_inc(stored, 16)
            sp.wait_ge(stored, 16 * len(parts))


def spread_rows(sp, m, used, loaded):
    with sp.Fori(0, TILES // (2 * CHUNK), 1) as pair:
        for b in (0, 1):
            sp.wait_ge(used, pair * 2 + b + 1)
            sp.dma_start(m.dst_bc[:, b, :],
                         m.dst_rows[bass.ds((pair * 2 + b) * (CHUNK * P), CHUNK * P)]
                         .rearrange("(o n) -> o n", o=1).to_broadcast([P, CHUNK * P])).then_inc(loaded[b], 16)


def attention_scores(nc, m):
    with ExitStack() as ctx:
        def sb(name, shape, dt=F32):
            return ctx.enter_context(nc.sbuf_tensor(name, shape, dt))

        R = 2 * CHUNK
        onehot_t = sb("onehot_t", [P, 2, CHUNK * P])
        off = sb("off", [P, R, P])
        masked = sb("masked", [P, CHUNK, HEADS, P])
        prod = sb("prod", [P, 2, CHUNK, D])
        sc = sb("sc", [P, 2, CHUNK * HEADS])
        tmax = sb("tmax", [P, CHUNK, HEADS])
        gathered, base = edge_buffers(ctx, nc, m, "score")
        (staged, spread_ready, q_spread, scored, saved, multiplied, masked_ready, masked_turned, reduced, maxed,
         zeroed) = sems(
            ctx, nc, "score", "staged", "spread_ready", "q_spread", "scored", "saved", "multiplied",
            "masked_ready", "masked_turned", "reduced", "maxed", "zeroed")
        loaded = sems(ctx, nc, "score", "loaded0", "loaded1")
        block = ctx.enter_context(nc.Block())

        @block.sync
        def _(sp):
            spread_rows(sp, m, spread_ready, loaded)

        @block.gpsimd
        def _(pool):
            gather_all(pool, m, m.table8k, staged, scored)

        @block.tensor
        def _(pe):
            def step(s, c, live):
                if live(0):
                    wins = windows_of(pe, m, s * CHUNK)
                    pe.wait_ge(spread_ready, s + 3)
                    for j in range(CHUNK):
                        pe.wait_ge(multiplied, s * CHUNK + j + 1)
                        pe.matmul(bank(m, j, 0, D), onehot_t[:, c % 2, j * P:(j + 1) * P], window(m.q, wins[j]),
                                  start=True, stop=True).then_inc(q_spread, 1)
                if live(1):
                    for j in range(CHUNK):
                        pe.wait_ge(masked_ready, (s - 1) * CHUNK + j + 1)
                        pe.wait_ge(reduced, (s - 1) * CHUNK + j + 1)
                        for h in range(HEADS):
                            mm = pe.transpose(bank(m, 4 + j, h * P, (h + 1) * P), masked[:, j, h, :], m.ident[:, :])
                        mm.then_inc(masked_turned, 1)

            over_chunks(pe, step, 1)

        @block.scalar
        def _(act):
            def step(s, c, live):
                if live(0):
                    stage_records(act, nc, m, s * CHUNK, c, F_ROW8, scored, staged)
                if live(2):
                    b, t = c % 2, (s - 2) * CHUNK
                    act.wait_ge(scored, t + CHUNK + SLOTS)
                    for j in range(CHUNK):
                        act.wait_ge(masked_turned, t + j + 1)
                        for h in range(HEADS):
                            ins = nc.scalar.activation(masked[:, j, h, :], off[:, b * CHUNK + j, :], ACT.Identity,
                                                       bias=sc[:, b, j * HEADS + h:j * HEADS + h + 1], scale=1.0)
                        ins.then_inc(masked_ready, 1)

            act.wait_ge(zeroed, 1)
            over_chunks(act, step, 2)

        @block.vector
        def _(dve):
            dve.sem_inc(scored, SLOTS)
            dve.sem_inc(spread_ready, 2)
            dve.sem_inc(multiplied, CHUNK)
            dve.sem_inc(masked_turned, CHUNK)
            dve.sem_inc(reduced, CHUNK)
            nc.vector.memset(m.mx[:, :, :], -BIG).then_inc(zeroed, 1)

            def masks(s, c):
                b = c % 2
                if not (isinstance(s, int) and s < 2):
                    dve.wait_ge(q_spread, (s - 1) * CHUNK)
                dve.wait_ge(loaded[b], (s - b) * 8 + 16)
                nc.vector.tensor_scalar(onehot_t[:, b, :], m.dst_bc[:, b, :], m.rowid[:, :], None,
                                        ALU.is_equal).then_inc(spread_ready, 1)
                dve.wait_ge(staged, s + 1)
                if not (isinstance(s, int) and s < 2):
                    dve.wait_ge(masked_ready, (s - 1) * CHUNK)
                for j in range(CHUNK):
                    nc.vector.tensor_scalar(off[:, b * CHUNK + j, :], m.cols[:, :], m.chunk[:, c, j, F_DST:F_DST + 1],
                                            -BIG, ALU.not_equal, ALU.mult)

            def scores(s, c):
                b, t = c % 2, s * CHUNK
                for j in range(CHUNK):
                    dve.wait_ge(gathered[c * CHUNK + j], base + (s - c) * (16 // CHUNKS) + 16)
                    dve.wait_ge(q_spread, t + j + 1)
                    nc.vector.tensor_tensor(prod[:, b, j, :], m.g[:, c * CHUNK + j, 0:D], bank(m, j, 0, D),
                                            ALU.mult).then_inc(multiplied, 1)
                dve.wait_ge(multiplied, t + 2 * CHUNK)
                nc.vector.tensor_reduce(sc[:, b, :], prod[:, b, :, :].rearrange("p j (h d) -> p (j h) d", h=HEADS),
                                        AX.X, ALU.add).then_inc(scored, CHUNK)
                dve.wait_ge(scored, t + CHUNK + SLOTS)
                nc.vector.tensor_copy(m.scores[:, bass.ds(t, CHUNK), :].rearrange("p t h -> p (t h)"), sc[:, b, :])

            def maxima(s, c):
                t = s * CHUNK
                wins = windows_of(dve, m, t)
                if not (isinstance(s, int) and s == 0):
                    dve.wait_ge(maxed, t)
                for j in range(CHUNK):
                    dve.wait_ge(masked_turned, t + j + 1 + CHUNK)
                    nc.vector.tensor_reduce(tmax[:, j, :], bank(m, 4 + j, 0, 512).rearrange("p (h e) -> p h e", h=HEADS),
                                            AX.X, ALU.max).then_inc(reduced, 1)
                for j in range(CHUNK):
                    dve.wait_ge(reduced, t + CHUNK + CHUNK)
                    if not (isinstance(s, int) and s == 0 and j == 0):
                        dve.wait_ge(maxed, t + j)
                    mx = window(m.mx, wins[j])
                    nc.vector.tensor_tensor(mx, mx, tmax[:, j, :], ALU.max).then_inc(maxed, 1)

            def step(s, c, live):
                if live(0):
                    masks(s, c)
                if live(1):
                    scores(s - 1, (c - 1) % CHUNKS)
                if live(2):
                    maxima(s - 2, (c - 2) % CHUNKS)

            over_chunks(dve, step, 2)


def attention_sum(nc, m):
    with ExitStack() as ctx:
        def sb(name, shape, dt=F32):
            return ctx.enter_context(nc.sbuf_tensor(name, shape, dt))

        R = 2 * CHUNK
        onehot_t = sb("onehot_t2", [P, 2, CHUNK * P])
        diff = sb("diff", [P, 2, CHUNK, HEADS])
        vx = sb("vx", [P, R, ACCW])
        gathered, base = edge_buffers(ctx, nc, m, "sum")
        (staged, spread_ready, onehot_ready, max_spread, diff_ready, exp_ready, by_act, by_dve, multiplied,
         added) = sems(
            ctx, nc, "sum", "staged", "spread_ready", "onehot_ready", "max_spread", "diff_ready", "exp_ready",
            "by_act", "by_dve", "multiplied", "added")
        loaded = sems(ctx, nc, "sum", "loaded0", "loaded1")
        block = ctx.enter_context(nc.Block())
        DVE_HEADS, ACT_HEADS = (0, 1), (2, 3)

        @block.sync
        def _(sp):
            spread_rows(sp, m, spread_ready, loaded)

        @block.gpsimd
        def _(pool):
            gather_all(pool, m, m.table8v, staged, multiplied)

        @block.tensor
        def _(pe):
            def step(s, c, live):
                if live(0):
                    wins = windows_of(pe, m, s * CHUNK)
                    pe.wait_ge(spread_ready, s + 3)
                    pe.wait_ge(diff_ready, s + 1)
                    for j in range(CHUNK):
                        mm = pe.matmul(bank(m, c % 2, j * HEADS, (j + 1) * HEADS), onehot_t[:, c % 2, j * P:(j + 1) * P],
                                       window(m.mx, wins[j]), start=True, stop=True)
                    mm.then_inc(max_spread, 1)
                if live(2):
                    t, cc = (s - 2) * CHUNK, (c - 2) % CHUNKS
                    for j in range(CHUNK):
                        pe.wait_ge(added, t + j + 1)
                        pe.wait_ge(by_dve, t + j + 1)
                        pe.wait_ge(by_act, t + j + 1)
                        pe.matmul(bank(m, 4 + j, 0, ACCW), m.onehot[:, cc * CHUNK + j, :], vx[:, (cc % 2) * CHUNK + j, :],
                                  start=True, stop=True).then_inc(multiplied, 1)

            over_chunks(pe, step, 2)

        @block.scalar
        def _(act):
            def step(s, c, live):
                if live(0):
                    stage_records(act, nc, m, s * CHUNK, c, F_ROW8, multiplied, staged)
                if live(2):
                    b = c % 2
                    act.wait_ge(multiplied, (s - 2) * CHUNK + CHUNK + SLOTS - R)
                    act.wait_ge(diff_ready, s + 1)
                    nc.scalar.activation(vx[:, b * CHUNK:(b + 1) * CHUNK, D:ACCW], diff[:, b, :, :], ACT.Exp).then_inc(exp_ready, 1)
                if live(3):
                    b, cc = (c - 3) % 2, (c - 3) % CHUNKS
                    act.wait_ge(exp_ready, s - 2)
                    for j in range(CHUNK):
                        act.wait_ge(gathered[cc * CHUNK + j], base + (s - 3 - cc) * (16 // CHUNKS) + 16)
                        for h in ACT_HEADS:
                            ins = nc.scalar.activation(vx[:, b * CHUNK + j, h * DK:(h + 1) * DK],
                                                       m.g[:, cc * CHUNK + j, h * DK:(h + 1) * DK], ACT.Copy,
                                                       scale=vx[:, b * CHUNK + j, D + h:D + h + 1])
                        ins.then_inc(by_act, 1)

            act.wait_ge(added, 1)
            over_chunks(act, step, 3)

        @block.vector
        def _(dve):
            dve.sem_inc(multiplied, SLOTS)
            dve.sem_inc(spread_ready, 2)
            dve.sem_inc(diff_ready, 2)
            dve.sem_inc(added, CHUNK)

            def onehots(s, c):
                b = c % 2
                if not (isinstance(s, int) and s < 2):
                    dve.wait_ge(max_spread, s - 1)
                dve.wait_ge(loaded[b], (s - b) * 8 + 16)
                nc.vector.tensor_scalar(onehot_t[:, b, :], m.dst_bc[:, b, :], m.rowid[:, :], None,
                                        ALU.is_equal).then_inc(spread_ready, 1)
                dve.wait_ge(staged, s + 1)
                for j in range(CHUNK):
                    dve.wait_ge(multiplied, s * CHUNK + j + 1)
                    nc.vector.tensor_scalar(m.onehot[:, c * CHUNK + j, :], m.cols[:, :], m.chunk[:, c, j, F_DST:F_DST + 1],
                                            None, ALU.is_equal).then_inc(onehot_ready, 1)

            def differences(s, c):
                b = c % 2
                if not (isinstance(s, int) and s < 2):
                    dve.wait_ge(exp_ready, s - 1)
                dve.wait_ge(max_spread, s + 1)
                nc.vector.tensor_tensor(diff[:, b, :, :].rearrange("p j h -> p (j h)"),
                                        m.scores[:, bass.ds(s * CHUNK, CHUNK), :].rearrange("p t h -> p (t h)"),
                                        bank(m, b, 0, CHUNK * HEADS), ALU.subtract).then_inc(diff_ready, 1)

            def weigh(s, c):
                b, t = c % 2, s * CHUNK
                dve.wait_ge(exp_ready, s + 1)
                for j in range(CHUNK):
                    dve.wait_ge(gathered[c * CHUNK + j], base + (s - c) * (16 // CHUNKS) + 16)
                    for h in DVE_HEADS:
                        ins = nc.vector.tensor_scalar(vx[:, b * CHUNK + j, h * DK:(h + 1) * DK],
                                                      m.g[:, c * CHUNK + j, h * DK:(h + 1) * DK],
                                                      vx[:, b * CHUNK + j, D + h:D + h + 1], None, ALU.mult)
                    ins.then_inc(by_dve, 1)

            def add(s, c):
                t = s * CHUNK
                wins = windows_of(dve, m, t)
                for j in range(CHUNK):
                    dve.wait_ge(multiplied, t + j + 1 + SLOTS)
                    dve.wait_ge(added, t + j + CHUNK)
                    acc = window(m.acc, wins[j])
                    nc.vector.tensor_tensor(acc, acc, bank(m, 4 + j, 0, ACCW), ALU.add).then_inc(added, 1)

            def step(s, c, live):
                if live(0):
                    onehots(s, c)
                if live(1):
                    differences(s - 1, (c - 1) % CHUNKS)
                if live(2):
                    weigh(s - 2, (c - 2) % CHUNKS)
                if live(3):
                    add(s - 3, (c - 3) % CHUNKS)

            over_chunks(dve, step, 3)


def layer_norm(nc, m, stage, prepare, out):
    with ExitStack() as ctx:
        chain, stats_ready, root_ready = sems(ctx, nc, stage, "norm_chain", "norm_stats", "norm_root")
        block = ctx.enter_context(nc.Block())

        @block.vector
        def _(dve):
            steps = [0]

            def step(ins):
                steps[0] += 1
                ins.then_inc(chain, 1)
                dve.wait_ge(chain, steps[0])

            prepare(step)
            for t in range(NT):
                step_or_none = nc.vector.bn_stats(m.stats[:, t, :], m.acc[:, t, 0:D])
            step(step_or_none)
            for t in range(NT):
                last = nc.vector.bn_aggr(m.mv[:, t, :], m.stats[:, t, :])
            last.then_inc(stats_ready, 1)
            dve.wait_ge(root_ready, 1)
            step(nc.vector.reciprocal(m.rstd[:, :], m.std[:, :]))
            for t in range(NT):
                nc.vector.tensor_scalar(out[:, t, 0:D], m.acc[:, t, 0:D], m.mv[:, t, 0:1], m.rstd[:, t:t + 1],
                                        ALU.subtract, ALU.mult)

        @block.scalar
        def _(act):
            act.wait_ge(stats_ready, 1)
            nc.scalar.activation(m.std[:, :], m.mv[:, :, 1], ACT.Sqrt, bias=m.eps[:, :], scale=1.0).then_inc(root_ready, 1)


def dense_pair(nc, m, stage, src, w_left, w_right, table, left_scale, left_keep, right_keep, right_bias):
    with ExitStack() as ctx:
        def sb(name, shape, dt=F32):
            return ctx.enter_context(nc.sbuf_tensor(f"{stage}_{name}", shape, dt))

        w = sb("w", [P, 2, 2 * D])
        xs = sb("xs", [P, 2, D])
        xt = sb("xt", [P, 2, 2, P])
        tb = sb("tb", [P, 2, D])
        weights_in, xs_ready, turned, xt_ready, product, tb_ready, kept = sems(
            ctx, nc, stage, "weights_in", "xs_ready", "turned", "xt_ready", "product", "tb_ready", "kept")
        stored = [sems(ctx, nc, stage, f"stored{b}")[0] for b in (0, 1)]
        block = ctx.enter_context(nc.Block())
        KEEPS = 1 + (left_keep is not None)

        def over_tiles(eng, tile):
            tile(0, 0, True)
            tile(1, 1, True)
            with eng.Fori(1, NT // 2, 1) as pair:
                t = pair * 2
                tile(t, 0, False)
                tile(t + 1, 1, False)
            tile(NT - 1, 0, False)

        @block.sync
        def _(sp):
            sp.dma_start(w[:, :, 0:D], w_left.rearrange("(k p) d -> p k d", p=P)).then_inc(weights_in, 16)
            sp.dma_start(w[:, :, D:2 * D], w_right.rearrange("(k p) d -> p k d", p=P)).then_inc(weights_in, 16)

            def tile(t, b, first):
                sp.wait_ge(tb_ready, t + 1)
                sp.dma_start(table[bass.ds(t * P, P), :], tb[:, b, :]).then_inc(stored[b], 16)

            over_tiles(sp, tile)
            sp.wait_ge(stored[0], 16 * (NT // 2 + 1))
            sp.wait_ge(stored[1], 16 * (NT // 2))

        @block.tensor
        def _(pe):
            def tile(t, b, first):
                if not first:
                    pe.wait_ge(xt_ready, t - 1)
                pe.wait_ge(xs_ready, t + 1)
                for k in (0, 1):
                    mm = pe.transpose(bank(m, b, k * P, (k + 1) * P), xs[:, b, k * P:(k + 1) * P], m.ident[:, :])
                mm.then_inc(turned, 1)
                if first:
                    pe.wait_ge(weights_in, 32)
                else:
                    pe.wait_ge(tb_ready, t - 1)
                    pe.wait_ge(kept, KEEPS * (t - 1))
                pe.wait_ge(xt_ready, t + 1)
                for side in (0, 1):
                    for k in (0, 1):
                        mm = pe.matmul(bank(m, 2 + 2 * side + b, 0, D), xt[:, b, k, :], w[:, k, side * D:(side + 1) * D],
                                       start=(k == 0), stop=(k == 1))
                mm.then_inc(product, 1)

            over_tiles(pe, tile)

        @block.scalar
        def _(act):
            def load(t, b, first):
                if not first:
                    act.wait_ge(turned, t - 1)
                    act.wait_ge(turned, 1)
                nc.scalar.activation(xs[:, b, :], window(src, t, 0, D), ACT.Copy).then_inc(xs_ready, 1)

            def tile(t, b, first):
                if not first:
                    act.wait_ge(stored[b], (t - b) * 8)
                    if left_keep is not None:
                        act.wait_ge(kept, 2 * (t - 1))
                act.wait_ge(product, t + 1)
                if left_scale is None:
                    nc.scalar.activation(tb[:, b, :], bank(m, 2 + b, 0, D), ACT.Copy).then_inc(tb_ready, 1)
                else:
                    act.wait_ge(product, 1)
                    nc.scalar.activation(tb[:, b, :], bank(m, 2 + b, 0, D), ACT.Copy,
                                         scale=left_scale[:, bass.ds(t, 1)]).then_inc(tb_ready, 1)

            load(0, 0, True)
            load(1, 1, True)
            tile(0, 0, True)
            load(2, 0, False)
            tile(1, 1, True)
            with act.Fori(1, NT // 2, 1) as pair:
                t = pair * 2
                load(t + 1, 1, False)
                tile(t, 0, False)
                load(t + 2, 0, False)
                tile(t + 1, 1, False)
            tile(NT - 1, 0, False)

        @block.vector
        def _(dve):
            def tile(t, b, first):
                if not first:
                    dve.wait_ge(product, t - 1)
                dve.wait_ge(turned, t + 1)
                nc.vector.tensor_copy(xt[:, b, :, :], bank(m, b, 0, D).rearrange("p (k n) -> p k n", k=2)).then_inc(xt_ready, 1)
                dve.wait_ge(product, t + 1)
                right = bank(m, 4 + b, 0, D)
                if right_bias is None:
                    nc.vector.tensor_copy(window(right_keep, t, 0, D), right).then_inc(kept, 1)
                else:
                    nc.vector.tensor_tensor(window(right_keep, t, 0, D), right_bias, right, ALU.add).then_inc(kept, 1)
                if left_keep is not None:
                    dve.wait_ge(tb_ready, t + 1)
                    nc.vector.tensor_copy(window(left_keep, t, 0, D), tb[:, b, :]).then_inc(kept, 1)

            over_tiles(dve, tile)


def attention_tables(nc, m, a):
    with ExitStack() as ctx:
        def sb(name, shape, dt=F32):
            return ctx.enter_context(nc.sbuf_tensor(name, shape, dt))

        w = sb("w_kvq", [P, 2, NTYPES, 3 * D])
        xs = sb("xs5", [P, D])
        xm = sb("xm5", [P, NTYPES, 2, P])
        kv = sb("kv5", [P, 2 * D])
        kvt = sb("kvt5", [P, 4, P])
        rel = sb("rel", [P, 2, 2, RELS8 * DK])
        att = sb("att", [DK, 2, RELS8, P])
        pri = sb("pri", [P, RELS8 * HEADS])
        tb = sb("tb5", [P, 2, RELS8, D])
        types_i = sb("types_i", [P, ROWS], I32)
        (weights_in, rel_in, types_zero, types_in, chain, rel_ready, xs_ready, turned, xm_ready, typed, kv_ready,
         kv_turned, kvt_ready, product, even, odd, q_kept, att_turned) = sems(
            ctx, nc, "att", "weights_in", "rel_in", "types_zero", "types_in", "chain", "rel_ready", "xs_ready", "turned",
            "xm_ready", "typed", "kv_ready", "kv_turned", "kvt_ready", "product", "even", "odd", "q_kept", "att_turned")
        stored = sems(ctx, nc, "att", "stored_k", "stored_v")
        block = ctx.enter_context(nc.Block())
        tables = [m.table8k.rearrange("(n r) d -> n (r d)", r=RELS8), m.table8v.rearrange("(n r) d -> n (r d)", r=RELS8)]

        @block.sync
        def _(sp):
            for j, src in enumerate((a.k_lin, a.v_lin, a.q_lin)):
                for ty in range(NTYPES):
                    sp.dma_start(w[:, :, ty, j * D:(j + 1) * D], src[ty].rearrange("(k p) d -> p k d", p=P)).then_inc(weights_in, 16)
            for h in range(HEADS):
                o = (h % 2) * DK
                sp.dma_start(att[:, h // 2, :, o:o + DK], a.rel_att[:, h, :, :].rearrange("r d e -> d r e")).then_inc(rel_in, 16)
                sp.dma_start(rel[o:o + DK, 1, h // 2, :].rearrange("p (r e) -> p r e", r=RELS8),
                             a.rel_msg[:, h, :, :].rearrange("r d e -> d r e")).then_inc(rel_in, 16)
            sp.dma_start(pri[:, :], a.pri.rearrange("(o r) h -> o (r h)", o=1).to_broadcast([P, RELS8 * HEADS])).then_inc(rel_in, 16)
            sp.wait_ge(types_zero, 1)
            sp.dma_start(types_i[:, 0:NODES], a.node_type.rearrange("(o n) -> o n", o=1).to_broadcast([P, NODES])).then_inc(types_in, 16)
            with sp.Fori(0, NT, 1) as t:
                for j in (0, 1):
                    sp.wait_ge(even, t * 4 + 2 * j + 2)
                    sp.wait_ge(odd, t * 4 + 2 * j + 2)
                    sp.dma_start(tables[j][bass.ds(t * P, P), :], tb[:, j, :, :].rearrange("p r d -> p (r d)")).then_inc(stored[j], 16)
            for j in (0, 1):
                sp.wait_ge(stored[j], 16 * NT)

        @block.tensor
        def _(pe):
            def tile(t, first):
                pe.wait_ge(xs_ready, t + 1)
                for k in (0, 1):
                    mm = pe.transpose(bank(m, 0, k * P, (k + 1) * P), xs[:, k * P:(k + 1) * P], m.ident[:, :])
                mm.then_inc(turned, 1)
                if first:
                    pe.wait_ge(weights_in, 16 * 3 * NTYPES)
                else:
                    pe.wait_ge(q_kept, t)
                pe.wait_ge(xm_ready, t + 1)
                n = 0
                for ty in range(NTYPES):
                    for k in (0, 1):
                        for b, lo, hi in ((1, 0, 2 * D), (2, 2 * D, 3 * D)):
                            mm = pe.matmul(bank(m, b, 0, hi - lo), xm[:, ty, k, :], w[:, k, ty, lo:hi],
                                           start=(n == 0), stop=(n == 2 * NTYPES - 1))
                        n += 1
                mm.then_inc(typed, 1)
                pe.wait_ge(kv_ready, t + 1)
                for c in range(4):
                    mm = pe.transpose(bank(m, 3, c * P, (c + 1) * P), kv[:, c * P:(c + 1) * P], m.ident[:, :])
                mm.then_inc(kv_turned, 1)
                if first:
                    pe.wait_ge(rel_ready, 1)
                pe.wait_ge(kvt_ready, t + 1)
                for g in range(8):
                    j, h = g // HEADS, g % HEADS
                    s, n = (odd, t * 4 + g // 2 - 1) if g % 2 else (even, t * 4 + g // 2 - 1)
                    if g >= 4 or not first:
                        pe.wait_ge(s, n)
                    o = (h % 2) * DK
                    pe.matmul(bank(m, 4 + g % 4, 0, 512), kvt[o:o + DK, 2 * j + h // 2, :], rel[o:o + DK, j, h // 2, :],
                              start=True, stop=True).then_inc(product, 1)

            pe.wait_ge(rel_in, 16 * 9)
            for hh in (0, 1):
                for r in range(RELS8):
                    mm = pe.transpose(bank(m, 4 + hh, r * DK, (r + 1) * DK), att[:, hh, r, :], m.ident[0:DK, 0:DK])
            mm.then_inc(att_turned, 1)
            tile(0, True)
            with pe.Fori(1, NT, 1) as t:
                tile(t, False)

        def to_table(eng, copy, t, first, half, done):
            for g in range(half, 8, 2):
                j, h = g // HEADS, g % HEADS
                if not first:
                    eng.wait_ge(stored[j], t * 16)
                eng.wait_ge(product, t * 8 + g + 1)
                copy(tb[:, j, :, h * DK:(h + 1) * DK], bank(m, 4 + g % 4, 0, 512).rearrange("p (r e) -> p r e", r=RELS8)).then_inc(done, 1)

        @block.scalar
        def _(act):
            copy = lambda o, i: nc.scalar.activation(o, i, ACT.Copy)
            copy(xs[:, :], m.x[:, 0, :]).then_inc(xs_ready, 1)

            def tile(t, first, last):
                act.wait_ge(typed, t + 1)
                copy(kv[:, :], bank(m, 1, 0, 512)).then_inc(kv_ready, 1)
                if not last:
                    act.wait_ge(turned, t + 1)
                    act.wait_ge(turned, 1)
                    copy(xs[:, :], window(m.x, t + 1)).then_inc(xs_ready, 1)
                act.wait_ge(kv_turned, t + 1)
                copy(kvt[:, :, :], bank(m, 3, 0, 512).rearrange("p (c n) -> p c n", c=4)).then_inc(kvt_ready, 1)
                to_table(act, copy, t, first, 1, odd)

            tile(0, True, False)
            with act.Fori(1, NT - 1, 1) as t:
                tile(t, False, False)
            tile(NT - 1, False, True)

        @block.vector
        def _(dve):
            steps = [0]

            def step(ins):
                steps[0] += 1
                ins.then_inc(chain, 1)
                dve.wait_ge(chain, steps[0])

            nc.vector.memset(types_i[:, :], 0).then_inc(types_zero, 1)
            dve.wait_ge(rel_in, 16 * 9)
            step(nc.vector.tensor_scalar(pri[:, :], pri[:, :], 1.0 / SQRT_DK, None, ALU.mult))
            dve.wait_ge(att_turned, 1)
            for h in range(HEADS):
                o = (h % 2) * DK
                view = lambda v: v.rearrange("p (r e) -> p r e", r=RELS8)
                by = pri[o:o + DK, :].rearrange("p (r h) -> p r h", h=HEADS)[:, :, h:h + 1].to_broadcast([DK, RELS8, DK])
                ins = nc.vector.tensor_tensor(view(rel[o:o + DK, 0, h // 2, :]), by,
                                              view(m.ps[o:o + DK, 4 + h // 2, 0:512]), ALU.mult)
            ins.then_inc(rel_ready, 1)
            dve.wait_ge(types_in, 16)

            def tile(t, first):
                if not first:
                    dve.wait_ge(typed, t)
                dve.wait_ge(turned, t + 1)
                for ty in range(NTYPES):
                    for k in (0, 1):
                        ins = nc.vector.scalar_tensor_tensor(
                            xm[:, ty, k, :], types_i[:, bass.ds(t * P, P)], float(ty),
                            bank(m, 0, k * P, (k + 1) * P), ALU.is_equal, ALU.mult)
                ins.then_inc(xm_ready, 1)
                dve.wait_ge(typed, t + 1)
                nc.vector.tensor_copy(window(m.q, t), bank(m, 2, 0, D)).then_inc(q_kept, 1)
                to_table(dve, nc.vector.tensor_copy, t, first, 0, even)

            tile(0, True)
            with dve.Fori(1, NT, 1) as t:
                tile(t, False)


def attention_output(nc, m, a):
    with ExitStack() as ctx:
        def sb(name, shape, dt=F32):
            return ctx.enter_context(nc.sbuf_tensor(name, shape, dt))

        w = sb("w_a", [P, 2, NTYPES * D])
        xs = sb("xs8", [P, 2, D])
        xt = sb("xt8", [P, 2, 2, P])
        rden = sb("rden", [P, NT, HEADS])
        types_i = sb("types_i8", [P, NT], I32)
        skip = sb("skip", [P, NTYPES])
        gate = sb("gate", [P, NTYPES])
        gates = sb("gates", [P, NTYPES, NT])
        tmp = sb("tmp8", [P, 4, D])
        weights_in, small_in, types_zero, chain, exp_ready, divided, xs_ready, turned, xt_ready, product, summed, own = sems(
            ctx, nc, "out", "weights_in", "small_in", "types_zero", "chain", "exp_ready", "divided", "xs_ready",
            "turned", "xt_ready", "product", "summed", "own")
        block = ctx.enter_context(nc.Block())

        @block.sync
        def _(sp):
            sp.dma_start(skip[:, :], a.skip.rearrange("(o n) -> o n", o=1).to_broadcast([P, NTYPES])).then_inc(small_in, 16)
            sp.wait_ge(types_zero, 1)
            with nc.allow_non_contiguous_dma(reason="a node per partition"):
                sp.dma_start(types_i[:, 0:NT - 1], a.node_type[0:(NT - 1) * P].rearrange("(t p) -> p t", p=P)).then_inc(small_in, 16)
                sp.dma_start(types_i[0:LAST, NT - 1:NT], a.node_type[(NT - 1) * P:NODES].rearrange("(p o) -> p o", o=1)).then_inc(small_in, 16)
            for ty in range(NTYPES):
                sp.dma_start(w[:, :, ty * D:(ty + 1) * D], a.a_lin[ty].rearrange("(k p) d -> p k d", p=P)).then_inc(weights_in, 16)

        @block.tensor
        def _(pe):
            pe.wait_ge(weights_in, 16 * NTYPES)

            def tile(t, first):
                pe.wait_ge(xs_ready, t + 1)
                for k in (0, 1):
                    mm = pe.transpose(bank(m, 0, k * P, (k + 1) * P), xs[:, 0, k * P:(k + 1) * P], m.ident[:, :])
                mm.then_inc(turned, 1)
                if not first:
                    pe.wait_ge(summed, t)
                pe.wait_ge(xt_ready, t + 1)
                for k in (0, 1):
                    for b in (0, 1):
                        mm = pe.matmul(bank(m, 1 + b, 0, 512), xt[:, 0, k, :], w[:, k, b * 512:(b + 1) * 512],
                                       start=(k == 0), stop=(k == 1))
                mm.then_inc(product, 1)

            tile(0, True)
            with pe.Fori(1, NT, 1) as t:
                tile(t, False)

        @block.scalar
        def _(act):
            act.wait_ge(small_in, 48)
            nc.scalar.activation(gate[:, :], skip[:, :], ACT.Exp, scale=-1.0).then_inc(exp_ready, 1)
            act.wait_ge(divided, 1)
            nc.scalar.activation(xs[:, 0, :], m.acc[:, 0, 0:D], ACT.Copy).then_inc(xs_ready, 1)
            with act.Fori(1, NT, 1) as t:
                act.wait_ge(turned, t)
                act.wait_ge(turned, 1)
                nc.scalar.activation(xs[:, 0, :], window(m.acc, t, 0, D), ACT.Copy).then_inc(xs_ready, 1)

        @block.vector
        def _(dve):
            steps = [0]

            def step(ins):
                steps[0] += 1
                ins.then_inc(chain, 1)
                dve.wait_ge(chain, steps[0])

            nc.vector.memset(types_i[:, :], 0).then_inc(types_zero, 1)
            step(nc.vector.tensor_scalar(rden[:, :, :], m.acc[:, :, D:ACCW], 1e-30, None, ALU.max))
            step(nc.vector.reciprocal(rden[:, :, :], rden[:, :, :]))
            for h in range(HEADS):
                v = m.acc[:, :, h * DK:(h + 1) * DK]
                ins = nc.vector.tensor_tensor(v, v, rden[:, :, h:h + 1].to_broadcast([P, NT, DK]), ALU.mult)
            ins.then_inc(divided, 1)
            dve.wait_ge(exp_ready, 1)
            step(nc.vector.tensor_scalar(gate[:, :], gate[:, :], 1.0, None, ALU.add))
            step(nc.vector.reciprocal(skip[:, :], gate[:, :]))
            for ty in range(NTYPES):
                ins = nc.vector.tensor_scalar(gates[:, ty, :], types_i[:, :], float(ty), skip[:, ty:ty + 1], ALU.is_equal, ALU.mult)
            step(ins)

            def tile(t, first):
                if not first:
                    dve.wait_ge(product, t)
                dve.wait_ge(turned, t + 1)
                nc.vector.tensor_copy(xt[:, 0, :, :], bank(m, 0, 0, D).rearrange("p (k n) -> p k n", k=2)).then_inc(xt_ready, 1)
                dve.wait_ge(product, t + 1)
                for ty in range(NTYPES):
                    prev = window(m.x, t) if ty == 0 else tmp[:, ty - 1, :]
                    out = window(m.acc, t, 0, D) if ty == NTYPES - 1 else tmp[:, ty, :]
                    if ty:
                        dve.wait_ge(own, t * 3 + ty)
                    ins = nc.vector.scalar_tensor_tensor(out, bank(m, 1 + ty // 2, (ty % 2) * D, (ty % 2 + 1) * D),
                                                         gates[:, ty, bass.ds(t, 1)], prev, ALU.mult, ALU.add)
                    ins.then_inc(own if ty < NTYPES - 1 else summed, 1)

            tile(0, True)
            with dve.Fori(1, NT, 1) as t:
                tile(t, False)


def vector_block(nc, m, stage, body):
    with ExitStack() as ctx:
        chain, = sems(ctx, nc, stage, "chain")
        block = ctx.enter_context(nc.Block())

        @block.vector
        def _(dve):
            steps = [0]

            def step(ins):
                steps[0] += 1
                ins.then_inc(chain, 1)
                dve.wait_ge(chain, steps[0])

            body(step)


def four_graph_layers(nc, a, out):
    with ExitStack() as ctx:
        def sb(name, shape, dt=F32):
            return ctx.enter_context(nc.sbuf_tensor(name, shape, dt))

        m = Named()
        m.iota_i = sb("iota_i", [P, P], I32)
        m.iota_p = sb("iota_p", [P, 1], I32)
        m.cols = sb("cols", [P, P])
        m.rowid = sb("rowid", [P, 1])
        m.ones = sb("ones", [P, P])
        m.eps = sb("eps", [P, 1])
        m.ident = sb("ident", [P, P])
        m.lower = sb("lower", [P, P])
        m.tile_ids = sb("tile_ids", [1, TILES])
        m.win = sb("win", [1, TILES], I32)
        m.x = sb("x", [P, NT, D])
        m.rec = sb("rec_all", [P, TILES, REC])
        m.ps = ctx.enter_context(nc.psum_tensor("ps", [P, 8, 512], F32))
        m.records = nc.dram_tensor("records", (P * TILES, REC), F32, kind="Internal").ap()
        m.table20 = nc.dram_tensor("table20", (ROWS * RELS20, D), F32, kind="Internal").ap()
        m.dst_rows = nc.dram_tensor("dst_rows", (TILES * P,), F32, kind="Internal").ap()
        m.table1 = nc.dram_tensor("table1", (ROWS, D), F32, kind="Internal").ap()
        m.table8k = nc.dram_tensor("table8k", (ROWS * RELS8, D), F32, kind="Internal").ap()
        m.table8v = nc.dram_tensor("table8v", (ROWS * RELS8, D), F32, kind="Internal").ap()

        m.tick, m.sp_tick = sems(ctx, nc, "own", "tick", "sp_tick")
        m.scattered = sems(ctx, nc, "all", "scattered0", "scattered1")
        constants(nc, m)
        with ExitStack() as c2:
            made, = sems(c2, nc, "ids", "made")
            m.spent.append(made)
            ids_i = c2.enter_context(nc.sbuf_tensor("ids_i", [1, TILES], I32))
            block = c2.enter_context(nc.Block())

            @block.gpsimd
            def _(pool):
                nc.gpsimd.iota(ids_i[:, :], [[1, TILES]], base=0, channel_multiplier=0).then_inc(made, 1)

            @block.vector
            def _(dve):
                dve.wait_ge(made, 1)
                nc.vector.tensor_copy(m.tile_ids[:, :], ids_i[:, :])

        sort_and_relation_table(nc, m, a)

        m.acc = sb("acc", [P, NT, ACCW])
        m.rows_i = sb("rows_i", [P, CHUNKS, CHUNK], I32)
        m.chunk = sb("chunk", [P, CHUNKS, CHUNK, REC])
        m.stats = sb("stats", [P, NT, 6])
        m.mv = sb("mv", [P, NT, 2])
        m.std = sb("std", [P, NT])
        m.rstd = sb("rstd", [P, NT])
        m.dis = sb("dis", [P, NT])
        m.q = sb("q", [P, NT, D])
        m.mx = sb("mx", [P, NT, HEADS])
        m.scores = sb("scores", [P, TILES, HEADS])
        m.bias = sb("bias", [P, 3, D])
        m.gathered = sems(ctx, nc, "all", *(f"gathered{k}" for k in range(SLOTS)))
        m.gathers_before = 0
        m.mx_written, m.bias_in = sems(ctx, nc, "all", "mx_written", "bias_in")
        feat = m.acc[:, :, 0:D]

        def relu_add(step):
            step(nc.vector.scalar_tensor_tensor(feat, feat, 0.0, m.x[:, :, :], ALU.max, ALU.add))

        destination_rows(nc, m)

        vector_block(nc, m, "zero", lambda step: step(nc.vector.memset(m.acc[:, :, :], 0.0)))
        aggregate_edges(nc, m, "rel", m.table20, F_ROW20, weighted=True)
        layer_norm(nc, m, "rel", relu_add, m.x)

        vector_block(nc, m, "count", lambda step: step(nc.vector.memset(m.acc[:, :, D:ACCW], 0.0)))
        dense_pair(nc, m, "conv", m.x, a.m1, a.w1, m.table1, None, None, m.acc, None)
        aggregate_edges(nc, m, "conv_edges", m.table1, F_SRC, count=True)

        def after_conv(step):
            relu_add(step)
            step(nc.vector.tensor_scalar(m.dis[:, :], m.acc[:, :, D], 1.0, None, ALU.add))
        layer_norm(nc, m, "conv", after_conv, m.x)

        with ExitStack() as c2:
            rooted, = sems(c2, nc, "dis", "rooted")
            block = c2.enter_context(nc.Block())

            @block.scalar
            def _(act):
                nc.scalar.activation(m.std[:, :], m.dis[:, :], ACT.Sqrt).then_inc(rooted, 1)

            @block.vector
            def _(dve):
                nc.vector.memset(m.acc[:, :, :], 0.0)
                dve.wait_ge(rooted, 1)
                nc.vector.reciprocal(m.dis[:, :], m.std[:, :])

            @block.sync
            def _(sp):
                for k, v in enumerate((a.b[0], a.b[1], a.resb)):
                    sp.dma_start(m.bias[:, k, :], v.rearrange("(o n) -> o n", o=1).to_broadcast([P, D])).then_inc(m.bias_in, 16)
                sp.wait_ge(m.bias_in, 48)

        attention_tables(nc, m, a)
        attention_scores(nc, m)
        attention_sum(nc, m)
        attention_output(nc, m, a)
        layer_norm(nc, m, "att", lambda step: None, m.x)

        def biases(step):
            for k in (0, 1):
                step(nc.vector.tensor_tensor(m.bias[:, k, :], m.bias[:, k, :], m.bias[:, 2, :], ALU.add))
        vector_block(nc, m, "bias", biases)
        h = m.acc2 = sb("h", [P, NT, D])

        def conv_out(step, into):
            for t in range(NT):
                ins = nc.vector.scalar_tensor_tensor(into[:, t, 0:D], m.acc[:, t, 0:D], m.dis[:, t:t + 1], m.q[:, t, :],
                                                     ALU.mult, ALU.add)
            step(ins)

        dense_pair(nc, m, "gcn0", m.x, a.w3[0], a.resw, m.table1, m.dis, m.acc, m.q, m.bias[:, 0, :])
        aggregate_edges(nc, m, "gcn0_edges", m.table1, F_SRC)

        def hidden(step):
            conv_out(step, h)
            step(nc.vector.tensor_scalar(h[:, :, :], h[:, :, :], 0.0, None, ALU.max))
        vector_block(nc, m, "gcn0_out", hidden)
        dense_pair(nc, m, "gcn1", h, a.w3[1], a.resw, m.table1, m.dis, m.acc, m.q, m.bias[:, 1, :])
        aggregate_edges(nc, m, "gcn1_edges", m.table1, F_SRC)

        def last(step):
            conv_out(step, m.acc)
            relu_add(step)
        layer_norm(nc, m, "gcn", last, h)

        with ExitStack() as c2:
            stored, = sems(c2, nc, "end", "stored")
            block = c2.enter_context(nc.Block())

            @block.sync
            def _(sp):
                sp.dma_start(out[0:(NT - 1) * P, :].rearrange("(t p) d -> p t d", p=P), h[:, 0:NT - 1, :]).then_inc(stored, 16)
                sp.dma_start(out[(NT - 1) * P:NODES, :], h[0:LAST, NT - 1, :]).then_inc(stored, 16)
                sp.wait_ge(stored, 32)


_INS = {
    "x": "x", "src": "src", "dst": "dst", "rel20": "edge_type_20", "rel8": "edge_type_8", "weight": "edge_weight1",
    "node_type": "node_type_4", "w20": "L0_gnn_weight", "w1": "L1_gnn_W", "m1": "L1_gnn_M",
    "k_lin": "L2_gnn_k_linears", "q_lin": "L2_gnn_q_linears", "v_lin": "L2_gnn_v_linears", "a_lin": "L2_gnn_a_linears",
    "rel_att": "L2_gnn_relation_att", "rel_msg": "L2_gnn_relation_msg", "pri": "L2_gnn_relation_pri",
    "skip": "L2_gnn_skip", "w3": "L3_gnn_W", "b": "L3_gnn_b", "resw": "L3_gnn_resW", "resb": "L3_gnn_resb",
}


def kernel(**inputs):
    import numpy as np
    import concourse.bacc as bacc
    from concourse.bass_utils import run_bass_kernel_spmd

    nc = bacc.Bacc("TRN2", target_bir_lowering=False, num_devices=1)
    arrays, a = {}, Named()
    for short, name in _INS.items():
        v = np.ascontiguousarray(inputs[name])
        arrays[f"in_{short}"] = v
        a.__dict__[short] = nc.dram_tensor(f"in_{short}", v.shape, mybir.dt.from_np(v.dtype), kind="ExternalInput").ap()
    out = nc.dram_tensor("out_x", (NODES, D), F32, kind="ExternalOutput").ap()
    four_graph_layers(nc, a, out)
    r = run_bass_kernel_spmd(nc, [arrays], core_ids=[0])
    return r.results[0]["out_x"]
```

```python
from contextlib import ExitStack

import concourse.bass as bass
from concourse import mybir

F32 = mybir.dt.float32
I32 = mybir.dt.int32
BF16 = mybir.dt.bfloat16
ALU = mybir.AluOpType
ACT = mybir.ActivationFunctionType
AX = mybir.AxisListType

P = 128
NODES = 3125
EDGES = 50000
D = 256
HEADS = 4
DK = D // HEADS
RELS20 = 20
RELS8 = 8
NTYPES = 4
SQRT_DK = 8.0
EPS = 1e-5

NT = -(-NODES // P)
LAST = NODES - (NT - 1) * P
ROWS = NT * P
EP = 125
EJ = EDGES // EP
SLOTS = 16
GROUP = 2
TILES = (EDGES + NT * (GROUP * P - 1)) // (GROUP * P) * GROUP
CHUNK = 4
CHUNKS = SLOTS // CHUNK
GROUPS = CHUNK // GROUP
assert TILES % (2 * CHUNK) == 0
ACCW = D + HEADS
REC = 8
F_ROW20, F_SRC, F_ROW8, F_DST, F_WEIGHT = range(5)
NO_DST = 255.0
BIG = 3.0e38


class Named:
    pass


def window(buf, t, lo=0, hi=None):
    hi = buf.shape[2] if hi is None else hi
    return buf[:, bass.ds(t, 1), lo:hi].rearrange("p a b -> p (a b)")


def sems(ctx, nc, stage, *names):
    return [ctx.enter_context(nc.semaphore(f"{stage}_{n}")) for n in names]


def bank(m, b, lo, hi):
    return m.ps[:, b, lo:hi]


def constants(nc, m):
    with ExitStack() as ctx:
        made, used = sems(ctx, nc, "const", "made", "used")
        m.spent = [made, used]
        block = ctx.enter_context(nc.Block())

        @block.gpsimd
        def _(pool):
            nc.gpsimd.iota(m.iota_i[:, :], [[1, P]], base=0, channel_multiplier=0).then_inc(made, 1)
            nc.gpsimd.iota(m.iota_p[:, :], [[1, 1]], base=0, channel_multiplier=1).then_inc(made, 1)

        @block.vector
        def _(dve):
            dve.wait_ge(made, 2)
            nc.vector.tensor_copy(m.cols[:, :], m.iota_i[:, :]).then_inc(used, 1)
            nc.vector.tensor_copy(m.rowid[:, :], m.iota_p[:, :]).then_inc(used, 1)
            nc.vector.memset(m.ones[:, :], 1.0).then_inc(used, 1)
            nc.vector.memset(m.eps[:, :], EPS).then_inc(used, 1)
            dve.wait_ge(used, 2)
            nc.vector.tensor_scalar(m.ident[:, :], m.cols[:, :], m.rowid[:, :], None, ALU.is_equal)
            nc.vector.tensor_scalar(m.lower[:, :], m.cols[:, :], m.rowid[:, :], None, ALU.is_gt)


def sort_and_relation_table(nc, m, a):
    with ExitStack() as ctx:
        def sb(name, shape, dt=F32):
            return ctx.enter_context(nc.sbuf_tensor(name, shape, dt))

        dst_i = sb("dst_i", [EP, EJ], I32)
        src_i = sb("src_i", [EP, EJ], I32)
        r20_i = sb("r20_i", [EP, EJ], I32)
        r8_i = sb("r8_i", [EP, EJ], I32)
        weight = sb("weight", [EP, EJ])
        fld = sb("fld", [EP, 4, EJ])
        onehot = sb("onehot", [EP, NT, EJ], BF16)
        count = sb("count", [EP, NT, EJ])
        small = sb("small", [P, 8, NT + 1])
        small_i = sb("small_i", [P, 2, NT + 1], I32)
        tiles_f = sb("tiles_f", [1, TILES])
        tiles_i = sb("tiles_i", [1, TILES], I32)
        cmp = sb("cmp", [1, TILES])
        rec = sb("rec", [EP, EJ, REC])
        pos = sb("pos", [EP, EJ])
        slots = sb("slots", [EP, 2, 8], I32)
        rows = sb("rows", [EP, 2, 8, REC])
        w20 = sb("w20", [P, 2, RELS20 * D])
        xs = sb("xs0", [P, 2, D])
        xt = sb("xt0", [P, 2, 2, P])
        half = RELS20 * D // 2
        tb = sb("tb0", [P, 2, half])

        (inputs, edges_in, x_in, x_zero, w_in, blank, chain, sums_ready, totals, staged,
         xs_ready, turned, xt_ready, product, emptied, records_in) = sems(
            ctx, nc, "sort", "inputs", "edges_in", "x_in", "x_zero", "w_in", "blank", "chain", "sums_ready",
            "totals", "staged", "xs_ready", "turned", "xt_ready", "product", "emptied", "records_in")
        scattered = m.scattered
        stored = sems(ctx, nc, "sort", "stored0", "stored1")
        m.spent += (inputs, edges_in, x_in, x_zero, w_in, blank, chain, sums_ready, totals, staged, xs_ready,
                      turned, xt_ready, product, emptied, records_in, *stored)
        block = ctx.enter_context(nc.Block())
        GROUPS20 = RELS20 * D // 512
        HG = GROUPS20 // 2
        BEFORE_TOTALS = 4
        table = m.table20.rearrange("(n r) d -> n (r d)", r=RELS20)
        SG = 8
        NG = EJ // SG

        @block.sync
        def _(sp):
            ev = lambda v: v.rearrange("(p j) -> p j", p=EP)
            sp.dma_start(dst_i[:, :], ev(a.dst)).then_inc(edges_in, 16)
            sp.wait_ge(x_zero, 1)
            sp.dma_start(m.x[:, 0:NT - 1, :], a.x[0:(NT - 1) * P, :].rearrange("(t p) d -> p t d", p=P)).then_inc(x_in, 16)
            sp.dma_start(m.x[0:LAST, NT - 1, :], a.x[(NT - 1) * P:NODES, :]).then_inc(x_in, 16)
            for r in range(RELS20):
                sp.dma_start(w20[:, :, r * D:(r + 1) * D], a.w20[r].rearrange("(k p) d -> p k d", p=P)).then_inc(w_in, 16)
            sp.dma_start(src_i[:, :], ev(a.src)).then_inc(inputs, 16)
            sp.dma_start(r20_i[:, :], ev(a.rel20)).then_inc(inputs, 16)
            sp.dma_start(r8_i[:, :], ev(a.rel8)).then_inc(inputs, 16)
            sp.dma_start(weight[:, :], a.weight.rearrange("(p j) o -> p (j o)", p=EP)).then_inc(inputs, 16)
            sp.wait_ge(blank, 2)
            sp.dma_start(m.records.rearrange("(p t) f -> p t f", p=P), m.rec[:, :, :]).then_inc(records_in, 16)

            def store(t, h):
                sp.dma_start(table[bass.ds(t * P, P), h * half:(h + 1) * half], tb[:, h, :]).then_inc(stored[h], 16)

            with sp.Fori(0, NT, 1) as t:
                for h in (0, 1):
                    sp.wait_ge(emptied, t * GROUPS20 + (h + 1) * HG)
                    sp.sem_inc(m.sp_tick, 1)
                    store(t, h)
            for h in (0, 1):
                sp.wait_ge(stored[h], 16 * NT)
                sp.wait_ge(scattered[h], 16 * (SG * NG // 2))

        @block.gpsimd
        def _(pool):
            pool.wait_ge(records_in, 16)
            with pool.Fori(0, NG, 2) as g:
                for b in (0, 1):
                    pool.wait_ge(staged, 2 * g + (2 * b + 2))
                    pool.sem_inc(m.tick, 1)
                    for j in range(SG):
                        pool.indirect_dma_start(
                            out=m.records, out_offset=bass.IndirectOffsetOnAxis(ap=slots[:, b, j:j + 1], axis=0),
                            in_=rows[:, b, j, :], in_offset=None).then_inc(scattered[b], 16)

        @block.scalar
        def _(act):
            def load(t):
                nc.scalar.activation(xs[:, 0, :], window(m.x, t), ACT.Copy).then_inc(xs_ready, 1)

            def node_tile(t, first, last):
                act.wait_ge(turned, t + 1)
                if not first:
                    act.wait_ge(product, t * GROUPS20)
                nc.scalar.activation(xt[:, 0, :, :], bank(m, 6, 0, D).rearrange("p (k n) -> p k n", k=2),
                                     ACT.Copy).then_inc(xt_ready, 1)
                if not last:
                    load(t + 1)
                for g in range(GROUPS20):
                    if not first and g % HG == 0:
                        act.wait_ge(stored[g // HG], t * 16)
                    act.wait_ge(product, t * GROUPS20 + g + 1)
                    nc.scalar.activation(tb[:, g // HG, (g % HG) * 512:(g % HG + 1) * 512], bank(m, g % 6, 0, 512),
                                         ACT.Copy).then_inc(emptied, 1)

            act.wait_ge(x_in, 32)
            load(0)
            node_tile(0, True, False)
            with act.Fori(1, NT - 1, 1) as t:
                node_tile(t, False, False)
            node_tile(NT - 1, False, True)

        @block.tensor
        def _(pe):
            def node_tile(t, first):
                pe.wait_ge(xs_ready, t + 1)
                for k in (0, 1):
                    mm = pe.transpose(bank(m, 6, k * P, (k + 1) * P), xs[:, 0, k * P:(k + 1) * P], m.ident[:, :])
                mm.then_inc(turned, 1)
                pe.wait_ge(xt_ready, t + 1)
                for g in range(GROUPS20):
                    if g >= 6:
                        pe.wait_ge(emptied, t * GROUPS20 + g - 5)
                    elif not first and g == 0:
                        pe.wait_ge(emptied, t * GROUPS20)
                    for k in (0, 1):
                        mm = pe.matmul(bank(m, g % 6, 0, 512), xt[:, 0, k, :], w20[:, k, g * 512:(g + 1) * 512],
                                       start=(k == 0), stop=(k == 1))
                    mm.then_inc(product, 1)

            pe.wait_ge(w_in, 16 * RELS20)
            node_tile(0, True)
            with pe.Fori(1, BEFORE_TOTALS, 1) as t:
                node_tile(t, False)
            pe.wait_ge(sums_ready, 1)
            pe.matmul(bank(m, 7, 0, NT), m.lower[0:EP, 0:P], small[0:EP, 0, 0:NT], start=True, stop=True)
            pe.matmul(bank(m, 7, 64, 64 + NT), m.ones[0:EP, :], small[0:EP, 0, 0:NT], start=True, stop=True).then_inc(totals, 1)
            with pe.Fori(BEFORE_TOTALS, NT, 1) as t:
                node_tile(t, False)

        @block.vector
        def _(dve):
            steps = [0]

            def step(ins):
                steps[0] += 1
                ins.then_inc(chain, 1)
                dve.wait_ge(chain, steps[0])

            nc.vector.memset(m.x[:, NT - 1, :], 0.0).then_inc(x_zero, 1)
            nc.vector.memset(m.rec[:, :, :], 0.0).then_inc(blank, 1)
            dve.wait_ge(blank, 1)
            nc.vector.memset(m.rec[:, :, F_DST], NO_DST).then_inc(blank, 1)

            dve.wait_ge(edges_in, 16)
            step(nc.vector.tensor_single_scalar(r8_win := fld_i(fld, 0), dst_i[:, :], 7, op=ALU.logical_shift_right))
            step(nc.vector.tensor_copy(fld[:, 1, :], r8_win))
            step(nc.vector.tensor_tensor(onehot[:, :, :], fld[:, 1:2, :].to_broadcast([EP, NT, EJ]),
                                         m.cols[0:EP, 0:NT].rearrange("p (b o) -> p b o", o=1).to_broadcast([EP, NT, EJ]),
                                         ALU.is_equal))
            oh_flat = onehot[:, :, :].rearrange("p b j -> p (b j)")
            step(nc.vector.tensor_tensor_scan(count[:, :, :].rearrange("p b j -> p (b j)"), oh_flat, oh_flat, 0.0,
                                              ALU.add, ALU.max))
            ends = count[:, :, EJ - 1]
            sm = lambda k, w=NT: small[0:EP, k, 0:w]
            step(nc.vector.memset(small[:, 1, :], 0.0))
            step(nc.vector.tensor_copy(small[0:EP, 1, 1:NT + 1], ends))
            step(nc.vector.tensor_tensor(small[0:EP, 0, 0:NT], small[0:EP, 1, 1:NT + 1], small[0:EP, 1, 0:NT], ALU.subtract))
            nc.vector.tensor_copy(small[0:EP, 7, 0:NT], small[0:EP, 0, 0:NT]).then_inc(sums_ready, 1)
            dve.wait_ge(inputs, 64)
            step(nc.vector.memset(rec[:, :, :], 0.0))
            step(nc.vector.tensor_copy(fld[:, 2, :], dst_i[:, :]))
            step(nc.vector.scalar_tensor_tensor(rec[:, :, F_DST], fld[:, 1, :], -float(P), fld[:, 2, :], ALU.mult, ALU.add))
            step(nc.vector.tensor_copy(fld[:, 0, :], src_i[:, :]))
            step(nc.vector.tensor_copy(rec[:, :, F_SRC], fld[:, 0, :]))
            step(nc.vector.scalar_tensor_tensor(rec[:, :, F_ROW20], fld[:, 0, :], float(RELS20), r20_i[:, :], ALU.mult, ALU.add))
            step(nc.vector.scalar_tensor_tensor(rec[:, :, F_ROW8], fld[:, 0, :], float(RELS8), r8_i[:, :], ALU.mult, ALU.add))
            step(nc.vector.tensor_copy(rec[:, :, F_WEIGHT], weight[:, :]))
            dve.wait_ge(totals, 1)
            step(nc.vector.tensor_scalar(small_i[:, 0, 0:NT], bank(m, 7, 64, 64 + NT), float(GROUP * P - 1), None, ALU.add))
            step(nc.vector.tensor_single_scalar(small_i[:, 1, 0:NT], small_i[:, 0, 0:NT], 8, op=ALU.logical_shift_right))
            step(nc.vector.tensor_scalar(small[:, 2, 0:NT], small_i[:, 1, 0:NT], float(GROUP), None, ALU.mult))
            step(nc.vector.memset(small[:, 3, :], 0.0))
            step(nc.vector.tensor_tensor_scan(small[:, 3, 1:NT + 1], small[:, 2, 0:NT], small[:, 2, 0:NT], 0.0, ALU.add, ALU.max))
            step(nc.vector.scalar_tensor_tensor(sm(4), sm(3), float(P), bank(m, 7, 0, NT)[0:EP, :], ALU.mult, ALU.add))
            step(nc.vector.tensor_tensor(sm(5), sm(4), sm(1), ALU.subtract))
            step(nc.vector.tensor_scalar(sm(6), sm(5), -1.0, None, ALU.add))
            step(nc.vector.tensor_tensor(count[:, :, :], count[:, :, :],
                                         small[0:EP, 6, 0:NT].rearrange("p (b o) -> p b o", o=1).to_broadcast([EP, NT, EJ]), ALU.add))
            step(nc.vector.tensor_tensor(count[:, :, :], count[:, :, :], onehot[:, :, :], ALU.mult))
            step(nc.vector.tensor_reduce(pos[:, :], count[:, :, :].rearrange("p b j -> p j b"), AX.X, ALU.add))
            step(nc.vector.tensor_copy(fld_i(fld, 0), pos[:, :]))
            step(nc.vector.tensor_single_scalar(fld_i(fld, 2), fld_i(fld, 0), 7, op=ALU.logical_shift_right))
            step(nc.vector.tensor_single_scalar(fld_i(fld, 3), fld_i(fld, 0), P - 1, op=ALU.bitwise_and))
            step(nc.vector.tensor_copy(fld[:, 0, :], fld_i(fld, 3)))
            step(nc.vector.tensor_copy(pos[:, :], fld_i(fld, 2)))
            step(nc.vector.scalar_tensor_tensor(pos[:, :], fld[:, 0, :], float(TILES), pos[:, :], ALU.mult, ALU.add))
            done = steps[0]

            def stage(g, b, first):
                if not first:
                    dve.wait_ge(scattered[b], (g - b) * (SG * 8))
                    dve.wait_ge(chain, done)
                nc.vector.tensor_copy(slots[:, b, :], pos[:, bass.ds(g * SG, SG)]).then_inc(staged, 1)
                nc.vector.tensor_copy(rows[:, b, :, :], rec[:, bass.ds(g * SG, SG), :]).then_inc(staged, 1)

            stage(0, 0, True)
            stage(1, 1, True)
            with dve.Fori(1, NG // 2, 1) as pair:
                for b in (0, 1):
                    stage(pair * 2 + b, b, False)

            step(nc.vector.memset(tiles_f[:, :], -1.0))
            for b in range(NT):
                step(nc.vector.tensor_scalar(cmp[:, :], m.tile_ids[0:1, :], small[0:1, 3, b:b + 1], None, ALU.is_ge))
                step(nc.vector.tensor_tensor(tiles_f[:, :], tiles_f[:, :], cmp[:, :], ALU.add))
            step(nc.vector.tensor_copy(m.win[0:1, :], tiles_f[:, :]))

    with ExitStack() as ctx:
        back, = sems(ctx, nc, "sorted", "records_back")
        block = ctx.enter_context(nc.Block())

        @block.sync
        def _(sp):
            for s in m.spent:
                sp.sem_clear(s)
            sp.dma_start(m.rec[:, :, :], m.records.rearrange("(p t) f -> p t f", p=P)).then_inc(back, 16)
            sp.wait_ge(back, 16)


def fld_i(fld, k):
    return fld[:, k, :].bitcast(I32)


def edge_buffers(ctx, nc, m, stage):
    m.g = ctx.enter_context(nc.sbuf_tensor(f"{stage}_g", [P, SLOTS, ACCW], F32))
    m.onehot = ctx.enter_context(nc.sbuf_tensor(f"{stage}_onehot", [P, SLOTS, P], F32))
    m.dst_bc = ctx.enter_context(nc.sbuf_tensor(f"{stage}_dst_bc", [P, 2, CHUNK * P], F32))
    m.gather_stages += 1


def slot_gathered(eng, m, s, c, j):
    k = c * CHUNK + j
    before = 16 * -(-(TILES - k) // SLOTS) * (m.gather_stages - 1)
    eng.wait_ge(m.gathered[k], (s - c) * (16 // CHUNKS) + (before + 16))


def stage_records(act, nc, m, t, c, field, used, ready):
    act.wait_ge(used, t + CHUNK)
    act.wait_ge(used, 1)
    nc.scalar.activation(m.rows_i[:, c, :], m.rec[:, bass.ds(t, CHUNK), field], ACT.Copy)
    nc.scalar.activation(m.chunk[:, c, :, :], m.rec[:, bass.ds(t, CHUNK), :], ACT.Copy).then_inc(ready, 1)


def gather_all(pool, m, table, staged):
    def step(s, c, live):
        if live(0):
            pool.wait_ge(staged, s + 1)
            pool.sem_inc(m.tick, 1)
            for j in range(CHUNK):
                pool.indirect_dma_start(
                    out=m.g[:, c * CHUNK + j, 0:D], out_offset=None, in_=table,
                    in_offset=bass.IndirectOffsetOnAxis(ap=m.rows_i[:, c, j:j + 1], axis=0)
                ).then_inc(m.gathered[c * CHUNK + j], 16)

    over_chunks(pool, step, 0)


def windows_of(eng, m, t):
    return [eng.value_load(m.win[0:1, bass.ds(t + g * GROUP, 1)], min_val=0, max_val=NT - 1) for g in range(GROUPS)]


def over_chunks(eng, step, lag):
    total = TILES // CHUNK
    turns = total // CHUNKS
    exists = lambda s: lambda d: 0 <= s - d < total
    assert lag <= CHUNKS
    for s in range(CHUNKS):
        step(s, s, exists(s))
    with eng.Fori(1, turns, 1) as turn:
        for c in range(CHUNKS):
            step(turn * CHUNKS + c, c, lambda d: True)
    for s in range(turns * CHUNKS, total + lag):
        step(s, s % CHUNKS, exists(s))


def aggregate_edges(nc, m, stage, table, field, weighted=False, count=False):
    width = D + 1 if count else D
    BANKS = 8
    with ExitStack() as ctx:
        edge_buffers(ctx, nc, m, stage)
        multiplied, onehot_ready, added, staged = sems(
            ctx, nc, stage, "multiplied", "onehot_ready", "added", "staged")
        block = ctx.enter_context(nc.Block())

        @block.gpsimd
        def _(pool):
            gather_all(pool, m, table, staged)

        @block.scalar
        def _(act):
            over_chunks(act, lambda s, c, live: live(0) and stage_records(
                act, nc, m, s * CHUNK, c, field, multiplied, staged), 0)

        @block.tensor
        def _(pe):
            pe.sem_inc(multiplied, SLOTS)

            def step(s, c, live):
                if live(0):
                    pe.wait_ge(onehot_ready, s + 1)
                    for j in range(CHUNK):
                        k = c * CHUNK + j
                        if j % GROUP == 0:
                            pe.wait_ge(added, s * GROUPS + j // GROUP + 1)
                        slot_gathered(pe, m, s, c, j)
                        pe.matmul(bank(m, k // GROUP % BANKS, 0, width), m.onehot[:, k, :], m.g[:, k, 0:width],
                                  start=(j % GROUP == 0), stop=(j % GROUP == GROUP - 1)).then_inc(multiplied, 1)

            over_chunks(pe, step, 0)

        @block.vector
        def _(dve):
            if count:
                nc.vector.memset(m.g[:, :, D:D + 1], 1.0).then_inc(added, BANKS)
            else:
                dve.sem_inc(added, BANKS)

            def onehots(s, c):
                dve.wait_ge(staged, s + 1)
                for j in range(CHUNK):
                    rec = m.chunk[:, c, j, :]
                    out = m.onehot[:, c * CHUNK + j, :]
                    if weighted:
                        ins = nc.vector.tensor_scalar(out, m.cols[:, :], rec[:, F_DST:F_DST + 1],
                                                      rec[:, F_WEIGHT:F_WEIGHT + 1], ALU.is_equal, ALU.mult)
                    else:
                        ins = nc.vector.tensor_scalar(out, m.cols[:, :], rec[:, F_DST:F_DST + 1], None, ALU.is_equal)
                ins.then_inc(onehot_ready, 1)

            def add(s, c):
                wins = windows_of(dve, m, s * CHUNK)
                for g in range(GROUPS):
                    dve.wait_ge(multiplied, s * CHUNK + (g + 1) * GROUP + SLOTS)
                    dve.wait_ge(added, s * GROUPS + g + BANKS)
                    acc = window(m.acc, wins[g], 0, width)
                    nc.vector.tensor_tensor(acc, acc, bank(m, (c * GROUPS + g) % BANKS, 0, width), ALU.add).then_inc(added, 1)

            def step(s, c, live):
                if live(0):
                    onehots(s, c)
                if live(1):
                    add(s - 1, (c - 1) % CHUNKS)

            over_chunks(dve, step, 1)


def destination_rows(nc, m):
    with ExitStack() as ctx:
        turned, copied, stored = sems(ctx, nc, "rows", "turned", "copied", "stored")
        flat = ctx.enter_context(nc.sbuf_tensor("flat_rows", [P, 4, P], F32))
        block = ctx.enter_context(nc.Block())
        parts = [(b, min(P, TILES - b * P)) for b in range(-(-TILES // P))]

        @block.tensor
        def _(pe):
            for b, n in parts:
                mm = pe.transpose(m.ps[0:n, 0, b * P:(b + 1) * P], m.rec[:, b * P:b * P + n, F_DST], m.ident[:, :])
            mm.then_inc(turned, 1)

        @block.vector
        def _(dve):
            dve.wait_ge(turned, 1)
            for b, n in parts:
                ins = nc.vector.tensor_copy(flat[0:n, b, :], m.ps[0:n, 0, b * P:(b + 1) * P])
            ins.then_inc(copied, 1)

        @block.sync
        def _(sp):
            sp.wait_ge(copied, 1)
            for b, n in parts:
                sp.dma_start(m.dst_rows[b * P * P:(b * P + n) * P].rearrange("(t e) -> t e", e=P),
                             flat[0:n, b, :]).then_inc(stored, 16)
            sp.wait_ge(stored, 16 * len(parts))


def spread_rows(sp, m, used, loaded):
    with sp.Fori(0, TILES // (2 * CHUNK), 1) as pair:
        for b in (0, 1):
            sp.wait_ge(used, pair * 2 + b + 1)
            sp.dma_start(m.dst_bc[:, b, :],
                         m.dst_rows[bass.ds((pair * 2 + b) * (CHUNK * P), CHUNK * P)]
                         .rearrange("(o n) -> o n", o=1).to_broadcast([P, CHUNK * P])).then_inc(loaded[b], 16)


def attention_scores(nc, m):
    with ExitStack() as ctx:
        def sb(name, shape, dt=F32):
            return ctx.enter_context(nc.sbuf_tensor(name, shape, dt))

        onehot_t = sb("onehot_t", [P, 2, CHUNK * P])
        off = sb("off", [P, SLOTS, P])
        masked = sb("masked", [P, CHUNK, HEADS, P])
        prod = sb("prod", [P, 2, CHUNK, D])
        sc = sb("sc", [P, 2, CHUNK * HEADS])
        tmax = sb("tmax", [P, CHUNK, HEADS])
        edge_buffers(ctx, nc, m, "score")
        (staged, spread_ready, q_spread, scored, saved, multiplied, masked_ready, masked_turned, reduced, maxed,
         zeroed) = sems(
            ctx, nc, "score", "staged", "spread_ready", "q_spread", "scored", "saved", "multiplied",
            "masked_ready", "masked_turned", "reduced", "maxed", "zeroed")
        loaded = sems(ctx, nc, "score", "loaded0", "loaded1")
        block = ctx.enter_context(nc.Block())

        @block.sync
        def _(sp):
            spread_rows(sp, m, spread_ready, loaded)

        @block.gpsimd
        def _(pool):
            gather_all(pool, m, m.table8k, staged)

        @block.tensor
        def _(pe):
            def step(s, c, live):
                if live(0):
                    wins = windows_of(pe, m, s * CHUNK)
                    pe.wait_ge(spread_ready, s + 3)
                    for j in range(CHUNK):
                        if j % GROUP == 0:
                            pe.wait_ge(multiplied, s * CHUNK + j + GROUP)
                        pe.matmul(bank(m, j, 0, D), onehot_t[:, c % 2, j * P:(j + 1) * P], window(m.q, wins[j // GROUP]),
                                  start=True, stop=True).then_inc(q_spread, 1)
                if live(1):
                    for g in range(GROUPS):
                        pe.wait_ge(masked_ready, (s - 1) * GROUPS + g + 1)
                        pe.wait_ge(reduced, (s - 1) * GROUPS + g + 1)
                        for j in range(g * GROUP, (g + 1) * GROUP):
                            for h in range(HEADS):
                                mm = pe.transpose(bank(m, 4 + j, h * P, (h + 1) * P), masked[:, j, h, :], m.ident[:, :])
                        mm.then_inc(masked_turned, 1)

            over_chunks(pe, step, 1)

        @block.scalar
        def _(act):
            def step(s, c, live):
                if live(0):
                    stage_records(act, nc, m, s * CHUNK, c, F_ROW8, scored, staged)
                if live(2):
                    b, t = c % 2, (s - 2) * CHUNK
                    act.wait_ge(scored, t + CHUNK + SLOTS)
                    for j in range(CHUNK):
                        if j % GROUP == 0:
                            act.wait_ge(masked_turned, (s - 2) * GROUPS + j // GROUP + 1)
                        for h in range(HEADS):
                            ins = nc.scalar.activation(masked[:, j, h, :], off[:, (c - 2) % CHUNKS * CHUNK + j, :], ACT.Identity,
                                                       bias=sc[:, b, j * HEADS + h:j * HEADS + h + 1], scale=1.0)
                        if j % GROUP == GROUP - 1:
                            ins.then_inc(masked_ready, 1)

            act.wait_ge(zeroed, 1)
            over_chunks(act, step, 2)

        @block.vector
        def _(dve):
            dve.sem_inc(scored, SLOTS)
            dve.sem_inc(spread_ready, 2)
            dve.sem_inc(multiplied, CHUNK)
            dve.sem_inc(masked_turned, GROUPS)
            dve.sem_inc(reduced, GROUPS)
            nc.vector.memset(m.mx[:, :, :], -BIG).then_inc(zeroed, 1)

            def masks(s, c):
                b = c % 2
                dve.wait_ge(loaded[b], (s - b) * 8 + 16)
                nc.vector.tensor_scalar(onehot_t[:, b, :], m.dst_bc[:, b, :], m.rowid[:, :], None,
                                        ALU.is_equal).then_inc(spread_ready, 1)
                dve.wait_ge(staged, s + 1)
                for j in range(CHUNK):
                    nc.vector.tensor_scalar(off[:, c * CHUNK + j, :], m.cols[:, :], m.chunk[:, c, j, F_DST:F_DST + 1],
                                            -BIG, ALU.not_equal, ALU.mult)

            def scores(s, c):
                b, t = c % 2, s * CHUNK
                for j in range(CHUNK):
                    slot_gathered(dve, m, s, c, j)
                    dve.wait_ge(q_spread, t + j + 1)
                    nc.vector.tensor_tensor(prod[:, b, j, :], m.g[:, c * CHUNK + j, 0:D], bank(m, j, 0, D),
                                            ALU.mult).then_inc(multiplied, 1)
                dve.wait_ge(multiplied, t + 2 * CHUNK)
                nc.vector.tensor_reduce(sc[:, b, :], prod[:, b, :, :].rearrange("p j (h d) -> p (j h) d", h=HEADS),
                                        AX.X, ALU.add).then_inc(scored, CHUNK)

            def keep(s, c):
                b, t = c % 2, s * CHUNK
                dve.wait_ge(scored, t + CHUNK + SLOTS)
                nc.vector.tensor_copy(m.scores[:, bass.ds(t, CHUNK), :].rearrange("p t h -> p (t h)"), sc[:, b, :])

            def maxima(s, c):
                if not (isinstance(s, int) and s == 0):
                    dve.wait_ge(maxed, s * GROUPS)
                for g in range(GROUPS):
                    dve.wait_ge(masked_turned, (s + 1) * GROUPS + g + 1)
                    both = m.ps[:, 4 + g * GROUP:4 + (g + 1) * GROUP, :].rearrange("p j (h e) -> p h j e", h=HEADS)
                    nc.vector.tensor_reduce(tmax[:, g, :], both, AX.XY, ALU.max).then_inc(reduced, 1)
                wins = windows_of(dve, m, s * CHUNK)
                for g in range(GROUPS):
                    dve.wait_ge(reduced, (s + 1) * GROUPS + g + 1)
                    if g:
                        dve.wait_ge(maxed, s * GROUPS + g)
                    mx = window(m.mx, wins[g])
                    nc.vector.tensor_tensor(mx, mx, tmax[:, g, :], ALU.max).then_inc(maxed, 1)

            def step(s, c, live):
                if live(0):
                    masks(s, c)
                if live(1):
                    scores(s - 1, (c - 1) % CHUNKS)
                if live(2):
                    maxima(s - 2, (c - 2) % CHUNKS)
                if live(1):
                    keep(s - 1, (c - 1) % CHUNKS)

            over_chunks(dve, step, 2)


def attention_sum(nc, m):
    with ExitStack() as ctx:
        def sb(name, shape, dt=F32):
            return ctx.enter_context(nc.sbuf_tensor(name, shape, dt))

        R = 2 * CHUNK
        onehot_t = sb("onehot_t2", [P, 2, CHUNK * P])
        diff = sb("diff", [P, 2, CHUNK, HEADS])
        vx = sb("vx", [P, R, ACCW])
        edge_buffers(ctx, nc, m, "sum")
        (staged, spread_ready, onehot_ready, max_spread, diff_ready, exp_ready, by_act, by_dve, multiplied,
         added) = sems(
            ctx, nc, "sum", "staged", "spread_ready", "onehot_ready", "max_spread", "diff_ready", "exp_ready",
            "by_act", "by_dve", "multiplied", "added")
        loaded = sems(ctx, nc, "sum", "loaded0", "loaded1")
        block = ctx.enter_context(nc.Block())
        DVE_HEADS, ACT_HEADS = (0, 1), (2, 3)

        @block.sync
        def _(sp):
            spread_rows(sp, m, spread_ready, loaded)

        @block.gpsimd
        def _(pool):
            gather_all(pool, m, m.table8v, staged)

        @block.tensor
        def _(pe):
            def step(s, c, live):
                if live(0):
                    wins = windows_of(pe, m, s * CHUNK)
                    pe.wait_ge(spread_ready, s + 3)
                    pe.wait_ge(diff_ready, s + 1)
                    for j in range(CHUNK):
                        mm = pe.matmul(bank(m, c % 2, j * HEADS, (j + 1) * HEADS), onehot_t[:, c % 2, j * P:(j + 1) * P],
                                       window(m.mx, wins[j // GROUP]), start=True, stop=True)
                    mm.then_inc(max_spread, 1)
                if live(2):
                    cc = (c - 2) % CHUNKS
                    pe.wait_ge(by_dve, s - 1)
                    pe.wait_ge(by_act, s - 1)
                    for j in range(CHUNK):
                        if j % GROUP == 0:
                            pe.wait_ge(added, (s - 2) * GROUPS + j // GROUP + 1)
                        pe.matmul(bank(m, 4 + (cc * CHUNK + j) // GROUP % 4, 0, ACCW), m.onehot[:, cc * CHUNK + j, :],
                                  vx[:, (cc % 2) * CHUNK + j, :], start=(j % GROUP == 0),
                                  stop=(j % GROUP == GROUP - 1)).then_inc(multiplied, 1)

            over_chunks(pe, step, 2)

        @block.scalar
        def _(act):
            def step(s, c, live):
                if live(3):
                    b, cc = (c - 3) % 2, (c - 3) % CHUNKS
                    act.wait_ge(exp_ready, s - 2)
                    for j in range(CHUNK):
                        slot_gathered(act, m, s - 3, cc, j)
                        for h in ACT_HEADS:
                            ins = nc.scalar.activation(vx[:, b * CHUNK + j, h * DK:(h + 1) * DK],
                                                       m.g[:, cc * CHUNK + j, h * DK:(h + 1) * DK], ACT.Copy,
                                                       scale=vx[:, b * CHUNK + j, D + h:D + h + 1])
                    ins.then_inc(by_act, 1)
                if live(2):
                    b = c % 2
                    act.wait_ge(multiplied, (s - 2) * CHUNK + CHUNK + SLOTS - R)
                    act.wait_ge(diff_ready, s + 1)
                    nc.scalar.activation(vx[:, b * CHUNK:(b + 1) * CHUNK, D:ACCW], diff[:, b, :, :], ACT.Exp).then_inc(exp_ready, 1)
                if live(0):
                    stage_records(act, nc, m, s * CHUNK, c, F_ROW8, multiplied, staged)

            act.wait_ge(added, 1)
            over_chunks(act, step, 3)

        @block.vector
        def _(dve):
            dve.sem_inc(multiplied, SLOTS)
            dve.sem_inc(spread_ready, 2)
            dve.sem_inc(diff_ready, 2)
            dve.sem_inc(added, 4)

            def onehots(s, c):
                b = c % 2
                if not (isinstance(s, int) and s < 2):
                    dve.wait_ge(max_spread, s - 1)
                dve.wait_ge(loaded[b], (s - b) * 8 + 16)
                nc.vector.tensor_scalar(onehot_t[:, b, :], m.dst_bc[:, b, :], m.rowid[:, :], None,
                                        ALU.is_equal).then_inc(spread_ready, 1)
                dve.wait_ge(staged, s + 1)
                for j in range(CHUNK):
                    nc.vector.tensor_scalar(m.onehot[:, c * CHUNK + j, :], m.cols[:, :], m.chunk[:, c, j, F_DST:F_DST + 1],
                                            None, ALU.is_equal).then_inc(onehot_ready, 1)

            def differences(s, c):
                b = c % 2
                if not (isinstance(s, int) and s < 2):
                    dve.wait_ge(exp_ready, s - 1)
                dve.wait_ge(max_spread, s + 1)
                nc.vector.tensor_tensor(diff[:, b, :, :].rearrange("p j h -> p (j h)"),
                                        m.scores[:, bass.ds(s * CHUNK, CHUNK), :].rearrange("p t h -> p (t h)"),
                                        bank(m, b, 0, CHUNK * HEADS), ALU.subtract).then_inc(diff_ready, 1)

            def weigh(s, c):
                b, t = c % 2, s * CHUNK
                dve.wait_ge(exp_ready, s + 1)
                for j in range(CHUNK):
                    slot_gathered(dve, m, s, c, j)
                    for h in DVE_HEADS:
                        ins = nc.vector.tensor_scalar(vx[:, b * CHUNK + j, h * DK:(h + 1) * DK],
                                                      m.g[:, c * CHUNK + j, h * DK:(h + 1) * DK],
                                                      vx[:, b * CHUNK + j, D + h:D + h + 1], None, ALU.mult)
                ins.then_inc(by_dve, 1)

            def add(s, c, wins):
                for g in range(GROUPS):
                    dve.wait_ge(multiplied, s * CHUNK + (g + 1) * GROUP + SLOTS)
                    dve.wait_ge(added, s * GROUPS + g + 4)
                    acc = window(m.acc, wins[g])
                    nc.vector.tensor_tensor(acc, acc, bank(m, 4 + (c * GROUPS + g) % 4, 0, ACCW), ALU.add).then_inc(added, 1)

            def step(s, c, live):
                if live(0):
                    onehots(s, c)
                wins = windows_of(dve, m, (s - 3) * CHUNK) if live(3) else None
                if live(1):
                    differences(s - 1, (c - 1) % CHUNKS)
                if live(2):
                    weigh(s - 2, (c - 2) % CHUNKS)
                if live(3):
                    add(s - 3, (c - 3) % CHUNKS, wins)

            over_chunks(dve, step, 3)


def layer_norm(nc, m, stage, prepare, out):
    with ExitStack() as ctx:
        chain, stats_ready, root_ready = sems(ctx, nc, stage, "norm_chain", "norm_stats", "norm_root")
        block = ctx.enter_context(nc.Block())

        @block.vector
        def _(dve):
            steps = [0]

            def step(ins):
                steps[0] += 1
                ins.then_inc(chain, 1)
                dve.wait_ge(chain, steps[0])

            prepare(step)
            for t in range(NT):
                step_or_none = nc.vector.bn_stats(m.stats[:, t, :], m.acc[:, t, 0:D])
            step(step_or_none)
            for t in range(NT):
                last = nc.vector.bn_aggr(m.mv[:, t, :], m.stats[:, t, :])
            last.then_inc(stats_ready, 1)
            dve.wait_ge(root_ready, 1)
            step(nc.vector.reciprocal(m.rstd[:, :], m.std[:, :]))
            for t in range(NT):
                nc.vector.tensor_scalar(out[:, t, 0:D], m.acc[:, t, 0:D], m.mv[:, t, 0:1], m.rstd[:, t:t + 1],
                                        ALU.subtract, ALU.mult)

        @block.scalar
        def _(act):
            act.wait_ge(stats_ready, 1)
            nc.scalar.activation(m.std[:, :], m.mv[:, :, 1], ACT.Sqrt, bias=m.eps[:, :], scale=1.0).then_inc(root_ready, 1)


def dense_pair(nc, m, stage, src, w_left, w_right, table, left_scale, left_keep, right_keep, right_bias):
    with ExitStack() as ctx:
        def sb(name, shape, dt=F32):
            return ctx.enter_context(nc.sbuf_tensor(f"{stage}_{name}", shape, dt))

        w = sb("w", [P, 2, 2 * D])
        xs = sb("xs", [P, 2, D])
        xt = sb("xt", [P, 2, 2, P])
        tb = sb("tb", [P, 2, D])
        weights_in, xs_ready, turned, xt_ready, product, tb_ready, kept = sems(
            ctx, nc, stage, "weights_in", "xs_ready", "turned", "xt_ready", "product", "tb_ready", "kept")
        stored = [sems(ctx, nc, stage, f"stored{b}")[0] for b in (0, 1)]
        block = ctx.enter_context(nc.Block())
        KEEPS = 1 + (left_keep is not None)

        def over_tiles(eng, tile):
            tile(0, 0, True)
            tile(1, 1, True)
            with eng.Fori(1, NT // 2, 1) as pair:
                t = pair * 2
                tile(t, 0, False)
                tile(t + 1, 1, False)
            tile(NT - 1, 0, False)

        def turned_ahead(eng, turn, multiply):
            turn(0, 0, True)
            turn(1, 1, True)
            multiply(0, 0, True)
            turn(2, 0, False)
            multiply(1, 1, True)
            with eng.Fori(1, NT // 2, 1) as pair:
                t = pair * 2
                turn(t + 1, 1, False)
                multiply(t, 0, False)
                turn(t + 2, 0, False)
                multiply(t + 1, 1, False)
            multiply(NT - 1, 0, False)

        @block.sync
        def _(sp):
            sp.dma_start(w[:, :, 0:D], w_left.rearrange("(k p) d -> p k d", p=P)).then_inc(weights_in, 16)
            sp.dma_start(w[:, :, D:2 * D], w_right.rearrange("(k p) d -> p k d", p=P)).then_inc(weights_in, 16)

            def tile(t, b, first):
                sp.wait_ge(tb_ready, t + 1)
                sp.dma_start(table[bass.ds(t * P, P), :], tb[:, b, :]).then_inc(stored[b], 16)

            over_tiles(sp, tile)
            sp.wait_ge(stored[0], 16 * (NT // 2 + 1))
            sp.wait_ge(stored[1], 16 * (NT // 2))

        @block.tensor
        def _(pe):
            def turn(t, b, first):
                if not first:
                    pe.wait_ge(xt_ready, t - 1)
                pe.wait_ge(xs_ready, t + 1)
                for k in (0, 1):
                    mm = pe.transpose(bank(m, b, k * P, (k + 1) * P), xs[:, b, k * P:(k + 1) * P], m.ident[:, :])
                mm.then_inc(turned, 1)

            def multiply(t, b, first):
                if first:
                    pe.wait_ge(weights_in, 32)
                else:
                    pe.wait_ge(tb_ready, t - 1)
                    pe.wait_ge(kept, KEEPS * (t - 1))
                pe.wait_ge(xt_ready, t + 1)
                for side in (0, 1):
                    for k in (0, 1):
                        mm = pe.matmul(bank(m, 2 + 2 * side + b, 0, D), xt[:, b, k, :], w[:, k, side * D:(side + 1) * D],
                                       start=(k == 0), stop=(k == 1))
                mm.then_inc(product, 1)

            turned_ahead(pe, turn, multiply)

        @block.scalar
        def _(act):
            def load(t, b, first):
                if not first:
                    act.wait_ge(turned, t - 1)
                    act.wait_ge(turned, 1)
                nc.scalar.activation(xs[:, b, :], window(src, t, 0, D), ACT.Copy).then_inc(xs_ready, 1)

            def tile(t, b, first):
                if not first:
                    act.wait_ge(stored[b], (t - b) * 8)
                    if left_keep is not None:
                        act.wait_ge(kept, 2 * (t - 1))
                act.wait_ge(product, t + 1)
                if left_scale is None:
                    nc.scalar.activation(tb[:, b, :], bank(m, 2 + b, 0, D), ACT.Copy).then_inc(tb_ready, 1)
                else:
                    act.wait_ge(product, 1)
                    nc.scalar.activation(tb[:, b, :], bank(m, 2 + b, 0, D), ACT.Copy,
                                         scale=left_scale[:, bass.ds(t, 1)]).then_inc(tb_ready, 1)

            turned_ahead(act, load, tile)

        @block.vector
        def _(dve):
            def turn(t, b, first):
                if not first:
                    dve.wait_ge(product, t - 1)
                dve.wait_ge(turned, t + 1)
                nc.vector.tensor_copy(xt[:, b, :, :], bank(m, b, 0, D).rearrange("p (k n) -> p k n", k=2)).then_inc(xt_ready, 1)

            def keep(t, b, first):
                dve.wait_ge(product, t + 1)
                right = bank(m, 4 + b, 0, D)
                if right_bias is None:
                    nc.vector.tensor_copy(window(right_keep, t, 0, D), right).then_inc(kept, 1)
                else:
                    nc.vector.tensor_tensor(window(right_keep, t, 0, D), right_bias, right, ALU.add).then_inc(kept, 1)
                if left_keep is not None:
                    dve.wait_ge(tb_ready, t + 1)
                    nc.vector.tensor_copy(window(left_keep, t, 0, D), tb[:, b, :]).then_inc(kept, 1)

            turned_ahead(dve, turn, keep)


def attention_tables(nc, m, a):
    with ExitStack() as ctx:
        def sb(name, shape, dt=F32):
            return ctx.enter_context(nc.sbuf_tensor(name, shape, dt))

        w = sb("w_kvq", [P, 2, NTYPES, 3 * D])
        xs = sb("xs5", [P, D])
        xm = sb("xm5", [P, NTYPES, 2, P])
        kv = sb("kv5", [P, 2 * D])
        kvt = sb("kvt5", [P, 4, P])
        rel = sb("rel", [P, 2, 2, RELS8 * DK])
        att = sb("att", [DK, 2, RELS8, P])
        pri = sb("pri", [P, RELS8 * HEADS])
        tb = sb("tb5", [P, 2, RELS8, D])
        types_i = sb("types_i", [P, ROWS], I32)
        (weights_in, rel_in, types_zero, types_in, chain, rel_ready, xs_ready, turned, xm_ready, typed, kv_ready,
         kv_turned, kvt_ready, product, even, odd, q_kept, att_turned) = sems(
            ctx, nc, "att", "weights_in", "rel_in", "types_zero", "types_in", "chain", "rel_ready", "xs_ready", "turned",
            "xm_ready", "typed", "kv_ready", "kv_turned", "kvt_ready", "product", "even", "odd", "q_kept", "att_turned")
        stored = sems(ctx, nc, "att", "stored_k", "stored_v")
        block = ctx.enter_context(nc.Block())
        tables = [m.table8k.rearrange("(n r) d -> n (r d)", r=RELS8), m.table8v.rearrange("(n r) d -> n (r d)", r=RELS8)]

        @block.sync
        def _(sp):
            for j, src in enumerate((a.k_lin, a.v_lin, a.q_lin)):
                for ty in range(NTYPES):
                    sp.dma_start(w[:, :, ty, j * D:(j + 1) * D], src[ty].rearrange("(k p) d -> p k d", p=P)).then_inc(weights_in, 16)
            for h in range(HEADS):
                o = (h % 2) * DK
                sp.dma_start(att[:, h // 2, :, o:o + DK], a.rel_att[:, h, :, :].rearrange("r d e -> d r e")).then_inc(rel_in, 16)
                sp.dma_start(rel[o:o + DK, 1, h // 2, :].rearrange("p (r e) -> p r e", r=RELS8),
                             a.rel_msg[:, h, :, :].rearrange("r d e -> d r e")).then_inc(rel_in, 16)
            sp.dma_start(pri[:, :], a.pri.rearrange("(o r) h -> o (r h)", o=1).to_broadcast([P, RELS8 * HEADS])).then_inc(rel_in, 16)
            sp.wait_ge(types_zero, 1)
            sp.dma_start(types_i[:, 0:NODES], a.node_type.rearrange("(o n) -> o n", o=1).to_broadcast([P, NODES])).then_inc(types_in, 16)
            with sp.Fori(0, NT, 1) as t:
                for j in (0, 1):
                    sp.wait_ge(even, t * 4 + 2 * j + 2)
                    sp.wait_ge(odd, t * 4 + 2 * j + 2)
                    sp.dma_start(tables[j][bass.ds(t * P, P), :], tb[:, j, :, :].rearrange("p r d -> p (r d)")).then_inc(stored[j], 16)
            for j in (0, 1):
                sp.wait_ge(stored[j], 16 * NT)

        @block.tensor
        def _(pe):
            def turn(t):
                pe.wait_ge(xs_ready, t + 1)
                for k in (0, 1):
                    mm = pe.transpose(bank(m, 0, k * P, (k + 1) * P), xs[:, k * P:(k + 1) * P], m.ident[:, :])
                mm.then_inc(turned, 1)

            def tile(t, first, last):
                if first:
                    pe.wait_ge(weights_in, 16 * 3 * NTYPES)
                else:
                    pe.wait_ge(q_kept, t)
                pe.wait_ge(xm_ready, t + 1)
                n = 0
                for ty in range(NTYPES):
                    for k in (0, 1):
                        for b, lo, hi in ((1, 0, 2 * D), (2, 2 * D, 3 * D)):
                            mm = pe.matmul(bank(m, b, 0, hi - lo), xm[:, ty, k, :], w[:, k, ty, lo:hi],
                                           start=(n == 0), stop=(n == 2 * NTYPES - 1))
                        n += 1
                mm.then_inc(typed, 1)
                if not last:
                    turn(t + 1)
                pe.wait_ge(kv_ready, t + 1)
                for c in range(4):
                    mm = pe.transpose(bank(m, 3, c * P, (c + 1) * P), kv[:, c * P:(c + 1) * P], m.ident[:, :])
                mm.then_inc(kv_turned, 1)
                if first:
                    pe.wait_ge(rel_ready, 1)
                pe.wait_ge(kvt_ready, t + 1)
                for g in range(8):
                    j, h = g // HEADS, g % HEADS
                    s, n = (odd, t * 4 + g // 2 - 1) if g % 2 else (even, t * 4 + g // 2 - 1)
                    if g >= 4 or not first:
                        pe.wait_ge(s, n)
                    o = (h % 2) * DK
                    pe.matmul(bank(m, 4 + g % 4, 0, 512), kvt[o:o + DK, 2 * j + h // 2, :], rel[o:o + DK, j, h // 2, :],
                              start=True, stop=True).then_inc(product, 1)

            pe.wait_ge(rel_in, 16 * 9)
            for hh in (0, 1):
                for r in range(RELS8):
                    mm = pe.transpose(bank(m, 4 + hh, r * DK, (r + 1) * DK), att[:, hh, r, :], m.ident[0:DK, 0:DK])
            mm.then_inc(att_turned, 1)
            turn(0)
            tile(0, True, False)
            with pe.Fori(1, NT - 1, 1) as t:
                tile(t, False, False)
            tile(NT - 1, False, True)

        def to_table(eng, copy, t, first, half, done):
            for g in range(half, 8, 2):
                j, h = g // HEADS, g % HEADS
                if not first:
                    eng.wait_ge(stored[j], t * 16)
                eng.wait_ge(product, t * 8 + g + 1)
                copy(tb[:, j, :, h * DK:(h + 1) * DK], bank(m, 4 + g % 4, 0, 512).rearrange("p (r e) -> p r e", r=RELS8)).then_inc(done, 1)

        @block.scalar
        def _(act):
            copy = lambda o, i: nc.scalar.activation(o, i, ACT.Copy)
            copy(xs[:, :], m.x[:, 0, :]).then_inc(xs_ready, 1)

            def tile(t, first, last):
                if not last:
                    act.wait_ge(turned, t + 1)
                    act.wait_ge(turned, 1)
                    copy(xs[:, :], window(m.x, t + 1)).then_inc(xs_ready, 1)
                act.wait_ge(typed, t + 1)
                copy(kv[:, :], bank(m, 1, 0, 512)).then_inc(kv_ready, 1)
                act.wait_ge(kv_turned, t + 1)
                copy(kvt[:, :, :], bank(m, 3, 0, 512).rearrange("p (c n) -> p c n", c=4)).then_inc(kvt_ready, 1)
                to_table(act, copy, t, first, 1, odd)

            tile(0, True, False)
            with act.Fori(1, NT - 1, 1) as t:
                tile(t, False, False)
            tile(NT - 1, False, True)

        @block.vector
        def _(dve):
            steps = [0]

            def step(ins):
                steps[0] += 1
                ins.then_inc(chain, 1)
                dve.wait_ge(chain, steps[0])

            nc.vector.memset(types_i[:, :], 0).then_inc(types_zero, 1)
            dve.wait_ge(rel_in, 16 * 9)
            step(nc.vector.tensor_scalar(pri[:, :], pri[:, :], 1.0 / SQRT_DK, None, ALU.mult))
            dve.wait_ge(att_turned, 1)
            for h in range(HEADS):
                o = (h % 2) * DK
                view = lambda v: v.rearrange("p (r e) -> p r e", r=RELS8)
                by = pri[o:o + DK, :].rearrange("p (r h) -> p r h", h=HEADS)[:, :, h:h + 1].to_broadcast([DK, RELS8, DK])
                ins = nc.vector.tensor_tensor(view(rel[o:o + DK, 0, h // 2, :]), by,
                                              view(m.ps[o:o + DK, 4 + h // 2, 0:512]), ALU.mult)
            ins.then_inc(rel_ready, 1)
            dve.wait_ge(types_in, 16)

            def typed_columns(t):
                dve.wait_ge(turned, t + 1)
                for ty in range(NTYPES):
                    for k in (0, 1):
                        ins = nc.vector.scalar_tensor_tensor(
                            xm[:, ty, k, :], types_i[:, bass.ds(t * P, P)], float(ty),
                            bank(m, 0, k * P, (k + 1) * P), ALU.is_equal, ALU.mult)
                ins.then_inc(xm_ready, 1)

            def tile(t, first, last):
                dve.wait_ge(typed, t + 1)
                nc.vector.tensor_copy(window(m.q, t), bank(m, 2, 0, D)).then_inc(q_kept, 1)
                if not last:
                    typed_columns(t + 1)
                to_table(dve, nc.vector.tensor_copy, t, first, 0, even)

            typed_columns(0)
            tile(0, True, False)
            with dve.Fori(1, NT - 1, 1) as t:
                tile(t, False, False)
            tile(NT - 1, False, True)


def attention_output(nc, m, a):
    with ExitStack() as ctx:
        def sb(name, shape, dt=F32):
            return ctx.enter_context(nc.sbuf_tensor(name, shape, dt))

        w = sb("w_a", [P, 2, NTYPES * D])
        xs = sb("xs8", [P, 2, D])
        xt = sb("xt8", [P, 2, 2, P])
        rden = sb("rden", [P, NT, HEADS])
        types_i = sb("types_i8", [P, NT], I32)
        skip = sb("skip", [P, NTYPES])
        gate = sb("gate", [P, NTYPES])
        gates = sb("gates", [P, NTYPES, NT])
        tmp = sb("tmp8", [P, 4, D])
        weights_in, small_in, types_zero, chain, exp_ready, divided, xs_ready, turned, xt_ready, product, summed, own = sems(
            ctx, nc, "out", "weights_in", "small_in", "types_zero", "chain", "exp_ready", "divided", "xs_ready",
            "turned", "xt_ready", "product", "summed", "own")
        block = ctx.enter_context(nc.Block())

        @block.sync
        def _(sp):
            sp.dma_start(skip[:, :], a.skip.rearrange("(o n) -> o n", o=1).to_broadcast([P, NTYPES])).then_inc(small_in, 16)
            sp.wait_ge(types_zero, 1)
            with nc.allow_non_contiguous_dma(reason="a node per partition"):
                sp.dma_start(types_i[:, 0:NT - 1], a.node_type[0:(NT - 1) * P].rearrange("(t p) -> p t", p=P)).then_inc(small_in, 16)
                sp.dma_start(types_i[0:LAST, NT - 1:NT], a.node_type[(NT - 1) * P:NODES].rearrange("(p o) -> p o", o=1)).then_inc(small_in, 16)
            for ty in range(NTYPES):
                sp.dma_start(w[:, :, ty * D:(ty + 1) * D], a.a_lin[ty].rearrange("(k p) d -> p k d", p=P)).then_inc(weights_in, 16)

        @block.tensor
        def _(pe):
            pe.wait_ge(weights_in, 16 * NTYPES)

            def turn(t, b):
                pe.wait_ge(xs_ready, t + 1)
                for k in (0, 1):
                    mm = pe.transpose(bank(m, b, k * P, (k + 1) * P), xs[:, b, k * P:(k + 1) * P], m.ident[:, :])
                mm.then_inc(turned, 1)

            def multiply(t, b, first):
                if not first:
                    pe.wait_ge(summed, t - 1)
                pe.wait_ge(xt_ready, t + 1)
                for k in (0, 1):
                    for n in (0, 1):
                        mm = pe.matmul(bank(m, 2 + 2 * b + n, 0, 512), xt[:, b, k, :], w[:, k, n * 512:(n + 1) * 512],
                                       start=(k == 0), stop=(k == 1))
                mm.then_inc(product, 1)

            turn(0, 0)
            turn(1, 1)
            multiply(0, 0, True)
            turn(2, 0)
            multiply(1, 1, True)
            with pe.Fori(1, NT // 2, 1) as pair:
                turn(pair * 2 + 1, 1)
                multiply(pair * 2, 0, False)
                turn(pair * 2 + 2, 0)
                multiply(pair * 2 + 1, 1, False)
            multiply(NT - 1, 0, False)

        @block.scalar
        def _(act):
            act.wait_ge(small_in, 48)
            nc.scalar.activation(gate[:, :], skip[:, :], ACT.Exp, scale=-1.0).then_inc(exp_ready, 1)
            act.wait_ge(divided, 1)
            for t in (0, 1):
                nc.scalar.activation(xs[:, t, :], m.acc[:, t, 0:D], ACT.Copy).then_inc(xs_ready, 1)

            def load(t, b):
                act.wait_ge(turned, t - 1)
                act.wait_ge(turned, 1)
                nc.scalar.activation(xs[:, b, :], window(m.acc, t, 0, D), ACT.Copy).then_inc(xs_ready, 1)

            with act.Fori(1, NT // 2, 1) as pair:
                load(pair * 2, 0)
                load(pair * 2 + 1, 1)
            load(NT - 1, 0)

        @block.vector
        def _(dve):
            steps = [0]

            def step(ins):
                steps[0] += 1
                ins.then_inc(chain, 1)
                dve.wait_ge(chain, steps[0])

            nc.vector.memset(types_i[:, :], 0).then_inc(types_zero, 1)
            step(nc.vector.tensor_scalar(rden[:, :, :], m.acc[:, :, D:ACCW], 1e-30, None, ALU.max))
            step(nc.vector.reciprocal(rden[:, :, :], rden[:, :, :]))
            for h in range(HEADS):
                v = m.acc[:, :, h * DK:(h + 1) * DK]
                ins = nc.vector.tensor_tensor(v, v, rden[:, :, h:h + 1].to_broadcast([P, NT, DK]), ALU.mult)
            ins.then_inc(divided, 1)
            dve.wait_ge(exp_ready, 1)
            step(nc.vector.tensor_scalar(gate[:, :], gate[:, :], 1.0, None, ALU.add))
            step(nc.vector.reciprocal(skip[:, :], gate[:, :]))
            for ty in range(NTYPES):
                ins = nc.vector.tensor_scalar(gates[:, ty, :], types_i[:, :], float(ty), skip[:, ty:ty + 1], ALU.is_equal, ALU.mult)
            step(ins)

            def turned_copy(t, b, first):
                if not first:
                    dve.wait_ge(product, t - 1)
                dve.wait_ge(turned, t + 1)
                nc.vector.tensor_copy(xt[:, b, :, :], bank(m, b, 0, D).rearrange("p (k n) -> p k n", k=2)).then_inc(xt_ready, 1)

            def combine(t, b):
                dve.wait_ge(product, t + 1)
                for ty in range(NTYPES):
                    prev = window(m.x, t) if ty == 0 else tmp[:, ty - 1, :]
                    out = window(m.acc, t, 0, D) if ty == NTYPES - 1 else tmp[:, ty, :]
                    if ty:
                        dve.wait_ge(own, t * 3 + ty)
                    ins = nc.vector.scalar_tensor_tensor(
                        out, bank(m, 2 + 2 * b + ty // 2, (ty % 2) * D, (ty % 2 + 1) * D),
                        gates[:, ty, bass.ds(t, 1)], prev, ALU.mult, ALU.add)
                    ins.then_inc(own if ty < NTYPES - 1 else summed, 1)

            turned_copy(0, 0, True)
            turned_copy(1, 1, True)
            combine(0, 0)
            turned_copy(2, 0, False)
            combine(1, 1)
            with dve.Fori(1, NT // 2, 1) as pair:
                turned_copy(pair * 2 + 1, 1, False)
                combine(pair * 2, 0)
                turned_copy(pair * 2 + 2, 0, False)
                combine(pair * 2 + 1, 1)
            combine(NT - 1, 0)


def vector_block(nc, m, stage, body):
    with ExitStack() as ctx:
        chain, = sems(ctx, nc, stage, "chain")
        block = ctx.enter_context(nc.Block())

        @block.vector
        def _(dve):
            steps = [0]

            def step(ins):
                steps[0] += 1
                ins.then_inc(chain, 1)
                dve.wait_ge(chain, steps[0])

            body(step)


def four_graph_layers(nc, a, out):
    with ExitStack() as ctx:
        def sb(name, shape, dt=F32):
            return ctx.enter_context(nc.sbuf_tensor(name, shape, dt))

        m = Named()
        m.iota_i = sb("iota_i", [P, P], I32)
        m.iota_p = sb("iota_p", [P, 1], I32)
        m.cols = sb("cols", [P, P])
        m.rowid = sb("rowid", [P, 1])
        m.ones = sb("ones", [P, P])
        m.eps = sb("eps", [P, 1])
        m.ident = sb("ident", [P, P])
        m.lower = sb("lower", [P, P])
        m.tile_ids = sb("tile_ids", [1, TILES])
        m.win = sb("win", [1, TILES], I32)
        m.x = sb("x", [P, NT, D])
        m.rec = sb("rec_all", [P, TILES, REC])
        m.ps = ctx.enter_context(nc.psum_tensor("ps", [P, 8, 512], F32))
        m.records = nc.dram_tensor("records", (P * TILES, REC), F32, kind="Internal").ap()
        m.table20 = nc.dram_tensor("table20", (ROWS * RELS20, D), F32, kind="Internal").ap()
        m.dst_rows = nc.dram_tensor("dst_rows", (TILES * P,), F32, kind="Internal").ap()
        m.table1 = nc.dram_tensor("table1", (ROWS, D), F32, kind="Internal").ap()
        m.table8k = nc.dram_tensor("table8k", (ROWS * RELS8, D), F32, kind="Internal").ap()
        m.table8v = nc.dram_tensor("table8v", (ROWS * RELS8, D), F32, kind="Internal").ap()

        m.tick, m.sp_tick = sems(ctx, nc, "own", "tick", "sp_tick")
        m.scattered = sems(ctx, nc, "all", "scattered0", "scattered1")
        constants(nc, m)
        with ExitStack() as c2:
            made, = sems(c2, nc, "ids", "made")
            m.spent.append(made)
            ids_i = c2.enter_context(nc.sbuf_tensor("ids_i", [1, TILES], I32))
            block = c2.enter_context(nc.Block())

            @block.gpsimd
            def _(pool):
                nc.gpsimd.iota(ids_i[:, :], [[1, TILES]], base=0, channel_multiplier=0).then_inc(made, 1)

            @block.vector
            def _(dve):
                dve.wait_ge(made, 1)
                nc.vector.tensor_copy(m.tile_ids[:, :], ids_i[:, :])

        sort_and_relation_table(nc, m, a)

        m.acc = sb("acc", [P, NT, ACCW])
        m.rows_i = sb("rows_i", [P, CHUNKS, CHUNK], I32)
        m.chunk = sb("chunk", [P, CHUNKS, CHUNK, REC])
        m.stats = sb("stats", [P, NT, 6])
        m.mv = sb("mv", [P, NT, 2])
        m.std = sb("std", [P, NT])
        m.rstd = sb("rstd", [P, NT])
        m.dis = sb("dis", [P, NT])
        m.q = sb("q", [P, NT, D])
        m.mx = sb("mx", [P, NT, HEADS])
        m.scores = sb("scores", [P, TILES, HEADS])
        m.bias = sb("bias", [P, 3, D])
        m.gathered = sems(ctx, nc, "all", *(f"gathered{k}" for k in range(SLOTS)))
        m.gather_stages = 0
        m.mx_written, m.bias_in = sems(ctx, nc, "all", "mx_written", "bias_in")
        feat = m.acc[:, :, 0:D]

        def relu_add(step):
            step(nc.vector.scalar_tensor_tensor(feat, feat, 0.0, m.x[:, :, :], ALU.max, ALU.add))

        destination_rows(nc, m)

        vector_block(nc, m, "zero", lambda step: step(nc.vector.memset(m.acc[:, :, :], 0.0)))
        aggregate_edges(nc, m, "rel", m.table20, F_ROW20, weighted=True)
        layer_norm(nc, m, "rel", relu_add, m.x)

        vector_block(nc, m, "count", lambda step: step(nc.vector.memset(m.acc[:, :, D:ACCW], 0.0)))
        dense_pair(nc, m, "conv", m.x, a.m1, a.w1, m.table1, None, None, m.acc, None)
        aggregate_edges(nc, m, "conv_edges", m.table1, F_SRC, count=True)

        def after_conv(step):
            relu_add(step)
            step(nc.vector.tensor_scalar(m.dis[:, :], m.acc[:, :, D], 1.0, None, ALU.add))
        layer_norm(nc, m, "conv", after_conv, m.x)

        with ExitStack() as c2:
            rooted, = sems(c2, nc, "dis", "rooted")
            block = c2.enter_context(nc.Block())

            @block.scalar
            def _(act):
                nc.scalar.activation(m.std[:, :], m.dis[:, :], ACT.Sqrt).then_inc(rooted, 1)

            @block.vector
            def _(dve):
                nc.vector.memset(m.acc[:, :, :], 0.0)
                dve.wait_ge(rooted, 1)
                nc.vector.reciprocal(m.dis[:, :], m.std[:, :])

            @block.sync
            def _(sp):
                for k, v in enumerate((a.b[0], a.b[1], a.resb)):
                    sp.dma_start(m.bias[:, k, :], v.rearrange("(o n) -> o n", o=1).to_broadcast([P, D])).then_inc(m.bias_in, 16)
                sp.wait_ge(m.bias_in, 48)

        attention_tables(nc, m, a)
        attention_scores(nc, m)
        attention_sum(nc, m)
        attention_output(nc, m, a)
        layer_norm(nc, m, "att", lambda step: None, m.x)

        def biases(step):
            for k in (0, 1):
                step(nc.vector.tensor_tensor(m.bias[:, k, :], m.bias[:, k, :], m.bias[:, 2, :], ALU.add))
        vector_block(nc, m, "bias", biases)
        h = m.acc2 = sb("h", [P, NT, D])

        def conv_out(step, into):
            for t in range(NT):
                ins = nc.vector.scalar_tensor_tensor(into[:, t, 0:D], m.acc[:, t, 0:D], m.dis[:, t:t + 1], m.q[:, t, :],
                                                     ALU.mult, ALU.add)
            step(ins)

        dense_pair(nc, m, "gcn0", m.x, a.w3[0], a.resw, m.table1, m.dis, m.acc, m.q, m.bias[:, 0, :])
        aggregate_edges(nc, m, "gcn0_edges", m.table1, F_SRC)

        def hidden(step):
            conv_out(step, h)
            step(nc.vector.tensor_scalar(h[:, :, :], h[:, :, :], 0.0, None, ALU.max))
        vector_block(nc, m, "gcn0_out", hidden)
        dense_pair(nc, m, "gcn1", h, a.w3[1], a.resw, m.table1, m.dis, m.acc, m.q, m.bias[:, 1, :])
        aggregate_edges(nc, m, "gcn1_edges", m.table1, F_SRC)

        def last(step):
            conv_out(step, m.acc)
            relu_add(step)
        layer_norm(nc, m, "gcn", last, h)

        with ExitStack() as c2:
            stored, = sems(c2, nc, "end", "stored")
            block = c2.enter_context(nc.Block())

            @block.sync
            def _(sp):
                sp.dma_start(out[0:(NT - 1) * P, :].rearrange("(t p) d -> p t d", p=P), h[:, 0:NT - 1, :]).then_inc(stored, 16)
                sp.dma_start(out[(NT - 1) * P:NODES, :], h[0:LAST, NT - 1, :]).then_inc(stored, 16)
                sp.wait_ge(stored, 32)


_INS = {
    "x": "x", "src": "src", "dst": "dst", "rel20": "edge_type_20", "rel8": "edge_type_8", "weight": "edge_weight1",
    "node_type": "node_type_4", "w20": "L0_gnn_weight", "w1": "L1_gnn_W", "m1": "L1_gnn_M",
    "k_lin": "L2_gnn_k_linears", "q_lin": "L2_gnn_q_linears", "v_lin": "L2_gnn_v_linears", "a_lin": "L2_gnn_a_linears",
    "rel_att": "L2_gnn_relation_att", "rel_msg": "L2_gnn_relation_msg", "pri": "L2_gnn_relation_pri",
    "skip": "L2_gnn_skip", "w3": "L3_gnn_W", "b": "L3_gnn_b", "resw": "L3_gnn_resW", "resb": "L3_gnn_resb",
}


def kernel(**inputs):
    import numpy as np
    import concourse.bacc as bacc
    from concourse.bass_utils import run_bass_kernel_spmd

    nc = bacc.Bacc("TRN2", target_bir_lowering=False, num_devices=1)
    arrays, a = {}, Named()
    for short, name in _INS.items():
        v = np.ascontiguousarray(inputs[name])
        arrays[f"in_{short}"] = v
        a.__dict__[short] = nc.dram_tensor(f"in_{short}", v.shape, mybir.dt.from_np(v.dtype), kind="ExternalInput").ap()
    out = nc.dram_tensor("out_x", (NODES, D), F32, kind="ExternalOutput").ap()
    four_graph_layers(nc, a, out)
    r = run_bass_kernel_spmd(nc, [arrays], core_ids=[0])
    return r.results[0]["out_x"]
```
